# Optimizing a Trainium2 kernel written in Bass

```python
import numpy as np
import jax
import jax.numpy as jnp

def _softmax(x, axis=-1):
    return jax.nn.softmax(x, axis=axis)

def _gelu(x):
    return jax.nn.gelu(x, approximate=True)

def _silu(x):
    return jax.nn.silu(x)

def _sigmoid(x):
    return jax.nn.sigmoid(x)

def _layernorm(x, axis=-1, eps=1e-05):
    m = jnp.mean(x, axis=axis, keepdims=True)
    v = jnp.var(x, axis=axis, keepdims=True)
    return (x - m) / jnp.sqrt(v + eps)

def _scatter_add(tgt, idx, src, axis=0):
    return tgt.at[idx].add(src)

def _segment_sum(src, seg, n):
    return jax.ops.segment_sum(src, seg, n)
kernel_name = 'mk_gnn_resnorm_d2_gnn_r64_0ff81f'

def setup_inputs(seed: int=0):
    np.random.seed(seed)
    _w = jnp.asarray

    def _rec_inputs():
        import jax
        import jax.numpy as jnp
        _gk = jax.random.key(seed)
        x = -0.0003713 + 1 * jax.random.normal(jax.random.fold_in(_gk, 1), (100000, 128), jnp.float32)
        src = jax.random.randint(jax.random.fold_in(_gk, 2), (50000,), 0, 100000, jnp.int32)
        dst = jnp.minimum((100000 * jax.random.uniform(jax.random.fold_in(_gk, 3), (50000,)) ** 2.0).astype(jnp.int32), 99999)
        _o = jnp.argsort(dst, stable=True)
        src = src[_o]
        dst = dst[_o]
        edge_weight = jax.random.uniform(jax.random.fold_in(_gk, 13), (50000,), jnp.float32, 0.0, 1)
        return (x, src, dst, edge_weight)
    x, src, dst, edge_weight = _rec_inputs()

    def _L0_gnn_setup():
        import jax, jax.numpy as jnp
        import numpy as np
        NEG_SLOPE = 0.2

        def gat_conv(x, src, dst, n, W, att_src, att_dst, bias, concat):
            H, C = att_src.shape
            xp = (x @ W).reshape(n, H, C)
            a_src = jnp.einsum('nhc,hc->nh', xp, att_src)
            a_dst = jnp.einsum('nhc,hc->nh', xp, att_dst)
            e = jax.nn.leaky_relu(a_src[src] + a_dst[dst], NEG_SLOPE)
            m = jax.ops.segment_max(e, dst, num_segments=n)
            ex = jnp.exp(e - m[dst])
            s = jax.ops.segment_sum(ex, dst, num_segments=n)
            alpha = ex / s[dst]
            out = jax.ops.segment_sum(xp[src] * alpha[:, :, None], dst, num_segments=n)
            out = out.reshape(n, H * C) if concat else out.mean(axis=1)
            return out + bias
        key = jax.random.key(seed)
        ks = jax.random.split(key, 16)
        N, E, D, H = (100000, 25000, 128, 4)
        HID, OUT = (128, 128)
        C = HID // H
        x = jax.random.normal(ks[0], (N, D), dtype=jnp.float32)
        edge_index = jax.random.randint(ks[1], (2, E), 0, N, dtype=jnp.int32)
        g = lambda k, shp: jax.random.normal(k, shp, dtype=jnp.float32) * 0.1
        return {'x': x, 'edge_index': edge_index, 'W1': g(ks[2], (D, H * C)), 'as1': g(ks[3], (H, C)), 'ad1': g(ks[4], (H, C)), 'b1': jnp.zeros((H * C,), jnp.float32), 'W2': g(ks[5], (HID, H * C)), 'as2': g(ks[6], (H, C)), 'ad2': g(ks[7], (H, C)), 'b2': jnp.zeros((H * C,), jnp.float32), 'W3': g(ks[8], (HID, H * OUT)), 'as3': g(ks[9], (H, OUT)), 'ad3': g(ks[10], (H, OUT)), 'b3': jnp.zeros((OUT,), jnp.float32)}
    _L0_gnn_all = _L0_gnn_setup()
    _L0_gnn_in = {k: v for k, v in _L0_gnn_all.items() if k in ('W1', 'as1', 'ad1', 'b1', 'W2', 'as2', 'ad2', 'b2', 'W3', 'as3', 'ad3', 'b3')}
    del _L0_gnn_all

    def _L1_gnn_setup():
        import jax, jax.numpy as jnp
        import numpy as np
        N = 100000
        E = 12500
        D = 128
        key = jax.random.key(seed)
        ks = jax.random.split(key, 12)
        s = lambda fan_in: 1.0 / np.sqrt(fan_in)
        return {'h': jax.random.normal(ks[0], (N, D), dtype=jnp.float32), 'w': jax.random.uniform(ks[1], (E,), dtype=jnp.float32), 'src': jax.random.randint(ks[2], (E,), 0, N, dtype=jnp.int32), 'dst': jax.random.randint(ks[3], (E,), 0, N, dtype=jnp.int32), 'W1': jax.random.uniform(ks[4], (2 * D + 1, D), jnp.float32, -s(2 * D + 1), s(2 * D + 1)), 'b1': jnp.zeros((D,), jnp.float32), 'W2': jax.random.uniform(ks[5], (D, D), jnp.float32, -s(D), s(D)), 'b2': jnp.zeros((D,), jnp.float32), 'U1': jax.random.uniform(ks[6], (2 * D, D), jnp.float32, -s(2 * D), s(2 * D)), 'c1': jnp.zeros((D,), jnp.float32), 'U2': jax.random.uniform(ks[7], (D, D), jnp.float32, -s(D), s(D)), 'c2': jnp.zeros((D,), jnp.float32)}
    _L1_gnn_all = _L1_gnn_setup()
    _L1_gnn_in = {k: v for k, v in _L1_gnn_all.items() if k in ('W1', 'b1', 'W2', 'b2', 'U1', 'c1', 'U2', 'c2')}
    del _L1_gnn_all
    return {'x': x, 'src': src, 'dst': dst, 'edge_weight': edge_weight, 'L0_gnn_W1': _L0_gnn_in['W1'], 'L0_gnn_as1': _L0_gnn_in['as1'], 'L0_gnn_ad1': _L0_gnn_in['ad1'], 'L0_gnn_b1': _L0_gnn_in['b1'], 'L0_gnn_W2': _L0_gnn_in['W2'], 'L0_gnn_as2': _L0_gnn_in['as2'], 'L0_gnn_ad2': _L0_gnn_in['ad2'], 'L0_gnn_b2': _L0_gnn_in['b2'], 'L0_gnn_W3': _L0_gnn_in['W3'], 'L0_gnn_as3': _L0_gnn_in['as3'], 'L0_gnn_ad3': _L0_gnn_in['ad3'], 'L0_gnn_b3': _L0_gnn_in['b3'], 'L1_gnn_W1': _L1_gnn_in['W1'], 'L1_gnn_b1': _L1_gnn_in['b1'], 'L1_gnn_W2': _L1_gnn_in['W2'], 'L1_gnn_b2': _L1_gnn_in['b2'], 'L1_gnn_U1': _L1_gnn_in['U1'], 'L1_gnn_c1': _L1_gnn_in['c1'], 'L1_gnn_U2': _L1_gnn_in['U2'], 'L1_gnn_c2': _L1_gnn_in['c2']}

def reference(x, src, dst, edge_weight, L0_gnn_W1, L0_gnn_as1, L0_gnn_ad1, L0_gnn_b1, L0_gnn_W2, L0_gnn_as2, L0_gnn_ad2, L0_gnn_b2, L0_gnn_W3, L0_gnn_as3, L0_gnn_ad3, L0_gnn_b3, L1_gnn_W1, L1_gnn_b1, L1_gnn_W2, L1_gnn_b2, L1_gnn_U1, L1_gnn_c1, L1_gnn_U2, L1_gnn_c2):
    import jax
    import jax.numpy as jnp

    def _L0_gnn_ref(x, edge_index, W1, as1, ad1, b1, W2, as2, ad2, b2, W3, as3, ad3, b3):
        import jax, jax.numpy as jnp
        import numpy as np
        NEG_SLOPE = 0.2

        def gat_conv(x, src, dst, n, W, att_src, att_dst, bias, concat):
            H, C = att_src.shape
            xp = (x @ W).reshape(n, H, C)
            a_src = jnp.einsum('nhc,hc->nh', xp, att_src)
            a_dst = jnp.einsum('nhc,hc->nh', xp, att_dst)
            e = jax.nn.leaky_relu(a_src[src] + a_dst[dst], NEG_SLOPE)
            m = jax.ops.segment_max(e, dst, num_segments=n)
            ex = jnp.exp(e - m[dst])
            s = jax.ops.segment_sum(ex, dst, num_segments=n)
            alpha = ex / s[dst]
            out = jax.ops.segment_sum(xp[src] * alpha[:, :, None], dst, num_segments=n)
            out = out.reshape(n, H * C) if concat else out.mean(axis=1)
            return out + bias
        n = x.shape[0]
        loops = jnp.arange(n, dtype=edge_index.dtype)
        src = jnp.concatenate([edge_index[0], loops])
        dst = jnp.concatenate([edge_index[1], loops])
        h = jax.nn.relu(gat_conv(x, src, dst, n, W1, as1, ad1, b1, True))
        h = jax.nn.relu(gat_conv(h, src, dst, n, W2, as2, ad2, b2, True))
        return gat_conv(h, src, dst, n, W3, as3, ad3, b3, False)

    def _L1_gnn_ref(h, w, src, dst, W1, b1, W2, b2, U1, c1, U2, c2):
        import jax, jax.numpy as jnp
        import numpy as np
        N = 100000
        E = 12500
        D = 128
        n = h.shape[0]
        msg_in = jnp.concatenate([h[src], h[dst], w[:, None]], axis=1)
        msg = jax.nn.relu(msg_in @ W1 + b1) @ W2 + b2
        agg = jax.ops.segment_max(msg, dst, num_segments=n)
        deg = jax.ops.segment_sum(jnp.ones((dst.shape[0],), jnp.int32), dst, num_segments=n)
        agg = jnp.where((deg > 0)[:, None], agg, jnp.zeros((), h.dtype))
        upd_in = jnp.concatenate([h, agg], axis=1)
        return jax.nn.relu(upd_in @ U1 + c1) @ U2 + c2
    edge_index = jnp.stack([src, dst])
    x = _layernorm(x + _L0_gnn_ref(x, edge_index, L0_gnn_W1, L0_gnn_as1, L0_gnn_ad1, L0_gnn_b1, L0_gnn_W2, L0_gnn_as2, L0_gnn_ad2, L0_gnn_b2, L0_gnn_W3, L0_gnn_as3, L0_gnn_ad3, L0_gnn_b3), axis=-1)
    x = _layernorm(x + _L1_gnn_ref(x, edge_weight, src, dst, L1_gnn_W1, L1_gnn_b1, L1_gnn_W2, L1_gnn_b2, L1_gnn_U1, L1_gnn_c1, L1_gnn_U2, L1_gnn_c2), axis=-1)
    return x

_drawn_inputs = setup_inputs


def setup_inputs(seed=0):
    import zlib

    import numpy as np

    out = dict(_drawn_inputs(seed))
    spreads = {'L0_gnn_b1': (0.0, 0.289),
     'L0_gnn_b2': (0.0, 0.1),
     'L0_gnn_b3': (0.0, 0.1),
     'L1_gnn_b1': (0.0, 2.0),
     'L1_gnn_b2': (0.0, 0.744),
     'L1_gnn_c1': (0.0, 0.1),
     'L1_gnn_c2': (0.0, 0.1)}
    factors = {'edge_weight': 46.941,
     'L0_gnn_as1': 4.005,
     'L0_gnn_ad1': 100.604,
     'L0_gnn_as2': 8.0,
     'L0_gnn_ad2': 180.157,
     'L0_gnn_as3': 7.178,
     'L0_gnn_ad3': 130.502,
     'L1_gnn_W1': 3.182}
    for name, (base, spread) in spreads.items():
        noise = np.random.default_rng([zlib.crc32(name.encode()), seed]).standard_normal(out[name].shape)
        drawn = base * np.exp(spread * noise) if base else spread * noise
        out[name] = jnp.asarray(drawn.astype(out[name].dtype))
    for name, factor in factors.items():
        out[name] = (out[name] * factor).astype(out[name].dtype)
    return out
```

```python
import numpy as np
import concourse.bass as bass
from concourse import mybir
from contextlib import ExitStack

FP32 = mybir.dt.float32
I32 = mybir.dt.int32
ALU = mybir.AluOpType
ACT = mybir.ActivationFunctionType
AX = mybir.AxisListType

P = 128
N = 100000
E = 50000
H = 4
C = P // H
G = 4
COLS = 392
EP = P * COLS
EG = COLS // G
NG = (N + G * P - 1) // (G * P)
NP = NG * G * P
FAR = float(1 << 22)
BIG = 1e30
ROW = P + 2 * H
SLOPE = 0.2
EPS = 1e-5
DLANES = 4
MG = 8
LAYERS = (1, 2, 3)
WIDE = {1: C, 2: C, 3: P}
ACC = {l: H * (WIDE[l] + 1) for l in LAYERS}
STATE = {1: ACC[1] + 2 * H + P, 2: ACC[2] + 2 * H, 3: ACC[3] + 2 * H, 4: P}


def build(nc, A, out):
    ctx = ExitStack()
    with ctx:
        def sb(name, shape, dt=FP32):
            return ctx.enter_context(nc.sbuf_tensor(name, shape, dt))

        K = {}
        for name in ("ident", "W1", "W2", "W3m", "U1a", "U1b", "U2", "M1a", "M1b", "M2",
                     "b1r", "b2r", "b3r", "m2r", "c2r"):
            K[name] = sb("k_" + name, [P, P])
        K["W3"] = sb("k_W3", [P, H * P])
        K["w1c"] = sb("k_w1c", [1, P])
        for name in ("b1", "b2", "mb1", "c1", "eps"):
            K[name] = sb("k_" + name + "_col", [P, 1])
        for name in ("A1", "A2", "A3"):
            K[name] = sb("k_" + name, [P, 2 * H])
        for name in ("src_i", "dst_i", "scat_i", "slot_i", "gsrc_i", "gdst_i"):
            K[name] = sb("k_" + name, [P, COLS], I32)
        K["fresh"] = sb("k_fresh", [P, COLS])
        K["last"] = sb("k_last", [P, COLS])
        K["goes_on"] = sb("k_goes_on", [P, COLS])
        K["headend"] = sb("k_headend", [P, COLS])
        K["joins"] = sb("k_joins", [P, 1])
        K["chain"] = sb("k_chain", [P, P])
        K["head_slot_i"] = sb("k_head_slot_i", [P, 1], I32)
        K["head_row_i"] = sb("k_head_row_i", [P, 1], I32)
        K["head_out_i"] = sb("k_head_out_i", [P, 1], I32)
        K["tail_row_i"] = sb("k_tail_row_i", [P, 1], I32)
        K["head_read_i"] = sb("k_head_read_i", [P, 1], I32)
        K["not_headend"] = sb("k_not_headend", [P, COLS])
        K["tail"] = sb("k_tail", [P, 1])
        K["held"] = sb("k_held", [P, 2 * H, COLS])
        K["carry_m"] = sb("k_carry_m", [P, H])
        K["carry_acc"] = sb("k_carry_acc", [P, ACC[3]])

        T = {l: nc.dram_tensor(f"table_{l}", [NP + EP, P if l == 4 else ROW], FP32, kind=TABLE_KIND).ap()
             for l in (2, 3, 4)}
        T["map"] = nc.dram_tensor("node_row", [NP, 1], I32, kind=TABLE_KIND).ap()
        T["xd"] = nc.dram_tensor("slot_x", [EP, P], FP32, kind="Internal").ap()
        for l in (1, 2, 3, 4):
            T["st", l] = nc.dram_tensor(f"slot_state_{l}", [EP, STATE[l]], FP32, kind="Internal").ap()

        K["dma_sem"] = lambda name: ctx.enter_context(nc.semaphore(name))

        prepare(nc, A, K, T)
        map_nodes(nc, K, T)
        dense(nc, A, K, T, out)
        for layer in LAYERS:
            attend(nc, A, K, T, layer)
            seam_attend(nc, K, T, layer)
            if layer < 3:
                hold_logits(nc, K, T, layer + 1)
        message(nc, A, K, T, out)
        seam_message(nc, K, T, out)


def clear_semaphores(nc, used):
    with nc.Block() as block:
        @block.gpsimd
        def _(g):
            for s in used:
                g.sem_clear(s)


def prepare(nc, A, K, T):
    with ExitStack() as ctx:
        def sb(name, shape, dt=FP32):
            return ctx.enter_context(nc.sbuf_tensor(name, shape, dt))

        used = []

        def sem(name):
            used.append(ctx.enter_context(nc.semaphore(name)))
            return used[-1]

        att = {(k, l): sb(f"att_{k}{l}", [P, P if l < 3 else H * P]) for k in "sd" for l in LAYERS}
        prod = sb("prep_prod", [P, H * P])
        w3raw = sb("prep_w3", [P, H * P])
        prev_i = sb("prep_prev_i", [P, COLS], I32)
        next_i = sb("prep_next_i", [P, COLS], I32)
        dstf = sb("prep_dst", [P, COLS])
        prevf = sb("prep_prev", [P, COLS])
        nextf = sb("prep_next", [P, COLS])
        slotf = sb("prep_slot", [P, COLS])
        inhead = sb("prep_inhead", [P, COLS])
        work = sb("prep_work", [P, COLS])
        ends = sb("prep_ends", [P, 4])
        wide = sb("prep_wide", [P, P])
        ps = ctx.enter_context(nc.psum_tensor("prep_ps", [P, 512], FP32))
        loaded, built, turned, mapped = sem("p_loaded"), sem("p_built"), sem("p_turned"), sem("p_mapped")
        plain = [("ident", A["eye"][:, :]), ("W1", A["L0_gnn_W1"][:, :]), ("W2", A["L0_gnn_W2"][:, :]),
                 ("U1a", A["L1_gnn_U1"][0:P, :]), ("U1b", A["L1_gnn_U1"][P:2 * P, :]),
                 ("U2", A["L1_gnn_U2"][:, :]), ("M1a", A["L1_gnn_W1"][0:P, :]),
                 ("M1b", A["L1_gnn_W1"][P:2 * P, :]), ("w1c", A["L1_gnn_W1"][2 * P:2 * P + 1, :]),
                 ("M2", A["L1_gnn_W2"][:, :]), ("src_i", A["src"][:, :]), ("dst_i", A["dst"][:, :]),
                 ("slot_i", A["slot_ids"][:, :])]
        spread = [("b1r", "L0_gnn_b1"), ("b2r", "L0_gnn_b2"), ("b3r", "L0_gnn_b3"),
                  ("m2r", "L1_gnn_b2"), ("c2r", "L1_gnn_c2")]
        cols = [("b1", "L0_gnn_b1"), ("b2", "L0_gnn_b2"), ("mb1", "L1_gnn_b1"), ("c1", "L1_gnn_c1")]
        loads = len(plain) + len(spread) + len(cols) + 3 + 6

        with nc.Block() as block:
            @block.sync
            def _(sp):
                for name, src in plain:
                    sp.dma_start(K[name][:, :], src).then_inc(loaded, 16)
                sp.dma_start(w3raw[:, :], A["L0_gnn_W3"][:, :]).then_inc(loaded, 16)
                sp.dma_start(prev_i[:, :], A["dst_before"][:, :]).then_inc(loaded, 16)
                sp.dma_start(next_i[:, :], A["dst_after"][:, :]).then_inc(loaded, 16)
                for name, src in spread:
                    sp.dma_start(K[name][:, :], A[src].partition_broadcast(P)).then_inc(loaded, 16)
                for name, src in cols:
                    sp.dma_start(K[name][:, :], A[src].rearrange("(p a) -> p a", a=1)).then_inc(loaded, 16)
                for l in LAYERS:
                    for k in "sd":
                        sp.dma_start(att[k, l][:, :], A[f"L0_gnn_a{k}{l}"].rearrange("h c -> (h c)")
                                     .partition_broadcast(P)).then_inc(loaded, 16)
                sp.dma_start(T["map"].rearrange("(p n) a -> p (n a)", p=P),
                             A["node_ids"].rearrange("(p n) a -> p (n a)", p=P)).then_inc(mapped, 16)
                sp.wait_ge(mapped, 16)

            @block.vector
            def _(v):
                nc.vector.memset(K["eps"][:, :], EPS)
                v.wait_ge(loaded, 16 * loads)
                nc.vector.tensor_scalar(K["W3"][:, :], w3raw[:, :], 1.0 / H, None, ALU.mult)
                for src, dst in ((K["dst_i"], dstf), (prev_i, prevf), (next_i, nextf), (K["slot_i"], slotf)):
                    nc.vector.tensor_copy(dst[:, :], src[:, :])
                v.drain()
                nc.vector.tensor_reduce(K["W3m"][:, :], K["W3"][:, :].rearrange("p (h c) -> p c h", h=H), AX.X, ALU.add)
                for l in LAYERS:
                    w = {1: K["W1"], 2: K["W2"], 3: w3raw}[l]
                    n = P if l < 3 else H * P
                    for i, k in enumerate("sd"):
                        nc.vector.tensor_tensor(prod[:, 0:n], w[:, :], att[k, l][:, :], ALU.mult)
                        v.drain()
                        nc.vector.tensor_reduce(K[f"A{l}"][:, i * H:i * H + H],
                                                prod[:, 0:n].rearrange("p (h c) -> p h c", h=H), AX.X, ALU.add)
                        v.drain()
                first = dstf[:, 0:1]
                nc.vector.tensor_tensor(work[:, :], dstf[:, :], prevf[:, :], ALU.is_equal)
                nc.vector.tensor_tensor(K["goes_on"][:, :], dstf[:, :], nextf[:, :], ALU.is_equal)
                nc.vector.tensor_scalar(inhead[:, :], dstf[:, :], first, None, ALU.is_equal)
                v.drain()
                nc.vector.tensor_scalar(K["fresh"][:, :], work[:, :], -1.0, BIG, ALU.add, ALU.mult)
                nc.vector.tensor_scalar(K["joins"][:, :], work[:, 0:1], -1.0, BIG, ALU.add, ALU.mult)
                nc.vector.tensor_scalar(K["last"][:, :], K["goes_on"][:, :], -1.0, 1.0, ALU.mult, ALU.add)
                nc.vector.tensor_tensor(ends[:, 0:1], work[:, 0:1], inhead[:, COLS - 1:COLS], ALU.mult)
                nc.vector.tensor_tensor(ends[:, 1:2], K["goes_on"][:, COLS - 1:COLS],
                                        inhead[:, COLS - 1:COLS], ALU.mult)
                v.drain()
                nc.vector.memset(K["fresh"][:, 0:1], -BIG)
                nc.vector.tensor_tensor(K["headend"][:, :], K["last"][:, :], inhead[:, :], ALU.mult)
                nc.vector.tensor_scalar(ends[:, 2:3], ends[:, 0:1], -1.0, BIG, ALU.add, ALU.mult)
                nc.vector.tensor_scalar(ends[:, 3:4], ends[:, 1:2], FAR, None, ALU.mult)
                nc.vector.scalar_tensor_tensor(work[:, :], K["goes_on"][:, :], FAR, dstf[:, :], ALU.mult, ALU.add)
                v.drain()
                nc.vector.tensor_copy(K["scat_i"][:, :], work[:, :])
                nc.vector.tensor_copy(wide[:, :], ends[:, 2:3].to_broadcast([P, P]))
                nc.vector.tensor_tensor(prevf[:, :], K["headend"][:, :], slotf[:, :], ALU.mult)
                nc.vector.tensor_tensor(nextf[:, 0:1], dstf[:, 0:1], ends[:, 3:4], ALU.add)
                v.drain()
                nc.vector.tensor_reduce(work[:, 0:1], prevf[:, :], AX.X, ALU.add)
                nc.vector.tensor_copy(K["head_out_i"][:, :], nextf[:, 0:1])
                v.drain().then_inc(built, 1)
                nc.vector.tensor_scalar(work[:, 1:2], work[:, 0:1], float(NP), float(NP), ALU.max, ALU.subtract)
                nc.vector.tensor_scalar(work[:, 3:4], work[:, 0:1], float(NP), None, ALU.max)
                nc.vector.tensor_scalar(K["not_headend"][:, :], K["headend"][:, :], -1.0, 1.0, ALU.mult, ALU.add)
                nc.vector.tensor_tensor(work[:, 2:3], work[:, 0:1], ends[:, 3:4], ALU.add)
                v.drain()
                nc.vector.tensor_copy(K["head_slot_i"][:, :], work[:, 1:2])
                nc.vector.tensor_copy(K["head_row_i"][:, :], work[:, 2:3])
                nc.vector.tensor_copy(K["head_read_i"][:, :], work[:, 3:4])
                v.wait_ge(turned, 1)
                nc.vector.tensor_copy(K["chain"][:, :], ps[:, 0:P])

            @block.tensor
            def _(pe):
                pe.wait_ge(built, 1)
                nc.tensor.transpose(ps[:, 0:P], wide[:, :], K["ident"][:, :]).then_inc(turned, 1)

        clear_semaphores(nc, used)


def map_nodes(nc, K, T):
    with ExitStack() as ctx:
        def sb(name, shape, dt=FP32):
            return ctx.enter_context(nc.sbuf_tensor(name, shape, dt))

        used = []

        def sem(name):
            used.append(ctx.enter_context(nc.semaphore(name)))
            return used[-1]

        to = [sb(f"map_to{b}", [P, MG], I32) for b in range(2)]
        val = [sb(f"map_val{b}", [P, MG], I32) for b in range(2)]
        tail_to = sb("map_tail_to", [P, 1], I32)
        work = sb("map_work", [P, COLS])
        slotf = sb("map_slot", [P, COLS])
        staged, tick, kept = sem("m_staged"), sem("m_tick"), sem("m_kept")
        sent, fetched = ([K["dma_sem"](f"m_{s}{b}") for b in range(2)] for s in ("sent", "fetched"))
        tailed = K["dma_sem"]("m_tailed")
        groups = COLS // MG
        assert groups % 2 == 1

        def scatter(g, b, col, stage_no, turn):
            nc.gpsimd.tensor_copy(to[b][:, :], K["scat_i"][:, col]).then_inc(staged, 1)
            nc.gpsimd.tensor_copy(val[b][:, :], K["slot_i"][:, col]).then_inc(staged, 1)
            g.wait_ge(staged, stage_no)
            g.sem_inc(tick, 1)
            for t in range(MG):
                g.indirect_dma_start(T["map"][:, :], bass.IndirectOffsetOnAxis(ap=to[b][:, t:t + 1], axis=0),
                                     val[b][:, t:t + 1], None, bounds_check=NP - 1,
                                     oob_is_err=False).then_inc(sent[b], 16)

        def gather(g, b, col, stage_no):
            nc.gpsimd.tensor_copy(to[b][:, :], K["src_i"][:, col]).then_inc(staged, 1)
            g.wait_ge(staged, stage_no)
            g.sem_inc(tick, 1)
            for t in range(MG):
                g.indirect_dma_start(val[b][:, t:t + 1], None, T["map"][:, :],
                                     bass.IndirectOffsetOnAxis(ap=to[b][:, t:t + 1], axis=0)).then_inc(fetched[b], 16)

        with nc.Block() as block:
            @block.gpsimd
            def _(g):
                with g.Fori(0, groups // 2) as it:
                    for b in range(2):
                        scatter(g, b, bass.ds((it * 2 + b) * MG, MG), it * 4 + 2 * b + 2, it)
                    for b in range(2):
                        g.wait_ge(sent[b], (it + 1) * (16 * MG))
                        g.sem_inc(tick, 1)
                half = groups // 2
                scatter(g, 0, slice(COLS - MG, COLS), half * 4 + 2, half)
                g.wait_ge(sent[0], (half + 1) * 16 * MG)
                n0 = half * 4 + 2
                with g.Fori(0, half) as it:
                    for b in range(2):
                        gather(g, b, bass.ds((it * 2 + b) * MG, MG), it * 4 + 2 * b + (n0 + 1))
                        g.wait_ge(fetched[b], (it + 1) * (16 * MG))
                        g.sem_inc(tick, 1)
                        nc.gpsimd.tensor_copy(K["gsrc_i"][:, bass.ds((it * 2 + b) * MG, MG)], val[b][:, :]).then_inc(staged, 1)
                        g.wait_ge(staged, it * 4 + 2 * b + (n0 + 2))
                        g.sem_inc(tick, 1)
                gather(g, 0, slice(COLS - MG, COLS), n0 + 4 * half + 1)
                g.wait_ge(fetched[0], (half + 1) * 16 * MG)
                nc.gpsimd.tensor_copy(K["gsrc_i"][:, COLS - MG:COLS], val[0][:, :]).then_inc(staged, 1)
                nc.gpsimd.tensor_copy(tail_to[:, :], K["dst_i"][:, COLS - 1:COLS]).then_inc(kept, 1)
                g.wait_ge(kept, 1)
                g.indirect_dma_start(K["tail_row_i"][:, :], None, T["map"][:, :],
                                     bass.IndirectOffsetOnAxis(ap=tail_to[:, :], axis=0)).then_inc(tailed, 16)

            @block.vector
            def _(v):
                v.wait_ge(tailed, 16)
                nc.vector.tensor_copy(K["tail"][:, :], K["tail_row_i"][:, :])
                nc.vector.tensor_copy(slotf[:, :], K["slot_i"][:, :])
                v.drain()
                nc.vector.tensor_tensor(work[:, :], slotf[:, :], K["last"][:, :], ALU.mult)
                v.drain()
                nc.vector.tensor_tensor_scan(slotf[:, ::-1], K["goes_on"][:, ::-1], work[:, ::-1],
                                             K["tail"][:, :], ALU.mult, ALU.add)
                v.drain()
                nc.vector.tensor_copy(K["gdst_i"][:, :], slotf[:, :])

        clear_semaphores(nc, used)


def layer_norm_dve(nc, v, y, y_out, stats, aggr, rstd_in, n):
    for t in range(n):
        nc.vector.bn_stats(stats[:, t, :], y[:, t, :])
    v.drain()
    for t in range(n):
        nc.vector.bn_aggr(aggr[:, t, :], stats[:, t, :])
    v.drain()


def layer_norm_apply(nc, v, y, y_out, aggr, rstd, n):
    nc.vector.reciprocal(rstd[:, 1, 0:n], rstd[:, 0, 0:n])
    v.drain()
    for t in range(n):
        ins = nc.vector.tensor_scalar(y_out[:, t, :], y[:, t, :], aggr[:, t, 0:1], rstd[:, 1, t:t + 1],
                                      ALU.subtract, ALU.mult)
    return ins


def over_tiles(ap, n=G):
    return ap.unsqueeze(1).to_broadcast([P, n, ap.shape[-1]])


def dense(nc, A, K, T, out):
    with ExitStack() as ctx:
        def sb(name, shape, dt=FP32):
            return ctx.enter_context(nc.sbuf_tensor(name, shape, dt))

        used = []

        def sem(name):
            used.append(ctx.enter_context(nc.semaphore(name)))
            return used[-1]

        L = range(DLANES)
        x = [sb(f"d_x{i}", [P, G, P]) for i in L]
        fa = [sb(f"d_fa{i}", [P, G * P]) for i in L]
        fb = [sb(f"d_fb{i}", [P, G * P]) for i in L]
        r2 = [sb(f"d_r2{i}", [P, G, ROW]) for i in L]
        r3 = [sb(f"d_r3{i}", [P, G, ROW]) for i in L]
        y = [sb(f"d_y{i}", [P, G, P]) for i in L]
        x1 = [sb(f"d_x1{i}", [P, G, P]) for i in L]
        fin = [sb(f"d_fin{i}", [P, G, P]) for i in L]
        stats = [sb(f"d_stats{i}", [P, G, 6]) for i in L]
        aggr = [sb(f"d_aggr{i}", [P, G, 2]) for i in L]
        rstd = [sb(f"d_rstd{i}", [P, 2, G]) for i in L]
        pa = [ctx.enter_context(nc.psum_tensor(f"d_pa{i}", [P, G * P], FP32)) for i in L]
        pb = [ctx.enter_context(nc.psum_tensor(f"d_pb{i}", [P, G * P], FP32)) for i in L]
        x_in = [K["dma_sem"](f"d_x_in{i}") for i in L]
        x_free = sem("d_x_free")
        stored = [sem(f"d_stored{i}") for i in L]
        rows_free = sem("d_rows_free")
        tick, sp_tick = sem("d_tick"), sem("d_sp_tick")
        pe_s = [sem(f"d_pe{k}") for k in range(8)]
        ev = [sem(f"d_ev{k}") for k in range(8)]
        h2_sum, h2_done, var1, root1, x1_done, var2, root2, fin_done = (
            sem("d_" + s) for s in ("h2_sum", "h2_done", "var1", "root1", "x1_done", "var2", "root2", "fin_done"))
        rounds = NG // DLANES
        rows = [t.rearrange("(g p t) c -> g p (t c)", p=P, t=G)
                for t in (A["x"], T[2][0:NP, :], T[3][0:NP, :], T[4][0:NP, :], out)]
        flat = lambda ap: ap.rearrange("p t c -> p (t c)")
        stores = 4

        with nc.Block() as block:
            @block.gpsimd
            def _(g):
                with g.Fori(0, rounds) as it:
                    for i in L:
                        g.wait_ge(x_free, it * DLANES + i + 1)
                        g.sem_inc(tick, 1)
                        g.dma_start(flat(x[i][:, :, :]), rows[0][bass.ds(it * DLANES + i, 1), :, :].rearrange("a p c -> (a p) c")).then_inc(x_in[i], 16)

            @block.sync
            def _(sp):
                sp.sem_inc(rows_free, DLANES)
                with sp.Fori(0, rounds) as it:
                    def put(k, tile, i):
                        sp.dma_start(rows[k][bass.ds(it * DLANES + i, 1), :, :].rearrange("a p c -> (a p) c"),
                                     flat(tile[i][:, :, :])).then_inc(stored[i], 16)
                    for i in L:
                        sp.wait_ge(ev[2], it * DLANES + i + 1)
                        sp.sem_inc(sp_tick, 1)
                        put(1, r2, i)
                    for i in L:
                        sp.wait_ge(ev[4], it * DLANES + i + 1)
                        sp.sem_inc(sp_tick, 1)
                        put(2, r3, i)
                    for i in L:
                        sp.wait_ge(x1_done, it * DLANES + i + 1)
                        sp.sem_inc(sp_tick, 1)
                        put(3, x1, i)
                    for i in L:
                        sp.wait_ge(fin_done, it * DLANES + i + 1)
                        sp.sem_inc(sp_tick, 1)
                        put(4, fin, i)
                    for i in L:
                        sp.wait_ge(stored[i], (it + 1) * (16 * stores))
                        sp.sem_inc(rows_free, 1)

            @block.tensor
            def _(pe):
                with pe.Fori(0, rounds) as it:
                    def each(stage):
                        for i in L:
                            stage(i, it * DLANES + i + 1)

                    def turn_x(i, n):
                        pe.wait_ge(x_in[i], (it + 1) * 16)
                        pe.wait_ge(ev[7], n)
                        for t in range(G):
                            ins = nc.tensor.transpose(pa[i][:, t * P:(t + 1) * P], x[i][:, t, :], K["ident"][:, :])
                        ins.then_inc(pe_s[0], 1)

                    def times_w1(i, n):
                        pe.wait_ge(ev[0], n)
                        nc.tensor.matmul(pb[i][:, :], K["W1"][:, :], fa[i][:, :], start=True, stop=True).then_inc(pe_s[1], 1)

                    def times_w2(i, n):
                        pe.wait_ge(ev[1], n)
                        for t in range(G):
                            h = fb[i][:, t * P:(t + 1) * P]
                            nc.tensor.matmul(pa[i][:, t * P:(t + 1) * P], h, K["W2"][:, :], start=True, stop=True)
                            ins = nc.tensor.matmul(pb[i][:, t * 2 * H:(t + 1) * 2 * H], h, K["A2"][:, :], start=True, stop=True)
                        ins.then_inc(pe_s[2], 1)

                    def turn_h2(i, n):
                        pe.wait_ge(h2_done, n)
                        for t in range(G):
                            ins = nc.tensor.transpose(pb[i][:, t * P:(t + 1) * P], r3[i][:, t, 0:P], K["ident"][:, :])
                        ins.then_inc(pe_s[3], 1)

                    def times_w3(i, n):
                        pe.wait_ge(ev[3], n)
                        for t in range(G):
                            h = fa[i][:, t * P:(t + 1) * P]
                            nc.tensor.matmul(pa[i][:, t * P:(t + 1) * P], h, K["W3m"][:, :], start=True, stop=True)
                            ins = nc.tensor.matmul(pb[i][:, t * 2 * H:(t + 1) * 2 * H], h, K["A3"][:, :], start=True, stop=True)
                        ins.then_inc(pe_s[4], 1)

                    def turn_x1(i, n):
                        pe.wait_ge(x1_done, n)
                        for t in range(G):
                            ins = nc.tensor.transpose(pa[i][:, t * P:(t + 1) * P], x1[i][:, t, :], K["ident"][:, :])
                        ins.then_inc(pe_s[5], 1)

                    def times_u1(i, n):
                        pe.wait_ge(ev[5], n)
                        nc.tensor.matmul(pb[i][:, :], K["U1a"][:, :], fb[i][:, :], start=True, stop=True).then_inc(pe_s[6], 1)

                    def times_u2(i, n):
                        pe.wait_ge(ev[6], n)
                        for t in range(G):
                            ins = nc.tensor.matmul(pa[i][:, t * P:(t + 1) * P], fa[i][:, t * P:(t + 1) * P], K["U2"][:, :],
                                                   start=True, stop=True)
                        ins.then_inc(pe_s[7], 1)

                    for stage in (turn_x, times_w1, times_w2, turn_h2, times_w3, turn_x1, times_u1, times_u2):
                        each(stage)

            @block.scalar
            def _(act):
                with act.Fori(0, rounds) as it:
                    def each(stage):
                        for i in L:
                            stage(i, it * DLANES + i + 1)

                    def take_x(i, n):
                        act.wait_ge(pe_s[0], n)
                        nc.scalar.activation(fa[i][:, :], pa[i][:, :], ACT.Copy).then_inc(ev[0], 1)

                    def take_h1(i, n):
                        act.wait_ge(pe_s[1], n)
                        nc.scalar.activation(fb[i][:, :], pb[i][:, :], ACT.Relu, bias=K["b1"][:, :]).then_inc(ev[1], 1)

                    def relu_h2(i, n):
                        act.wait_ge(h2_sum, n)
                        act.wait_ge(rows_free, n)
                        nc.scalar.activation(r3[i][:, :, 0:P], y[i][:, :, :], ACT.Relu).then_inc(h2_done, 1)

                    def take_h2(i, n):
                        act.wait_ge(pe_s[3], n)
                        nc.scalar.activation(fa[i][:, :], pb[i][:, :], ACT.Copy).then_inc(ev[3], 1)

                    def root(i, n, ready, done):
                        act.wait_ge(ready, n)
                        nc.scalar.activation(rstd[i][:, 0, :], aggr[i][:, :, 1], ACT.Sqrt, bias=K["eps"][:, :]).then_inc(done, 1)

                    def take_x1(i, n):
                        act.wait_ge(pe_s[5], n)
                        nc.scalar.activation(fb[i][:, :], pa[i][:, :], ACT.Copy).then_inc(ev[5], 1)

                    def take_u(i, n):
                        act.wait_ge(pe_s[6], n)
                        nc.scalar.activation(fa[i][:, :], pb[i][:, :], ACT.Relu, bias=K["c1"][:, :]).then_inc(ev[6], 1)

                    each(take_x)
                    each(take_h1)
                    each(relu_h2)
                    each(take_h2)
                    each(lambda i, n: root(i, n, var1, root1))
                    each(take_x1)
                    each(take_u)
                    each(lambda i, n: root(i, n, var2, root2))

            @block.vector
            def _(v):
                v.sem_inc(x_free, DLANES)
                v.sem_inc(ev[7], DLANES)
                with v.Fori(0, rounds) as it:
                    def each(stage):
                        for i in L:
                            stage(i, it * DLANES + i + 1)

                    def take_xp2(i, n):
                        v.wait_ge(rows_free, n)
                        v.wait_ge(pe_s[2], n)
                        psum = pa[i][:, :].rearrange("p (t c) -> p t c", t=G)
                        nc.vector.tensor_copy(r2[i][:, :, 0:P], psum)
                        nc.vector.tensor_copy(r2[i][:, :, P:ROW], pb[i][:, 0:G * 2 * H].rearrange("p (t c) -> p t c", t=G))
                        nc.vector.tensor_tensor(y[i][:, :, :], psum, over_tiles(K["b2r"][:, :]), ALU.add)
                        v.drain().then_inc(ev[2], 1)
                        v.sem_inc(h2_sum, 1)

                    def residual(i, n):
                        v.wait_ge(pe_s[4], n)
                        nc.vector.tensor_copy(r3[i][:, :, P:ROW], pb[i][:, 0:G * 2 * H].rearrange("p (t c) -> p t c", t=G))
                        nc.vector.tensor_tensor(y[i][:, :, :], pa[i][:, :].rearrange("p (t c) -> p t c", t=G), x[i][:, :, :], ALU.add)
                        v.drain().then_inc(ev[4], 1)
                        v.sem_inc(x_free, 1)
                        nc.vector.tensor_tensor(y[i][:, :, :], y[i][:, :, :], over_tiles(K["b3r"][:, :]), ALU.add)
                        v.drain()
                        layer_norm_dve(nc, v, y[i], None, stats[i], aggr[i], None, G)
                        v.sem_inc(var1, 1)

                    def norm1(i, n):
                        v.wait_ge(root1, n)
                        layer_norm_apply(nc, v, y[i], x1[i], aggr[i], rstd[i], G)
                        v.drain().then_inc(x1_done, 1)

                    def residual2(i, n):
                        v.wait_ge(pe_s[7], n)
                        nc.vector.tensor_tensor(y[i][:, :, :], pa[i][:, :].rearrange("p (t c) -> p t c", t=G), x1[i][:, :, :], ALU.add)
                        v.drain().then_inc(ev[7], 1)
                        nc.vector.tensor_tensor(y[i][:, :, :], y[i][:, :, :], over_tiles(K["c2r"][:, :]), ALU.add)
                        v.drain()
                        layer_norm_dve(nc, v, y[i], None, stats[i], aggr[i], None, G)
                        v.sem_inc(var2, 1)

                    def norm2(i, n):
                        v.wait_ge(root2, n)
                        layer_norm_apply(nc, v, y[i], fin[i], aggr[i], rstd[i], G)
                        v.drain().then_inc(fin_done, 1)

                    for stage in (take_xp2, residual, norm1, residual2, norm2):
                        each(stage)

        clear_semaphores(nc, used)


def attend(nc, A, K, T, layer):
    wd, nacc = WIDE[layer], ACC[layer]
    sw = STATE[layer]
    lanes = range(2)
    with ExitStack() as ctx:
        def name_of(name):
            return f"a{layer}_{name}"

        def sb(name, shape, dt=FP32):
            return ctx.enter_context(nc.sbuf_tensor(name_of(name), shape, dt))

        used = []

        def sem(name):
            used.append(ctx.enter_context(nc.semaphore(name_of(name))))
            return used[-1]

        def bank(name):
            return ctx.enter_context(nc.psum_tensor(name_of(name), [P, G * P], FP32))

        in_w = P if layer == 1 else ROW
        out_w = P if layer == 3 else ROW
        S = [sb(f"src{b}", [P, G, in_w]) for b in lanes]
        D = [sb(f"dst{b}", [P, G, in_w]) for b in lanes]
        idx = [sb(f"idx{b}", [P, G], I32) for b in lanes]
        idd = [sb(f"idd{b}", [P, G], I32) for b in lanes]
        fresh = [sb(f"fresh{b}", [P, G]) for b in lanes]
        st = [sb(f"st{b}", [P, G, sw]) for b in lanes]
        m = [sb(f"m{b}", [P, G + 1, H]) for b in lanes]
        lg = [sb(f"lg{b}", [P, 2, G, H]) for b in lanes]
        lr = [sb(f"lr{b}", [P, 2, G, H]) for b in lanes]
        q = [sb(f"q{b}", [P, G, H]) for b in lanes]
        dd = [sb(f"dd{b}", [P, 3, G, H]) for b in lanes]
        wt = [sb(f"wt{b}", [P, 3, G, H]) for b in lanes]
        msg = [sb(f"msg{b}", [P, G, H, wd + 1]) for b in lanes]
        den = [sb(f"den{b}", [P, 2, G, H]) for b in lanes]
        o = [sb(f"o{b}", [P, G, H, wd]) for b in lanes]
        hf = [sb(f"hf{b}", [P, G, P]) for b in lanes]
        r = [sb(f"r{b}", [P, G, out_w]) for b in lanes]
        pm = [[bank(f"p{b}{k}") for k in range(4)] for b in lanes]
        arrived = [K["dma_sem"](name_of(f"arrived{b}")) for b in lanes]
        d_in = [sem(f"d_in{b}") for b in lanes]
        in_free, tick, sp_tick, staged = sem("in_free"), sem("tick"), sem("sp_tick"), sem("staged")
        f1, expd, f2, ev_st, o_done, h_done = (sem(s) for s in ("f1", "expd", "f2", "ev_st", "o_done", "h_done"))
        turned_h, took_h, times, rows_done = (sem(s) for s in ("turned_h", "took_h", "times", "rows_done"))
        st_stored, r_stored = ([sem(f"{s}{b}") for b in lanes] for s in ("st_stored", "r_stored"))
        st_free = sem("st_free")
        if layer == 1:
            fT = [sb(f"fT{b}", [P, 2, G * P]) for b in lanes]
            al = [sb(f"al{b}", [P, 2, G, 2 * H]) for b in lanes]
            xd_stored = [sem(f"xd_stored{b}") for b in lanes]
            turned, took, proj, took_al = (sem(s) for s in ("turned", "took", "proj", "took_al"))
        if layer < 3:
            hT = [sb(f"hT{b}", [P, G * P]) for b in lanes]
        else:
            zT = sb("zT", [P, H, G * P])
            xr = [sb(f"xr{b}", [P, G, P]) for b in lanes]
            xr_in = [sem(f"xr_in{b}") for b in lanes]
            stats = [sb(f"stats{b}", [P, G, 6]) for b in lanes]
            aggr = [sb(f"aggr{b}", [P, G, 2]) for b in lanes]
            rstd = [sb(f"rstd{b}", [P, 2, G]) for b in lanes]
            y = [sb(f"y{b}", [P, G, P]) for b in lanes]
            var, root, y_read, zfree = sem("var"), sem("root"), sem("y_read"), sem("zfree")

        iters = EG // 2
        flat = lambda ap: ap.rearrange("p t c -> p (t c)")
        slots = lambda ap: ap.rearrange("(p j) c -> p j c", p=P)
        st_rows = slots(T["st", layer])
        next_rows = slots(T[layer + 1][NP:NP + EP, :])
        xd_rows = slots(T["xd"])

        def cols(it, b):
            return bass.ds((it * 2 + b) * G, G)

        with nc.Block() as block:
            @block.gpsimd
            def _(g):
                with g.Fori(0, iters) as it:
                    for b in lanes:
                        n = it * 2 + b + 1
                        g.wait_ge(in_free, n)
                        g.sem_inc(tick, 1)
                        if layer == 1:
                            nc.gpsimd.tensor_copy(idx[b][:, :], K["src_i"][:, cols(it, b)]).then_inc(staged, 1)
                            nc.gpsimd.tensor_copy(idd[b][:, :], K["dst_i"][:, cols(it, b)]).then_inc(staged, 1)
                            g.wait_ge(staged, it * 4 + 2 * b + 2)
                            g.sem_inc(tick, 1)
                            for t in range(G):
                                for rows, at in ((S, idx), (D, idd)):
                                    g.indirect_dma_start(rows[b][:, t, :], None, A["x"][:, :],
                                                         bass.IndirectOffsetOnAxis(ap=at[b][:, t:t + 1], axis=0)).then_inc(arrived[b], 16)
                        else:
                            nc.gpsimd.tensor_copy(idx[b][:, :], K["gsrc_i"][:, cols(it, b)]).then_inc(staged, 1)
                            g.wait_ge(staged, it * 2 + b + 1)
                            g.sem_inc(tick, 1)
                            for t in range(G):
                                g.indirect_dma_start(S[b][:, t, :], None, T[layer][:, :],
                                                     bass.IndirectOffsetOnAxis(ap=idx[b][:, t:t + 1], axis=0)).then_inc(arrived[b], 16)

            per_group = 2 * G if layer == 1 else G

            @block.sync
            def _(sp):
                sp.sem_inc(st_free, 2)
                if layer == 1:
                    sp.sem_inc(in_free, 2)
                with sp.Fori(0, iters) as it:
                    for b in lanes:
                        n = it * 2 + b + 1
                        if layer == 1:
                            sp.wait_ge(arrived[b], (it + 1) * (16 * per_group))
                            sp.sem_inc(sp_tick, 1)
                            sp.dma_start(xd_rows[:, cols(it, b), :], D[b][:, :, :]).then_inc(xd_stored[b], 16)
                        else:
                            sp.wait_ge(in_free, n)
                            sp.sem_inc(sp_tick, 1)
                            sp.dma_start(D[b][:, :, :], slots(T[layer][NP:NP + EP, :])[:, cols(it, b), :]).then_inc(d_in[b], 16)
                            if layer == 3:
                                sp.dma_start(xr[b][:, :, :], xd_rows[:, cols(it, b), :]).then_inc(xr_in[b], 16)
                    if layer == 1:
                        for b in lanes:
                            sp.wait_ge(xd_stored[b], (it + 1) * 16)
                            sp.sem_inc(sp_tick, 1)
                            sp.wait_ge(took, it * 2 + b + 1)
                            sp.sem_inc(in_free, 1)
                    for b in lanes:
                        n = it * 2 + b + 1
                        sp.wait_ge(f2, n)
                        sp.sem_inc(sp_tick, 1)
                        sp.dma_start(st_rows[:, cols(it, b), :], st[b][:, :, :]).then_inc(st_stored[b], 16)
                    for b in lanes:
                        n = it * 2 + b + 1
                        sp.wait_ge(rows_done, n)
                        sp.sem_inc(sp_tick, 1)
                        sp.dma_start(next_rows[:, cols(it, b), :], r[b][:, :, :]).then_inc(r_stored[b], 16)
                    for b in lanes:
                        sp.wait_ge(st_stored[b], (it + 1) * 16)
                        sp.wait_ge(r_stored[b], (it + 1) * 16)
                        sp.sem_inc(st_free, 1)

            @block.tensor
            def _(pe):
                with pe.Fori(0, iters) as it:
                    if layer == 1:
                        for b in lanes:
                            n = it * 2 + b + 1
                            pe.wait_ge(arrived[b], (it + 1) * (16 * per_group))
                            pe.wait_ge(st_free, n)
                            for k, rows in enumerate((S, D)):
                                for t in range(G):
                                    ins = nc.tensor.transpose(pm[b][k][:, t * P:(t + 1) * P], rows[b][:, t, :], K["ident"][:, :])
                            ins.then_inc(turned, 1)
                        for b in lanes:
                            n = it * 2 + b + 1
                            pe.wait_ge(took, n)
                            for k in range(2):
                                for t in range(G):
                                    f = fT[b][:, k, t * P:(t + 1) * P]
                                    nc.tensor.matmul(pm[b][k][:, t * P:(t + 1) * P], f, K["W1"][:, :], start=True, stop=True)
                                    at = (k * G + t) * 2 * H
                                    ins = nc.tensor.matmul(pm[b][2][:, at:at + 2 * H], f, K["A1"][:, :], start=True, stop=True)
                            ins.then_inc(proj, 1)
                    for b in lanes:
                        n = it * 2 + b + 1
                        if layer < 3:
                            pe.wait_ge(h_done, n)
                            for t in range(G):
                                ins = nc.tensor.transpose(pm[b][2][:, t * P:(t + 1) * P], hf[b][:, t, :], K["ident"][:, :])
                            ins.then_inc(turned_h, 1)
                        else:
                            pe.wait_ge(o_done, n)
                            for h in range(H):
                                for t in range(G):
                                    ins = nc.tensor.transpose(pm[b][h][:, t * P:(t + 1) * P], o[b][:, t, h, :], K["ident"][:, :])
                            ins.then_inc(turned_h, 1)
                            pe.wait_ge(took_h, n)
                            for t in range(G):
                                for h in range(H):
                                    ins = nc.tensor.matmul(pm[b][0][:, t * P:(t + 1) * P], zT[:, h, t * P:(t + 1) * P],
                                                           K["W3"][:, h * P:(h + 1) * P], start=(h == 0), stop=(h == H - 1))
                            ins.then_inc(times, 1)
                    if layer < 3:
                        for b in lanes:
                            n = it * 2 + b + 1
                            pe.wait_ge(took_h, n)
                            for t in range(G):
                                h = hT[b][:, t * P:(t + 1) * P]
                                if layer == 1:
                                    nc.tensor.matmul(pm[b][3][:, t * P:(t + 1) * P], h, K["W2"][:, :], start=True, stop=True)
                                ins = nc.tensor.matmul(pm[b][2][:, t * 2 * H:(t + 1) * 2 * H], h, K[f"A{layer + 1}"][:, :],
                                                       start=True, stop=True)
                            ins.then_inc(times, 1)

            @block.scalar
            def _(act):
                if layer == 3:
                    act.sem_inc(zfree, 1)
                with act.Fori(0, iters) as it:
                    if layer == 1:
                        for b in lanes:
                            n = it * 2 + b + 1
                            act.wait_ge(turned, n)
                            for k in range(2):
                                ins = nc.scalar.activation(fT[b][:, k, :], pm[b][k][:, :], ACT.Copy)
                            ins.then_inc(took, 1)
                        for b in lanes:
                            n = it * 2 + b + 1
                            act.wait_ge(proj, n)
                            nc.scalar.activation(al[b][:, :, :, :].rearrange("p k t c -> p (k t c)"), pm[b][2][:, 0:2 * G * 2 * H], ACT.Copy)
                            nc.scalar.activation(st[b][:, :, sw - P:sw], pm[b][1][:, :].rearrange("p (t c) -> p t c", t=G),
                                                 ACT.Copy).then_inc(took_al, 1)
                    for b in lanes:
                        n = it * 2 + b + 1
                        act.wait_ge(f1, n)
                        nc.scalar.activation(wt[b][:, :, :, :].rearrange("p k t h -> p (k t h)"),
                                             dd[b][:, :, :, :].rearrange("p k t h -> p (k t h)"), ACT.Exp).then_inc(expd, 1)
                    if layer < 3:
                        for b in lanes:
                            n = it * 2 + b + 1
                            act.wait_ge(o_done, n)
                            nc.scalar.activation(flat(hf[b][:, :, :]), o[b][:, :, :, :].rearrange("p t h c -> p (t h c)"), ACT.Relu).then_inc(h_done, 1)
                    for b in lanes:
                        n = it * 2 + b + 1
                        act.wait_ge(turned_h, n)
                        if layer < 3:
                            nc.scalar.activation(hT[b][:, :], pm[b][2][:, :], ACT.Copy).then_inc(took_h, 1)
                        else:
                            act.wait_ge(zfree, n)
                            for h in range(H):
                                ins = nc.scalar.activation(zT[:, h, :], pm[b][h][:, :], ACT.Copy)
                            ins.then_inc(took_h, 1)
                            act.wait_ge(times, n)
                            act.sem_inc(zfree, 1)
                    if layer == 3:
                        for b in lanes:
                            n = it * 2 + b + 1
                            act.wait_ge(var, n)
                            nc.scalar.activation(rstd[b][:, 0, :], aggr[b][:, :, 1], ACT.Sqrt, bias=K["eps"][:, :]).then_inc(root, 1)

            @block.vector
            def _(v):
                if layer > 1:
                    v.sem_inc(in_free, 2)
                nc.vector.memset(m[1][:, :, :], 0.0)
                nc.vector.memset(st[1][:, G - 1, 0:nacc], 0.0)
                v.drain()
                with v.Fori(0, iters) as it:
                    for b in lanes:
                        n = it * 2 + b + 1
                        v.wait_ge(st_free, n)
                        nc.vector.tensor_copy(fresh[b][:, :], K["fresh"][:, cols(it, b)])
                        if layer == 1:
                            v.wait_ge(took_al, n)
                            nc.vector.tensor_tensor(lg[b][:, 0, :, :], al[b][:, 0, :, 0:H], al[b][:, 1, :, H:2 * H], ALU.add)
                            nc.vector.tensor_tensor(lg[b][:, 1, :, :], al[b][:, 1, :, 0:H], al[b][:, 1, :, H:2 * H], ALU.add)
                        else:
                            v.wait_ge(arrived[b], (it + 1) * (16 * per_group))
                            held = K["held"][:, :, cols(it, b)].rearrange("p c t -> p t c")
                            nc.vector.tensor_tensor(lg[b][:, 0, :, :], S[b][:, :, P:P + H], held[:, :, H:2 * H], ALU.add)
                            nc.vector.tensor_tensor(lg[b][:, 1, :, :], held[:, :, 0:H], held[:, :, H:2 * H], ALU.add)
                        nc.vector.tensor_copy(m[b][:, 0, :], m[1 - b][:, G, :])
                        v.drain()
                        logits, leaky = (z[b][:, :, :, :].rearrange("p k t h -> p (k t h)") for z in (lg, lr))
                        nc.vector.scalar_tensor_tensor(leaky, logits, SLOPE, logits, ALU.mult, ALU.max)
                        v.drain()
                        nc.vector.tensor_tensor(q[b][:, :, :], lr[b][:, 0, :, :], lr[b][:, 1, :, :], ALU.max)
                        v.drain()
                        for t in range(G):
                            nc.vector.scalar_tensor_tensor(m[b][:, t + 1, :], m[b][:, t, :], fresh[b][:, t:t + 1],
                                                           q[b][:, t, :], ALU.add, ALU.max)
                            v.drain()
                        now = m[b][:, 1:G + 1, :]
                        nc.vector.tensor_tensor(dd[b][:, 0, :, :], m[b][:, 0:G, :], now, ALU.subtract)
                        nc.vector.tensor_tensor(dd[b][:, 1, :, :], lr[b][:, 0, :, :], now, ALU.subtract)
                        nc.vector.tensor_tensor(dd[b][:, 2, :, :], lr[b][:, 1, :, :], now, ALU.subtract)
                        nc.vector.tensor_copy(st[b][:, :, nacc:nacc + H], now)
                        nc.vector.tensor_copy(st[b][:, :, nacc + H:nacc + 2 * H], lr[b][:, 1, :, :])
                        v.drain()
                        nc.vector.tensor_tensor(dd[b][:, 0, :, :], dd[b][:, 0, :, :],
                                                fresh[b][:, :].unsqueeze(2).to_broadcast([P, G, H]), ALU.add)
                        v.drain().then_inc(f1, 1)
                    for b in lanes:
                        n = it * 2 + b + 1
                        v.wait_ge(expd, n)
                        w = wt[b][:, 1, :, :]
                        if layer == 1:
                            rows = pm[b][0][:, :].rearrange("p (t h c) -> p t h c", t=G, h=H)
                        elif layer == 2:
                            rows = S[b][:, :, 0:P].rearrange("p t (h c) -> p t h c", h=H)
                        for t in range(G):
                            src = rows[:, t, :, :] if layer < 3 else S[b][:, t, 0:P].unsqueeze(1).to_broadcast([P, H, P])
                            nc.vector.tensor_tensor(msg[b][:, t, :, 0:wd], src, w[:, t, :].unsqueeze(2).to_broadcast([P, H, wd]), ALU.mult)
                        nc.vector.tensor_copy(msg[b][:, :, :, wd:wd + 1].rearrange("p t h a -> p t (h a)"), w)
                        v.drain()
                        acc = st[b][:, :, 0:nacc].rearrange("p t (h c) -> p t h c", h=H)
                        before = st[1 - b][:, G - 1, 0:nacc].rearrange("p (h c) -> p h c", h=H)
                        for t in range(G):
                            for h in range(H):
                                old = before[:, h, :] if t == 0 else acc[:, t - 1, h, :]
                                nc.vector.scalar_tensor_tensor(acc[:, t, h, :], old, wt[b][:, 0, t, h:h + 1],
                                                               msg[b][:, t, h, :], ALU.mult, ALU.add)
                            v.drain()
                        v.sem_inc(f2, 1)
                        w = wt[b][:, 2, :, :]
                        if layer > 1:
                            v.wait_ge(d_in[b], (it + 1) * 16)
                        if layer == 1:
                            rows = st[b][:, :, sw - P:sw].rearrange("p t (h c) -> p t h c", h=H)
                        elif layer == 2:
                            rows = D[b][:, :, 0:P].rearrange("p t (h c) -> p t h c", h=H)
                        for t in range(G):
                            src = rows[:, t, :, :] if layer < 3 else D[b][:, t, 0:P].unsqueeze(1).to_broadcast([P, H, P])
                            nc.vector.tensor_tensor(o[b][:, t, :, :], src, w[:, t, :].unsqueeze(2).to_broadcast([P, H, wd]), ALU.mult)
                        nc.vector.tensor_tensor(den[b][:, 0, :, :], acc[:, :, :, wd:wd + 1].rearrange("p t h a -> p t (h a)"), w, ALU.add)
                        v.drain()
                        nc.vector.reciprocal(den[b][:, 1, :, :], den[b][:, 0, :, :])
                        nc.vector.tensor_tensor(o[b][:, :, :, :], o[b][:, :, :, :], acc[:, :, :, 0:wd], ALU.add)
                        v.drain()
                        if layer > 1:
                            v.sem_inc(in_free, 1)
                        for t in range(G):
                            nc.vector.tensor_tensor(o[b][:, t, :, :], o[b][:, t, :, :],
                                                    den[b][:, 1, t, :].unsqueeze(2).to_broadcast([P, H, wd]), ALU.mult)
                        v.drain()
                        if layer < 3:
                            oo = o[b][:, :, :, :].rearrange("p t h c -> p t (h c)")
                            nc.vector.tensor_tensor(oo, oo, over_tiles(K[f"b{layer}r"][:, :]), ALU.add)
                            v.drain()
                        v.sem_inc(o_done, 1)
                    if layer < 3:
                        for b in lanes:
                            n = it * 2 + b + 1
                            v.wait_ge(times, n)
                            logits = pm[b][2][:, 0:G * 2 * H].rearrange("p (t c) -> p t c", t=G)
                            if layer == 1:
                                nc.vector.tensor_copy(r[b][:, :, 0:P], pm[b][3][:, :].rearrange("p (t c) -> p t c", t=G))
                            else:
                                nc.vector.tensor_copy(r[b][:, :, 0:P], hf[b][:, :, :])
                            nc.vector.tensor_copy(r[b][:, :, P:ROW], logits)
                            nc.vector.tensor_copy(K["held"][:, :, cols(it, b)].rearrange("p c t -> p t c"), logits)
                            v.drain().then_inc(rows_done, 1)
                    else:
                        for b in lanes:
                            n = it * 2 + b + 1
                            v.wait_ge(times, n)
                            v.wait_ge(xr_in[b], (it + 1) * 16)
                            nc.vector.tensor_tensor(y[b][:, :, :], pm[b][0][:, :].rearrange("p (t c) -> p t c", t=G), xr[b][:, :, :], ALU.add)
                            v.drain()
                            nc.vector.tensor_tensor(y[b][:, :, :], y[b][:, :, :], over_tiles(K["b3r"][:, :]), ALU.add)
                            v.drain()
                            layer_norm_dve(nc, v, y[b], None, stats[b], aggr[b], None, G)
                            v.sem_inc(var, 1)
                        for b in lanes:
                            n = it * 2 + b + 1
                            v.wait_ge(root, n)
                            layer_norm_apply(nc, v, y[b], r[b], aggr[b], rstd[b], G)
                            v.drain().then_inc(rows_done, 1)
                nc.vector.tensor_copy(K["carry_m"][:, :], m[1][:, G, :])
                nc.vector.tensor_copy(K["carry_acc"][:, 0:nacc], st[1][:, G - 1, 0:nacc])

        clear_semaphores(nc, used)


def seam_attend(nc, K, T, layer):
    wd, nacc, sw = WIDE[layer], ACC[layer], STATE[layer]
    blocks = 1 if layer < 3 else H
    hb = H // blocks
    with ExitStack() as ctx:
        def sb(name, shape, dt=FP32):
            return ctx.enter_context(nc.sbuf_tensor(f"s{layer}_{name}", shape, dt))

        used = []

        def sem(name):
            used.append(ctx.enter_context(nc.semaphore(f"s{layer}_{name}")))
            return used[-1]

        def bank(name):
            return ctx.enter_context(nc.psum_tensor(f"s{layer}_{name}", [P, 512], FP32))

        out_w = P if layer == 3 else ROW
        head = sb("head", [P, sw])
        xrow = sb("xrow", [P, ROW])
        tin = [sb(f"tin{k}", [P, 3, P]) for k in range(blocks)]
        tT = sb("tT", [P, 3, P])
        run = sb("run", [P, 3, P + 1])
        ex = sb("ex", [P, 2, P])
        we = sb("we", [P, 2, P])
        tw = sb("tw", [P, 2, P])
        cin = sb("cin", [P, 3, P])
        hm = sb("hm", [P, 4, P])
        e3 = sb("e3", [P, 3, P])
        w3 = sb("w3", [P, 3, P])
        u = sb("u", [P, 5, P])
        z = sb("z", [P, H, P] if layer == 3 else [P, 1, P])
        zT = sb("zT", [P, H, P] if layer == 3 else [P, 1, P])
        r = sb("r", [P, out_w])
        xr = sb("xr", [P, P])
        y = sb("y", [P, 1, P])
        stats, aggr, rstd = sb("stats", [P, 1, 6]), sb("aggr", [P, 1, 2]), sb("rstd", [P, 2, 1])
        val = sb("val", [P, 2 * H])
        pt, pback, ph, pr, pa = bank("pt"), bank("pback"), bank("ph"), bank("pr"), bank("pa")
        got, put = K["dma_sem"](f"s{layer}_got"), K["dma_sem"](f"s{layer}_put")
        packed, turned, f1, x1, carried, back, f2, x2, zdone, zturn, ztook, prod, rdone, var, root = (
            sem(s) for s in ("packed", "turned", "f1", "x1", "carried", "back", "f2", "x2", "zdone",
                             "zturn", "ztook", "prod", "rdone", "var", "root"))

        with nc.Block() as block:
            @block.gpsimd
            def _(g):
                at = bass.IndirectOffsetOnAxis(ap=K["head_slot_i"][:, :], axis=0)
                g.indirect_dma_start(head[:, :], None, T["st", layer][:, :], at).then_inc(got, 16)
                if layer > 1:
                    g.indirect_dma_start(xrow[:, :], None, T[layer][:, :],
                                         bass.IndirectOffsetOnAxis(ap=K["head_read_i"][:, :], axis=0)).then_inc(got, 16)
                if layer == 3:
                    g.indirect_dma_start(xr[:, :], None, T["xd"][:, :], at).then_inc(got, 16)
                g.wait_ge(rdone, 1)
                g.indirect_dma_start(T[layer + 1][:, :], bass.IndirectOffsetOnAxis(ap=K["head_row_i"][:, :], axis=0),
                                     r[:, :], None, bounds_check=NP + EP - 1, oob_is_err=False).then_inc(put, 16)
                g.wait_ge(put, 16)

            n_got = 16 * (1 + (layer > 1) + (layer == 3))

            @block.tensor
            def _(pe):
                for k in range(blocks):
                    pe.wait_ge(packed, k + 1)
                    for i in range(3):
                        ins = nc.tensor.transpose(pt[:, i * P:(i + 1) * P], tin[k][:, i, :], K["ident"][:, :])
                    ins.then_inc(turned, 1)
                    pe.wait_ge(carried, k + 1)
                    for i in range(3):
                        ins = nc.tensor.transpose(pback[:, i * P:(i + 1) * P], run[:, i, 0:P], K["ident"][:, :])
                    ins.then_inc(back, 1)
                pe.wait_ge(zdone, 1)
                for k in range(blocks):
                    ins = nc.tensor.transpose(ph[:, k * P:(k + 1) * P], z[:, k, :], K["ident"][:, :])
                ins.then_inc(zturn, 1)
                pe.wait_ge(ztook, 1)
                if layer == 3:
                    for k in range(H):
                        ins = nc.tensor.matmul(pr[:, 0:P], zT[:, k, :], K["W3"][:, k * P:(k + 1) * P], start=(k == 0), stop=(k == H - 1))
                else:
                    if layer == 1:
                        nc.tensor.matmul(pr[:, 0:P], zT[:, 0, :], K["W2"][:, :], start=True, stop=True)
                    ins = nc.tensor.matmul(pa[:, 0:2 * H], zT[:, 0, :], K[f"A{layer + 1}"][:, :], start=True, stop=True)
                ins.then_inc(prod, 1)

            @block.scalar
            def _(act):
                for k in range(blocks):
                    act.wait_ge(f1, k + 1)
                    nc.scalar.activation(we[:, :, :], ex[:, :, :], ACT.Exp).then_inc(x1, 1)
                    act.wait_ge(f2, k + 1)
                    nc.scalar.activation(w3[:, :, :], e3[:, :, :], ACT.Exp).then_inc(x2, 1)
                act.wait_ge(zturn, 1)
                nc.scalar.activation(zT[:, :, :].rearrange("p k c -> p (k c)"), ph[:, 0:blocks * P], ACT.Copy).then_inc(ztook, 1)
                if layer == 3:
                    act.wait_ge(var, 1)
                    nc.scalar.activation(rstd[:, 0, :], aggr[:, :, 1], ACT.Sqrt, bias=K["eps"][:, :]).then_inc(root, 1)

            @block.vector
            def _(v):
                def of_heads(ap, k):
                    return ap[:, k * hb:(k + 1) * hb].unsqueeze(2).to_broadcast([P, hb, wd])

                def heads(ap):
                    return ap.rearrange("p (h c) -> p h c", h=hb)

                tail_acc = K["carry_acc"][:, 0:nacc].rearrange("p (h c) -> p h c", h=H)
                head_acc = head[:, 0:nacc].rearrange("p (h c) -> p h c", h=H)
                nc.vector.memset(run[:, :, :], 0.0)
                v.wait_ge(got, n_got)
                for k in range(blocks):
                    hs = slice(k * hb, (k + 1) * hb)
                    nc.vector.tensor_copy(heads(tin[k][:, 0, :]), of_heads(K["carry_m"][:, :], k))
                    nc.vector.tensor_copy(heads(tin[k][:, 1, :]), tail_acc[:, hs, wd:wd + 1].to_broadcast([P, hb, wd]))
                    nc.vector.tensor_copy(heads(tin[k][:, 2, :]), tail_acc[:, hs, 0:wd])
                    v.drain().then_inc(packed, 1)
                    v.wait_ge(turned, k + 1)
                    nc.vector.tensor_copy(tT[:, :, :].rearrange("p i c -> p (i c)"), pt[:, 0:3 * P])
                    v.drain()
                    nc.vector.tensor_tensor_scan(run[:, 0, 1:P + 1], K["chain"][:, :], tT[:, 0, :], 0.0, ALU.add, ALU.max)
                    v.drain()
                    nc.vector.tensor_tensor(ex[:, 0, :], run[:, 0, 0:P], run[:, 0, 1:P + 1], ALU.subtract)
                    nc.vector.tensor_tensor(ex[:, 1, :], tT[:, 0, :], run[:, 0, 1:P + 1], ALU.subtract)
                    v.drain()
                    nc.vector.tensor_tensor(ex[:, 0, :], ex[:, 0, :], K["chain"][:, :], ALU.add)
                    v.drain().then_inc(f1, 1)
                    v.wait_ge(x1, k + 1)
                    for i in range(2):
                        nc.vector.tensor_tensor(tw[:, i, :], tT[:, i + 1, :], we[:, 1, :], ALU.mult)
                    v.drain()
                    for i in range(2):
                        nc.vector.tensor_tensor_scan(run[:, i + 1, 1:P + 1], we[:, 0, :], tw[:, i, :], 0.0, ALU.mult, ALU.add)
                    v.drain().then_inc(carried, 1)
                    v.wait_ge(back, k + 1)
                    nc.vector.tensor_copy(cin[:, :, :].rearrange("p i c -> p (i c)"), pback[:, 0:3 * P])
                    nc.vector.tensor_copy(heads(hm[:, 0, :]), of_heads(head[:, nacc:nacc + H], k))
                    nc.vector.tensor_copy(heads(hm[:, 1, :]), head_acc[:, hs, wd:wd + 1].to_broadcast([P, hb, wd]))
                    nc.vector.tensor_copy(heads(hm[:, 2, :]), of_heads(head[:, nacc + H:nacc + 2 * H], k))
                    v.drain()
                    nc.vector.tensor_scalar(cin[:, 0, :], cin[:, 0, :], K["joins"][:, :], None, ALU.add)
                    v.drain()
                    nc.vector.tensor_tensor(hm[:, 3, :], cin[:, 0, :], hm[:, 0, :], ALU.max)
                    v.drain()
                    nc.vector.tensor_tensor(e3[:, 0, :], cin[:, 0, :], hm[:, 3, :], ALU.subtract)
                    nc.vector.tensor_tensor(e3[:, 1, :], hm[:, 0, :], hm[:, 3, :], ALU.subtract)
                    nc.vector.tensor_tensor(e3[:, 2, :], hm[:, 2, :], hm[:, 3, :], ALU.subtract)
                    v.drain().then_inc(f2, 1)
                    v.wait_ge(x2, k + 1)
                    nc.vector.tensor_tensor(u[:, 0, :], cin[:, 1, :], w3[:, 0, :], ALU.mult)
                    nc.vector.tensor_tensor(u[:, 1, :], hm[:, 1, :], w3[:, 1, :], ALU.mult)
                    nc.vector.tensor_tensor(u[:, 2, :], cin[:, 2, :], w3[:, 0, :], ALU.mult)
                    nc.vector.tensor_tensor(heads(u[:, 3, :]), head_acc[:, hs, 0:wd], heads(w3[:, 1, :]), ALU.mult)
                    xd = head[:, sw - P:sw] if layer == 1 else xrow[:, 0:P]
                    nc.vector.tensor_tensor(u[:, 4, :], xd, w3[:, 2, :], ALU.mult)
                    v.drain()
                    nc.vector.tensor_tensor(u[:, 0, :], u[:, 0, :], u[:, 1, :], ALU.add)
                    nc.vector.tensor_tensor(u[:, 2, :], u[:, 2, :], u[:, 3, :], ALU.add)
                    v.drain()
                    nc.vector.tensor_tensor(u[:, 0, :], u[:, 0, :], w3[:, 2, :], ALU.add)
                    nc.vector.tensor_tensor(u[:, 2, :], u[:, 2, :], u[:, 4, :], ALU.add)
                    v.drain()
                    nc.vector.reciprocal(u[:, 1, :], u[:, 0, :])
                    v.drain()
                    nc.vector.tensor_tensor(z[:, k, :], u[:, 2, :], u[:, 1, :], ALU.mult)
                    v.drain()
                if layer < 3:
                    nc.vector.tensor_tensor(z[:, 0, :], z[:, 0, :], K[f"b{layer}r"][:, :], ALU.add)
                    v.drain()
                    nc.vector.tensor_scalar(z[:, 0, :], z[:, 0, :], 0.0, None, ALU.max)
                    v.drain()
                v.sem_inc(zdone, 1)
                v.wait_ge(prod, 1)
                if layer < 3:
                    nc.vector.tensor_copy(r[:, 0:P], pr[:, 0:P] if layer == 1 else z[:, 0, :])
                    nc.vector.tensor_copy(r[:, P:ROW], pa[:, 0:2 * H])
                    nc.vector.tensor_copy(val[:, :], pa[:, 0:2 * H])
                    v.drain().then_inc(rdone, 1)
                    for c in range(2 * H):
                        old = K["held"][:, c, :]
                        nc.vector.tensor_tensor(old, old, K["not_headend"][:, :], ALU.mult)
                    v.drain()
                    for c in range(2 * H):
                        old = K["held"][:, c, :]
                        nc.vector.scalar_tensor_tensor(old, K["headend"][:, :], val[:, c:c + 1], old, ALU.mult, ALU.add)
                else:
                    nc.vector.tensor_tensor(y[:, 0, :], pr[:, 0:P], xr[:, :], ALU.add)
                    v.drain()
                    nc.vector.tensor_tensor(y[:, 0, :], y[:, 0, :], K["b3r"][:, :], ALU.add)
                    v.drain()
                    layer_norm_dve(nc, v, y, None, stats, aggr, None, 1)
                    v.sem_inc(var, 1)
                    v.wait_ge(root, 1)
                    layer_norm_apply(nc, v, y, r[:, :].unsqueeze(1), aggr, rstd, 1)
                    v.drain().then_inc(rdone, 1)

        clear_semaphores(nc, used)


def hold_logits(nc, K, T, layer):
    with ExitStack() as ctx:
        tail = ctx.enter_context(nc.sbuf_tensor(f"h{layer}_tail", [P, ROW], FP32))
        masked = ctx.enter_context(nc.sbuf_tensor(f"h{layer}_masked", [P, 2 * H, COLS], FP32))
        got = K["dma_sem"](f"h{layer}_got")
        with nc.Block() as block:
            @block.gpsimd
            def _(g):
                g.indirect_dma_start(tail[:, :], None, T[layer][:, :],
                                     bass.IndirectOffsetOnAxis(ap=K["tail_row_i"][:, :], axis=0)).then_inc(got, 16)

            @block.vector
            def _(v):
                for c in range(2 * H):
                    nc.vector.tensor_tensor(masked[:, c, :], K["held"][:, c, :], K["last"][:, :], ALU.mult)
                v.wait_ge(got, 16)
                v.drain()
                for c in range(2 * H):
                    nc.vector.tensor_tensor_scan(K["held"][:, c, ::-1], K["goes_on"][:, ::-1], masked[:, c, ::-1],
                                                 tail[:, P + c:P + c + 1], ALU.mult, ALU.add)

def message(nc, A, K, T, out):
    lanes = range(2)
    with ExitStack() as ctx:
        def sb(name, shape, dt=FP32):
            return ctx.enter_context(nc.sbuf_tensor("e_" + name, shape, dt))

        used = []

        def sem(name):
            used.append(ctx.enter_context(nc.semaphore("e_" + name)))
            return used[-1]

        S = [sb(f"src{b}", [P, G, P]) for b in lanes]
        D = [sb(f"dst{b}", [P, G, P]) for b in lanes]
        idx = [sb(f"idx{b}", [P, 3, G], I32) for b in lanes]
        wrow = [sb(f"wrow{b}", [1, G * P]) for b in lanes]
        fresh = [sb(f"fresh{b}", [P, G]) for b in lanes]
        sT = [sb(f"sT{b}", [P, G * P]) for b in lanes]
        dT = [sb(f"dT{b}", [P, G * P]) for b in lanes]
        rT = [sb(f"rT{b}", [P, G * P]) for b in lanes]
        gT = [sb(f"gT{b}", [P, G * P]) for b in lanes]
        uT = [sb(f"uT{b}", [P, G * P]) for b in lanes]
        agg = [sb(f"agg{b}", [P, G, P]) for b in lanes]
        gb = [sb(f"gb{b}", [P, G, P]) for b in lanes]
        y = [sb(f"y{b}", [P, G, P]) for b in lanes]
        fin = [sb(f"fin{b}", [P, G, P]) for b in lanes]
        to = [sb(f"to{b}", [P, G], I32) for b in lanes]
        stats = [sb(f"stats{b}", [P, G, 6]) for b in lanes]
        aggr = [sb(f"aggr{b}", [P, G, 2]) for b in lanes]
        rstd = [sb(f"rstd{b}", [P, 2, G]) for b in lanes]
        pm = [[ctx.enter_context(nc.psum_tensor(f"e_p{b}{k}", [P, G * P], FP32)) for k in range(4)] for b in lanes]
        w_in, agg_stored = ([sem(f"{s}{b}") for b in lanes] for s in ("w_in", "agg_stored"))
        arrived, sent = ([K["dma_sem"](f"e_{s}{b}") for b in lanes] for s in ("arrived", "sent"))
        (in_free, tick, staged, turned, took, pre, took_r, msgs, maxed, gsum, turned_g, took_g, upd, took_u, last_mm,
         var, root, fin_done, out_free, w_free, agg_free) = (
            sem(s) for s in ("in_free", "tick", "staged", "turned", "took", "pre", "took_r", "msgs", "maxed", "gsum",
                             "turned_g", "took_g", "upd", "took_u", "last_mm", "var", "root", "fin_done", "out_free", "w_free", "agg_free"))
        sp_tick = sem("sp_tick")
        iters = EG // 2

        def cols(it, b):
            return bass.ds((it * 2 + b) * G, G)

        w_rows = A["w"].rearrange("(g t) p -> g (t p)", t=G)
        agg_rows = T["st", 4].rearrange("(p j) c -> p j c", p=P)

        with nc.Block() as block:
            @block.gpsimd
            def _(g):
                def gather(it, b, n, stage_no, col):
                    g.wait_ge(in_free, n)
                    g.sem_inc(tick, 1)
                    nc.gpsimd.tensor_copy(idx[b][:, 0, :], K["gsrc_i"][:, col]).then_inc(staged, 1)
                    nc.gpsimd.tensor_copy(idx[b][:, 1, :], K["gdst_i"][:, col]).then_inc(staged, 1)
                    g.wait_ge(staged, stage_no)
                    g.sem_inc(tick, 1)
                    for t in range(G):
                        for k, rows in enumerate((S, D)):
                            g.indirect_dma_start(rows[b][:, t, :], None, T[4][:, :],
                                                 bass.IndirectOffsetOnAxis(ap=idx[b][:, k, t:t + 1], axis=0)).then_inc(arrived[b], 16)

                g.sem_inc(in_free, 2)
                with g.Fori(0, iters) as it:
                    for b in lanes:
                        gather(it, b, it * 2 + b + 1, it * 6 + 2 * b + 2, cols(it, b))
                    for b in lanes:
                        nc.gpsimd.tensor_copy(to[b][:, :], K["scat_i"][:, cols(it, b)]).then_inc(staged, 1)
                    g.wait_ge(staged, it * 6 + 6)
                    g.sem_inc(tick, 1)
                    for b in lanes:
                        g.wait_ge(fin_done, it * 2 + b + 1)
                        g.sem_inc(in_free, 1)
                        for t in range(G):
                            g.indirect_dma_start(out[:, :], bass.IndirectOffsetOnAxis(ap=to[b][:, t:t + 1], axis=0),
                                                 fin[b][:, t, :], None, bounds_check=NP - 1, oob_is_err=False).then_inc(sent[b], 16)
                    for b in lanes:
                        g.wait_ge(sent[b], (it + 1) * (16 * G))
                        g.sem_inc(out_free, 1)

            @block.sync
            def _(sp):
                sp.sem_inc(agg_free, 2)
                with sp.Fori(0, iters) as it:
                    for b in lanes:
                        sp.wait_ge(w_free, it * 2 + b + 1)
                        sp.sem_inc(sp_tick, 1)
                        sp.dma_start(wrow[b][:, :], w_rows[bass.ds(it * 2 + b, 1), :]).then_inc(w_in[b], 16)
                    for b in lanes:
                        sp.wait_ge(maxed, it * 2 + b + 1)
                        sp.sem_inc(sp_tick, 1)
                        sp.dma_start(agg_rows[:, cols(it, b), :], agg[b][:, :, :]).then_inc(agg_stored[b], 16)
                    for b in lanes:
                        sp.wait_ge(agg_stored[b], (it + 1) * 16)
                        sp.sem_inc(agg_free, 1)

            @block.tensor
            def _(pe):
                pe.sem_inc(w_free, 2)
                with pe.Fori(0, iters) as it:
                    for b in lanes:
                        pe.wait_ge(arrived[b], (it + 1) * (16 * 2 * G))
                        for k, rows in enumerate((S, D)):
                            for t in range(G):
                                ins = nc.tensor.transpose(pm[b][k][:, t * P:(t + 1) * P], rows[b][:, t, :], K["ident"][:, :])
                        ins.then_inc(turned, 1)
                    for b in lanes:
                        pe.wait_ge(took, it * 2 + b + 1)
                        pe.wait_ge(w_in[b], (it + 1) * 16)
                        nc.tensor.matmul(pm[b][2][:, :], K["M1a"][:, :], sT[b][:, :], start=True, stop=False)
                        nc.tensor.matmul(pm[b][2][:, :], K["M1b"][:, :], dT[b][:, :], start=False, stop=False)
                        nc.tensor.matmul(pm[b][2][:, :], K["w1c"][:, :], wrow[b][:, :], start=False, stop=True).then_inc(pre, 1)
                    for b in lanes:
                        pe.wait_ge(took_r, it * 2 + b + 1)
                        pe.sem_inc(w_free, 1)
                        for t in range(G):
                            ins = nc.tensor.matmul(pm[b][3][:, t * P:(t + 1) * P], rT[b][:, t * P:(t + 1) * P], K["M2"][:, :], start=True, stop=True)
                        ins.then_inc(msgs, 1)
                    for b in lanes:
                        pe.wait_ge(gsum, it * 2 + b + 1)
                        for t in range(G):
                            ins = nc.tensor.transpose(pm[b][0][:, t * P:(t + 1) * P], gb[b][:, t, :], K["ident"][:, :])
                        ins.then_inc(turned_g, 1)
                    for b in lanes:
                        pe.wait_ge(took_g, it * 2 + b + 1)
                        nc.tensor.matmul(pm[b][1][:, :], K["U1a"][:, :], dT[b][:, :], start=True, stop=False)
                        nc.tensor.matmul(pm[b][1][:, :], K["U1b"][:, :], gT[b][:, :], start=False, stop=True).then_inc(upd, 1)
                    for b in lanes:
                        pe.wait_ge(took_u, it * 2 + b + 1)
                        for t in range(G):
                            ins = nc.tensor.matmul(pm[b][2][:, t * P:(t + 1) * P], uT[b][:, t * P:(t + 1) * P], K["U2"][:, :], start=True, stop=True)
                        ins.then_inc(last_mm, 1)

            @block.scalar
            def _(act):
                with act.Fori(0, iters) as it:
                    for b in lanes:
                        act.wait_ge(turned, it * 2 + b + 1)
                        nc.scalar.activation(sT[b][:, :], pm[b][0][:, :], ACT.Copy)
                        nc.scalar.activation(dT[b][:, :], pm[b][1][:, :], ACT.Copy).then_inc(took, 1)
                    for b in lanes:
                        act.wait_ge(pre, it * 2 + b + 1)
                        nc.scalar.activation(rT[b][:, :], pm[b][2][:, :], ACT.Relu, bias=K["mb1"][:, :]).then_inc(took_r, 1)
                    for b in lanes:
                        act.wait_ge(turned_g, it * 2 + b + 1)
                        nc.scalar.activation(gT[b][:, :], pm[b][0][:, :], ACT.Copy).then_inc(took_g, 1)
                    for b in lanes:
                        act.wait_ge(upd, it * 2 + b + 1)
                        nc.scalar.activation(uT[b][:, :], pm[b][1][:, :], ACT.Relu, bias=K["c1"][:, :]).then_inc(took_u, 1)
                    for b in lanes:
                        act.wait_ge(var, it * 2 + b + 1)
                        nc.scalar.activation(rstd[b][:, 0, :], aggr[b][:, :, 1], ACT.Sqrt, bias=K["eps"][:, :]).then_inc(root, 1)

            @block.vector
            def _(v):
                v.sem_inc(out_free, 2)
                nc.vector.memset(agg[1][:, :, :], 0.0)
                v.drain()
                with v.Fori(0, iters) as it:
                    for b in lanes:
                        nc.vector.tensor_copy(fresh[b][:, :], K["fresh"][:, cols(it, b)])
                    v.drain()
                    for b in lanes:
                        n = it * 2 + b + 1
                        v.wait_ge(agg_free, n)
                        v.wait_ge(msgs, n)
                        for t in range(G):
                            old = agg[1 - b][:, G - 1, :] if t == 0 else agg[b][:, t - 1, :]
                            nc.vector.scalar_tensor_tensor(agg[b][:, t, :], old, fresh[b][:, t:t + 1],
                                                           pm[b][3][:, t * P:(t + 1) * P], ALU.add, ALU.max)
                            v.drain()
                        v.sem_inc(maxed, 1)
                        nc.vector.tensor_tensor(gb[b][:, :, :], agg[b][:, :, :], over_tiles(K["m2r"][:, :]), ALU.add)
                        v.drain().then_inc(gsum, 1)
                    for b in lanes:
                        n = it * 2 + b + 1
                        v.wait_ge(last_mm, n)
                        nc.vector.tensor_tensor(y[b][:, :, :], pm[b][2][:, :].rearrange("p (t c) -> p t c", t=G), D[b][:, :, :], ALU.add)
                        v.drain()
                        nc.vector.tensor_tensor(y[b][:, :, :], y[b][:, :, :], over_tiles(K["c2r"][:, :]), ALU.add)
                        v.drain()
                        layer_norm_dve(nc, v, y[b], None, stats[b], aggr[b], None, G)
                        v.sem_inc(var, 1)
                    for b in lanes:
                        n = it * 2 + b + 1
                        v.wait_ge(root, n)
                        v.wait_ge(out_free, n)
                        nc.vector.reciprocal(rstd[b][:, 1, :], rstd[b][:, 0, :])
                        v.drain()
                        for t in range(G):
                            nc.vector.tensor_scalar(fin[b][:, t, :], y[b][:, t, :], aggr[b][:, t, 0:1], rstd[b][:, 1, t:t + 1],
                                                    ALU.subtract, ALU.mult)
                        v.drain().then_inc(fin_done, 1)
                nc.vector.tensor_copy(K["carry_acc"][:, 0:P], agg[1][:, G - 1, :])

        clear_semaphores(nc, used)


def seam_message(nc, K, T, out):
    with ExitStack() as ctx:
        def sb(name, shape, dt=FP32):
            return ctx.enter_context(nc.sbuf_tensor("z_" + name, shape, dt))

        used = []

        def sem(name):
            used.append(ctx.enter_context(nc.semaphore("z_" + name)))
            return used[-1]

        head, xd, g, y, r = sb("head", [P, P]), sb("xd", [P, P]), sb("g", [P, P]), sb("y", [P, 1, P]), sb("r", [P, 1, P])
        tT, run, cin = sb("tT", [P, P]), sb("run", [P, P + 1]), sb("cin", [P, P])
        xT, gT, uT = sb("xT", [P, P]), sb("gT", [P, P]), sb("uT", [P, P])
        stats, aggr, rstd = sb("stats", [P, 1, 6]), sb("aggr", [P, 1, 2]), sb("rstd", [P, 2, 1])
        ps = [ctx.enter_context(nc.psum_tensor(f"z_p{k}", [P, 512], FP32)) for k in range(6)]
        s, a, d = sem("pe"), sem("act"), sem("dve")
        got, put = K["dma_sem"]("z_got"), K["dma_sem"]("z_put")

        with nc.Block() as block:
            @block.gpsimd
            def _(p):
                p.indirect_dma_start(head[:, :], None, T["st", 4][:, :],
                                     bass.IndirectOffsetOnAxis(ap=K["head_slot_i"][:, :], axis=0)).then_inc(got, 16)
                p.indirect_dma_start(xd[:, :], None, T[4][:, :],
                                     bass.IndirectOffsetOnAxis(ap=K["head_read_i"][:, :], axis=0)).then_inc(got, 16)
                p.wait_ge(d, 4)
                p.indirect_dma_start(out[:, :], bass.IndirectOffsetOnAxis(ap=K["head_out_i"][:, :], axis=0),
                                     r[:, 0, :], None, bounds_check=NP - 1, oob_is_err=False).then_inc(put, 16)
                p.wait_ge(put, 16)

            @block.tensor
            def _(pe):
                nc.tensor.transpose(ps[0][:, 0:P], K["carry_acc"][:, 0:P], K["ident"][:, :])
                pe.wait_ge(got, 32)
                nc.tensor.transpose(ps[1][:, 0:P], xd[:, :], K["ident"][:, :]).then_inc(s, 1)
                pe.wait_ge(d, 1)
                nc.tensor.transpose(ps[2][:, 0:P], run[:, 0:P], K["ident"][:, :]).then_inc(s, 1)
                pe.wait_ge(d, 2)
                nc.tensor.transpose(ps[3][:, 0:P], g[:, :], K["ident"][:, :]).then_inc(s, 1)
                pe.wait_ge(a, 2)
                nc.tensor.matmul(ps[4][:, 0:P], K["U1a"][:, :], xT[:, :], start=True, stop=False)
                nc.tensor.matmul(ps[4][:, 0:P], K["U1b"][:, :], gT[:, :], start=False, stop=True).then_inc(s, 1)
                pe.wait_ge(a, 3)
                nc.tensor.matmul(ps[5][:, 0:P], uT[:, :], K["U2"][:, :], start=True, stop=True).then_inc(s, 1)

            @block.scalar
            def _(act):
                act.wait_ge(s, 1)
                nc.scalar.activation(xT[:, :], ps[1][:, 0:P], ACT.Copy).then_inc(a, 1)
                act.wait_ge(s, 3)
                nc.scalar.activation(gT[:, :], ps[3][:, 0:P], ACT.Copy).then_inc(a, 1)
                act.wait_ge(s, 4)
                nc.scalar.activation(uT[:, :], ps[4][:, 0:P], ACT.Relu, bias=K["c1"][:, :]).then_inc(a, 1)
                act.wait_ge(d, 3)
                nc.scalar.activation(rstd[:, 0, :], aggr[:, :, 1], ACT.Sqrt, bias=K["eps"][:, :]).then_inc(a, 1)

            @block.vector
            def _(v):
                nc.vector.memset(run[:, :], 0.0)
                v.wait_ge(s, 1)
                nc.vector.tensor_copy(tT[:, :], ps[0][:, 0:P])
                v.drain()
                nc.vector.tensor_tensor_scan(run[:, 1:P + 1], K["chain"][:, :], tT[:, :], 0.0, ALU.add, ALU.max)
                v.drain().then_inc(d, 1)
                v.wait_ge(s, 2)
                nc.vector.tensor_scalar(cin[:, :], ps[2][:, 0:P], K["joins"][:, :], None, ALU.add)
                v.drain()
                nc.vector.tensor_tensor(cin[:, :], cin[:, :], head[:, :], ALU.max)
                v.drain()
                nc.vector.tensor_tensor(g[:, :], cin[:, :], K["m2r"][:, :], ALU.add)
                v.drain().then_inc(d, 1)
                v.wait_ge(s, 5)
                nc.vector.tensor_tensor(y[:, 0, :], ps[5][:, 0:P], xd[:, :], ALU.add)
                v.drain()
                nc.vector.tensor_tensor(y[:, 0, :], y[:, 0, :], K["c2r"][:, :], ALU.add)
                v.drain()
                layer_norm_dve(nc, v, y, None, stats, aggr, None, 1)
                v.sem_inc(d, 1)
                v.wait_ge(a, 4)
                layer_norm_apply(nc, v, y, r, aggr, rstd, 1)
                v.drain().then_inc(d, 1)

        clear_semaphores(nc, used)



TABLE_KIND = "Internal"



def kernel(**inputs):
    import numpy as _np
    import concourse.bacc as _bacc
    from concourse import mybir as _mybir
    from concourse.bass_utils import run_bass_kernel_spmd as _run

    nc = _bacc.Bacc("TRN2", target_bir_lowering=False, num_devices=1)
    inputs = {k: _np.ascontiguousarray(v) for k, v in inputs.items()}
    x = _np.zeros((NP, P), inputs["x"].dtype)
    x[:N] = inputs["x"]
    pad = EP - E
    src = _np.concatenate([inputs["src"], _np.zeros(pad, inputs["src"].dtype)])
    dst = _np.concatenate([inputs["dst"], _np.full(pad, N, inputs["dst"].dtype)])
    w = _np.concatenate([inputs["edge_weight"], _np.zeros(pad, inputs["edge_weight"].dtype)])
    edge = _np.full(1, -1, dst.dtype)
    arrays = {
        "x": x, "src": src.reshape(P, COLS), "dst": dst.reshape(P, COLS),
        "dst_before": _np.concatenate([edge, dst[:-1]]).reshape(P, COLS),
        "dst_after": _np.concatenate([dst[1:], edge]).reshape(P, COLS),
        "w": _np.ascontiguousarray(w.reshape(P, COLS).T),
        "node_ids": _np.arange(NP, dtype=_np.int32).reshape(NP, 1),
        "slot_ids": (NP + _np.arange(EP, dtype=_np.int32)).reshape(P, COLS),
        "eye": _np.eye(P, dtype=_np.float32),
    }
    for name, value in inputs.items():
        if name.startswith(("L0_", "L1_")):
            arrays[name] = value
    feeds, aps = {}, {}
    for name, a in arrays.items():
        feeds["in_" + name] = a
        aps[name] = nc.dram_tensor("in_" + name, a.shape, _mybir.dt.from_np(a.dtype), kind="ExternalInput").ap()
    out = nc.dram_tensor("out_rows", (NP, P), _mybir.dt.float32, kind="ExternalOutput").ap()
    build(nc, aps, out)
    r = _run(nc, [feeds], core_ids=[0])
    return r.results[0]["out_rows"][:N]
```

```python
import concourse.bass as bass
from concourse import mybir
from contextlib import ExitStack

FP32 = mybir.dt.float32
BF16 = mybir.dt.bfloat16
I32 = mybir.dt.int32
ALU = mybir.AluOpType
ACT = mybir.ActivationFunctionType
AX = mybir.AxisListType

P = 128
N = 100000
E = 50000
H = 4
C = P // H
G = 4
COLS = 392
EP = P * COLS
EG = COLS // G
NG = (N + G * P - 1) // (G * P)
NP = NG * G * P
FAR = float(1 << 22)
BIG = 1e30
ROW = P + 2 * H
SLOPE = 0.2
EPS = 1e-5
DLANES = 4
MG = 8
LAYERS = (1, 2, 3)
BIASES = ("b1", "b2", "b3", "m2", "c2")
WIDE = {1: C, 2: C, 3: P}
ACC = {l: H * (WIDE[l] + 1) for l in LAYERS}
STATE = {1: ACC[1] + 2 * H + P, 2: ACC[2] + 2 * H, 3: ACC[3] + 2 * H, 4: P}


def build(nc, A, out):
    ctx = ExitStack()
    with ctx:
        def sb(name, shape, dt=FP32):
            return ctx.enter_context(nc.sbuf_tensor(name, shape, dt))

        K = {}
        for name in ("ident", "W1", "W2", "W3m", "U1a", "U1b", "U2", "M1a", "M1b", "M2",
                     "b2r", "b3r", "c2r"):
            K[name] = sb("k_" + name, [P, P])
        K["W3"] = sb("k_W3", [P, H * P])
        K["w1c"] = sb("k_w1c", [1, P])
        K["ones"] = sb("k_ones", [P, P], BF16)
        K["parts"] = sb("k_parts", [P, len(BIASES), G, P], BF16)
        for name in ("b1", "b2", "mb1", "c1", "eps"):
            K[name] = sb("k_" + name + "_col", [P, 1])
        for name in ("A1", "A2", "A3"):
            K[name] = sb("k_" + name, [P, 2 * H])
        for name in ("src_i", "dst_i", "scat_i", "slot_i", "gsrc_i", "gdst_i"):
            K[name] = sb("k_" + name, [P, COLS], I32)
        K["fresh"] = sb("k_fresh", [P, COLS])
        K["last"] = sb("k_last", [P, COLS])
        K["goes_on"] = sb("k_goes_on", [P, COLS])
        K["headend"] = sb("k_headend", [P, COLS])
        K["joins"] = sb("k_joins", [P, 1])
        K["chain"] = sb("k_chain", [P, P])
        K["head_slot_i"] = sb("k_head_slot_i", [P, 1], I32)
        K["head_row_i"] = sb("k_head_row_i", [P, 1], I32)
        K["head_out_i"] = sb("k_head_out_i", [P, 1], I32)
        K["tail_row_i"] = sb("k_tail_row_i", [P, 1], I32)
        K["head_read_i"] = sb("k_head_read_i", [P, 1], I32)
        K["not_headend"] = sb("k_not_headend", [P, COLS])
        K["tail"] = sb("k_tail", [P, 1])
        K["held"] = sb("k_held", [P, 2 * H, COLS])
        K["carry_m"] = sb("k_carry_m", [P, H])
        K["carry_acc"] = sb("k_carry_acc", [P, ACC[3]])

        T = {l: nc.dram_tensor(f"table_{l}", [NP + EP, P if l == 4 else ROW], FP32, kind=TABLE_KIND).ap()
             for l in (2, 3, 4)}
        T["map"] = nc.dram_tensor("node_row", [NP, 1], I32, kind=TABLE_KIND).ap()
        T["xd"] = nc.dram_tensor("slot_x", [EP, P], FP32, kind="Internal").ap()
        for l in (1, 2, 3, 4):
            T["st", l] = nc.dram_tensor(f"slot_state_{l}", [EP, STATE[l]], FP32, kind="Internal").ap()

        K["dma_sem"] = lambda name: ctx.enter_context(nc.semaphore(name))

        prepare(nc, A, K, T)
        dense(nc, A, K, T, out)
        look_up_dst(nc, K, T)
        for layer in LAYERS:
            attend(nc, A, K, T, layer)
            seam_attend(nc, K, T, layer)
            if layer < 3:
                hold_logits(nc, K, T, layer + 1)
        message(nc, A, K, T, out)
        seam_message(nc, K, T, out)


def clear_semaphores(nc, used):
    with nc.Block() as block:
        @block.gpsimd
        def _(g):
            for s in used:
                g.sem_clear(s)


def prepare(nc, A, K, T):
    with ExitStack() as ctx:
        def sb(name, shape, dt=FP32):
            return ctx.enter_context(nc.sbuf_tensor(name, shape, dt))

        used = []

        def sem(name):
            used.append(ctx.enter_context(nc.semaphore(name)))
            return used[-1]

        att = {(k, l): sb(f"att_{k}{l}", [P, P if l < 3 else H * P]) for k in "sd" for l in LAYERS}
        prod = sb("prep_prod", [P, H * P])
        w3raw = sb("prep_w3", [P, H * P])
        prev_i = sb("prep_prev_i", [P, COLS], I32)
        next_i = sb("prep_next_i", [P, COLS], I32)
        dstf = sb("prep_dst", [P, COLS])
        prevf = sb("prep_prev", [P, COLS])
        nextf = sb("prep_next", [P, COLS])
        slotf = sb("prep_slot", [P, COLS])
        inhead = sb("prep_inhead", [P, COLS])
        work = sb("prep_work", [P, COLS])
        ends = sb("prep_ends", [P, 4])
        wide = sb("prep_wide", [P, P])
        ps = ctx.enter_context(nc.psum_tensor("prep_ps", [P, 512], FP32))
        loaded, built, turned, mapped = sem("p_loaded"), sem("p_built"), sem("p_turned"), sem("p_mapped")
        plain = [("ident", A["eye"][:, :]), ("W1", A["L0_gnn_W1"][:, :]), ("W2", A["L0_gnn_W2"][:, :]),
                 ("U1a", A["L1_gnn_U1"][0:P, :]), ("U1b", A["L1_gnn_U1"][P:2 * P, :]),
                 ("U2", A["L1_gnn_U2"][:, :]), ("M1a", A["L1_gnn_W1"][0:P, :]),
                 ("M1b", A["L1_gnn_W1"][P:2 * P, :]), ("w1c", A["L1_gnn_W1"][2 * P:2 * P + 1, :]),
                 ("M2", A["L1_gnn_W2"][:, :]), ("src_i", A["src"][:, :]), ("dst_i", A["dst"][:, :]),
                 ("slot_i", A["slot_ids"][:, :])]
        spread = [("b2r", "L0_gnn_b2"), ("b3r", "L0_gnn_b3"), ("c2r", "L1_gnn_c2")]
        rows = ("L0_gnn_b1", "L0_gnn_b2", "L0_gnn_b3", "L1_gnn_b2", "L1_gnn_c2")
        cols = [("b1", "L0_gnn_b1"), ("b2", "L0_gnn_b2"), ("mb1", "L1_gnn_b1"), ("c1", "L1_gnn_c1")]
        loads = len(plain) + len(spread) + len(cols) + len(rows) + 3 + 6
        nb = len(BIASES) * P
        brow = sb("prep_brow", [1, nb])
        left = sb("prep_left", [1, nb])
        part = sb("prep_part", [1, 3, nb], BF16)
        split, spread_out = sem("p_split"), sem("p_spread_out")

        with nc.Block() as block:
            @block.sync
            def _(sp):
                for name, src in plain:
                    sp.dma_start(K[name][:, :], src).then_inc(loaded, 16)
                sp.dma_start(w3raw[:, :], A["L0_gnn_W3"][:, :]).then_inc(loaded, 16)
                sp.dma_start(prev_i[:, :], A["dst_before"][:, :]).then_inc(loaded, 16)
                sp.dma_start(next_i[:, :], A["dst_after"][:, :]).then_inc(loaded, 16)
                for name, src in spread:
                    sp.dma_start(K[name][:, :], A[src].partition_broadcast(P)).then_inc(loaded, 16)
                for i, src in enumerate(rows):
                    sp.dma_start(brow[:, i * P:(i + 1) * P], A[src].rearrange("(a n) -> a n", a=1)).then_inc(loaded, 16)
                for name, src in cols:
                    sp.dma_start(K[name][:, :], A[src].rearrange("(p a) -> p a", a=1)).then_inc(loaded, 16)
                for l in LAYERS:
                    for k in "sd":
                        sp.dma_start(att[k, l][:, :], A[f"L0_gnn_a{k}{l}"].rearrange("h c -> (h c)")
                                     .partition_broadcast(P)).then_inc(loaded, 16)
                sp.dma_start(T["map"].rearrange("(p n) a -> p (n a)", p=P),
                             A["node_ids"].rearrange("(p n) a -> p (n a)", p=P)).then_inc(mapped, 16)
                sp.wait_ge(mapped, 16)
                sp.wait_ge(split, 1)
                for k in range(3):
                    for t in range(G):
                        sp.dma_start(K["parts"][k:k + 1, :, t, :], part[:, k, :].rearrange("a (b n) -> a b n", n=P)).then_inc(spread_out, 16)
                sp.wait_ge(spread_out, 16 * 3 * G)

            @block.vector
            def _(v):
                nc.vector.memset(K["eps"][:, :], EPS)
                nc.vector.memset(K["ones"][:, :], 1.0)
                nc.vector.memset(K["parts"][:, :, :, :], 0.0)
                v.wait_ge(loaded, 16 * loads)
                nc.vector.tensor_copy(left[:, :], brow[:, :])
                for k in range(3):
                    v.drain()
                    nc.vector.tensor_copy(part[:, k, :], left[:, :])
                    v.drain()
                    nc.vector.tensor_tensor(left[:, :], left[:, :], part[:, k, :], ALU.subtract)
                v.drain().then_inc(split, 1)
                nc.vector.tensor_scalar(K["W3"][:, :], w3raw[:, :], 1.0 / H, None, ALU.mult)
                for src, dst in ((K["dst_i"], dstf), (prev_i, prevf), (next_i, nextf), (K["slot_i"], slotf)):
                    nc.vector.tensor_copy(dst[:, :], src[:, :])
                v.drain()
                nc.vector.tensor_reduce(K["W3m"][:, :], K["W3"][:, :].rearrange("p (h c) -> p c h", h=H), AX.X, ALU.add)
                for l in LAYERS:
                    w = {1: K["W1"], 2: K["W2"], 3: w3raw}[l]
                    n = P if l < 3 else H * P
                    for i, k in enumerate("sd"):
                        nc.vector.tensor_tensor(prod[:, 0:n], w[:, :], att[k, l][:, :], ALU.mult)
                        v.drain()
                        nc.vector.tensor_reduce(K[f"A{l}"][:, i * H:i * H + H],
                                                prod[:, 0:n].rearrange("p (h c) -> p h c", h=H), AX.X, ALU.add)
                        v.drain()
                first = dstf[:, 0:1]
                nc.vector.tensor_tensor(work[:, :], dstf[:, :], prevf[:, :], ALU.is_equal)
                nc.vector.tensor_tensor(K["goes_on"][:, :], dstf[:, :], nextf[:, :], ALU.is_equal)
                nc.vector.tensor_scalar(inhead[:, :], dstf[:, :], first, None, ALU.is_equal)
                v.drain()
                nc.vector.tensor_scalar(K["fresh"][:, :], work[:, :], -1.0, BIG, ALU.add, ALU.mult)
                nc.vector.tensor_scalar(K["joins"][:, :], work[:, 0:1], -1.0, BIG, ALU.add, ALU.mult)
                nc.vector.tensor_scalar(K["last"][:, :], K["goes_on"][:, :], -1.0, 1.0, ALU.mult, ALU.add)
                nc.vector.tensor_tensor(ends[:, 0:1], work[:, 0:1], inhead[:, COLS - 1:COLS], ALU.mult)
                nc.vector.tensor_tensor(ends[:, 1:2], K["goes_on"][:, COLS - 1:COLS],
                                        inhead[:, COLS - 1:COLS], ALU.mult)
                v.drain()
                nc.vector.memset(K["fresh"][:, 0:1], -BIG)
                nc.vector.tensor_tensor(K["headend"][:, :], K["last"][:, :], inhead[:, :], ALU.mult)
                nc.vector.tensor_scalar(ends[:, 2:3], ends[:, 0:1], -1.0, BIG, ALU.add, ALU.mult)
                nc.vector.tensor_scalar(ends[:, 3:4], ends[:, 1:2], FAR, None, ALU.mult)
                nc.vector.scalar_tensor_tensor(work[:, :], K["goes_on"][:, :], FAR, dstf[:, :], ALU.mult, ALU.add)
                v.drain()
                nc.vector.tensor_copy(K["scat_i"][:, :], work[:, :])
                nc.vector.tensor_copy(wide[:, :], ends[:, 2:3].to_broadcast([P, P]))
                nc.vector.tensor_tensor(prevf[:, :], K["headend"][:, :], slotf[:, :], ALU.mult)
                nc.vector.tensor_tensor(nextf[:, 0:1], dstf[:, 0:1], ends[:, 3:4], ALU.add)
                v.drain()
                nc.vector.tensor_reduce(work[:, 0:1], prevf[:, :], AX.X, ALU.add)
                nc.vector.tensor_copy(K["head_out_i"][:, :], nextf[:, 0:1])
                v.drain().then_inc(built, 1)
                nc.vector.tensor_scalar(work[:, 1:2], work[:, 0:1], float(NP), float(NP), ALU.max, ALU.subtract)
                nc.vector.tensor_scalar(work[:, 3:4], work[:, 0:1], float(NP), None, ALU.max)
                nc.vector.tensor_scalar(K["not_headend"][:, :], K["headend"][:, :], -1.0, 1.0, ALU.mult, ALU.add)
                nc.vector.tensor_tensor(work[:, 2:3], work[:, 0:1], ends[:, 3:4], ALU.add)
                v.drain()
                nc.vector.tensor_copy(K["head_slot_i"][:, :], work[:, 1:2])
                nc.vector.tensor_copy(K["head_row_i"][:, :], work[:, 2:3])
                nc.vector.tensor_copy(K["head_read_i"][:, :], work[:, 3:4])
                v.wait_ge(turned, 1)
                nc.vector.tensor_copy(K["chain"][:, :], ps[:, 0:P])

            @block.tensor
            def _(pe):
                pe.wait_ge(built, 1)
                nc.tensor.transpose(ps[:, 0:P], wide[:, :], K["ident"][:, :]).then_inc(turned, 1)

        clear_semaphores(nc, used)


def look_up_dst(nc, K, T):
    with ExitStack() as ctx:
        work = ctx.enter_context(nc.sbuf_tensor("l_work", [P, COLS], FP32))
        slotf = ctx.enter_context(nc.sbuf_tensor("l_slot", [P, COLS], FP32))
        with nc.Block() as block:
            @block.vector
            def _(v):
                nc.vector.tensor_copy(K["tail"][:, :], K["tail_row_i"][:, :])
                nc.vector.tensor_copy(slotf[:, :], K["slot_i"][:, :])
                v.drain()
                nc.vector.tensor_tensor(work[:, :], slotf[:, :], K["last"][:, :], ALU.mult)
                v.drain()
                nc.vector.tensor_tensor_scan(slotf[:, ::-1], K["goes_on"][:, ::-1], work[:, ::-1],
                                             K["tail"][:, :], ALU.mult, ALU.add)
                v.drain()
                nc.vector.tensor_copy(K["gdst_i"][:, :], slotf[:, :])


def add_bias(nc, K, bank, name):
    nc.tensor.matmul(bank[:, :], K["ones"][:, :], K["parts"][:, BIASES.index(name), :, :].rearrange("p t c -> p (t c)"),
                     start=True, stop=False)


def layer_norm_dve(nc, v, y, y_out, stats, aggr, rstd_in, n):
    for t in range(n):
        nc.vector.bn_stats(stats[:, t, :], y[:, t, :])
    v.drain()
    for t in range(n):
        nc.vector.bn_aggr(aggr[:, t, :], stats[:, t, :])
    v.drain()


def layer_norm_apply(nc, v, y, y_out, aggr, rstd, n):
    nc.vector.reciprocal(rstd[:, 1, 0:n], rstd[:, 0, 0:n])
    v.drain()
    for t in range(n):
        ins = nc.vector.tensor_scalar(y_out[:, t, :], y[:, t, :], aggr[:, t, 0:1], rstd[:, 1, t:t + 1],
                                      ALU.subtract, ALU.mult)
    return ins


def over_tiles(ap, n=G):
    return ap.unsqueeze(1).to_broadcast([P, n, ap.shape[-1]])


def dense(nc, A, K, T, out):
    with ExitStack() as ctx:
        def sb(name, shape, dt=FP32):
            return ctx.enter_context(nc.sbuf_tensor(name, shape, dt))

        used = []

        def sem(name):
            used.append(ctx.enter_context(nc.semaphore(name)))
            return used[-1]

        L = range(DLANES)
        x = [sb(f"d_x{i}", [P, G, P]) for i in L]
        fa = [sb(f"d_fa{i}", [P, G * P]) for i in L]
        fb = [sb(f"d_fb{i}", [P, G * P]) for i in L]
        r2 = [sb(f"d_r2{i}", [P, G, ROW]) for i in L]
        r3 = [sb(f"d_r3{i}", [P, G, ROW]) for i in L]
        y = [sb(f"d_y{i}", [P, G, P]) for i in L]
        x1 = [sb(f"d_x1{i}", [P, G, P]) for i in L]
        fin = [sb(f"d_fin{i}", [P, G, P]) for i in L]
        stats = [sb(f"d_stats{i}", [P, G, 6]) for i in L]
        aggr = [sb(f"d_aggr{i}", [P, G, 2]) for i in L]
        rstd = [sb(f"d_rstd{i}", [P, 2, G]) for i in L]
        pa = [ctx.enter_context(nc.psum_tensor(f"d_pa{i}", [P, G * P], FP32)) for i in L]
        pb = [ctx.enter_context(nc.psum_tensor(f"d_pb{i}", [P, G * P], FP32)) for i in L]
        x_in = [sem(f"d_x_in{i}") for i in L]
        r2_done = sem("d_r2_done")
        stored = [sem(f"d_stored{i}") for i in L]
        rows_free = sem("d_rows_free")
        tick, sp_tick = sem("d_tick"), sem("d_sp_tick")
        pe_s = [sem(f"d_pe{k}") for k in range(8)]
        ev = [sem(f"d_ev{k}") for k in range(8)]
        h2_done, var1, root1, x1_done, var2, root2, fin_done = (
            sem("d_" + s) for s in ("h2_done", "var1", "root1", "x1_done", "var2", "root2", "fin_done"))
        rounds = NG // DLANES
        to = [sb(f"map_to{b}", [P, MG], I32) for b in range(2)]
        val = [sb(f"map_val{b}", [P, MG], I32) for b in range(2)]
        tail_to = sb("map_tail_to", [P, 1], I32)
        staged, kept = sem("m_staged"), sem("m_kept")
        sent, fetched = ([K["dma_sem"](f"m_{s}{b}") for b in range(2)] for s in ("sent", "fetched"))
        tailed = K["dma_sem"]("m_tailed")
        groups = COLS // MG
        assert groups % 2 == 1

        def scatter(g, b, col, stage_no, turn):
            nc.gpsimd.tensor_copy(to[b][:, :], K["scat_i"][:, col]).then_inc(staged, 1)
            nc.gpsimd.tensor_copy(val[b][:, :], K["slot_i"][:, col]).then_inc(staged, 1)
            g.wait_ge(staged, stage_no)
            g.sem_inc(tick, 1)
            for t in range(MG):
                g.indirect_dma_start(T["map"][:, :], bass.IndirectOffsetOnAxis(ap=to[b][:, t:t + 1], axis=0),
                                     val[b][:, t:t + 1], None, bounds_check=NP - 1,
                                     oob_is_err=False).then_inc(sent[b], 16)

        def gather(g, b, col, stage_no):
            nc.gpsimd.tensor_copy(to[b][:, :], K["src_i"][:, col]).then_inc(staged, 1)
            g.wait_ge(staged, stage_no)
            g.sem_inc(tick, 1)
            for t in range(MG):
                g.indirect_dma_start(val[b][:, t:t + 1], None, T["map"][:, :],
                                     bass.IndirectOffsetOnAxis(ap=to[b][:, t:t + 1], axis=0)).then_inc(fetched[b], 16)

        rows = [t.rearrange("(g p t) c -> g p (t c)", p=P, t=G)
                for t in (A["x"], T[2][0:NP, :], T[3][0:NP, :], T[4][0:NP, :], out)]
        flat = lambda ap: ap.rearrange("p t c -> p (t c)")
        stores = 4

        with nc.Block() as block:
            @block.gpsimd
            def _(g):
                with g.Fori(0, groups // 2) as it:
                    for b in range(2):
                        scatter(g, b, bass.ds((it * 2 + b) * MG, MG), it * 4 + 2 * b + 2, it)
                    for b in range(2):
                        g.wait_ge(sent[b], (it + 1) * (16 * MG))
                        g.sem_inc(tick, 1)
                half = groups // 2
                scatter(g, 0, slice(COLS - MG, COLS), half * 4 + 2, half)
                g.wait_ge(sent[0], (half + 1) * 16 * MG)
                n0 = half * 4 + 2
                with g.Fori(0, half) as it:
                    for b in range(2):
                        gather(g, b, bass.ds((it * 2 + b) * MG, MG), it * 4 + 2 * b + (n0 + 1))
                        g.wait_ge(fetched[b], (it + 1) * (16 * MG))
                        g.sem_inc(tick, 1)
                        nc.gpsimd.tensor_copy(K["gsrc_i"][:, bass.ds((it * 2 + b) * MG, MG)], val[b][:, :]).then_inc(staged, 1)
                        g.wait_ge(staged, it * 4 + 2 * b + (n0 + 2))
                        g.sem_inc(tick, 1)
                gather(g, 0, slice(COLS - MG, COLS), n0 + 4 * half + 1)
                g.wait_ge(fetched[0], (half + 1) * 16 * MG)
                nc.gpsimd.tensor_copy(K["gsrc_i"][:, COLS - MG:COLS], val[0][:, :]).then_inc(staged, 1)
                nc.gpsimd.tensor_copy(tail_to[:, :], K["dst_i"][:, COLS - 1:COLS]).then_inc(kept, 1)
                g.wait_ge(kept, 1)
                g.indirect_dma_start(K["tail_row_i"][:, :], None, T["map"][:, :],
                                     bass.IndirectOffsetOnAxis(ap=tail_to[:, :], axis=0)).then_inc(tailed, 16)
                g.wait_ge(tailed, 16)

            @block.sync
            def _(sp):
                def load(i, group):
                    sp.dma_start(flat(x[i][:, :, :]), rows[0][bass.ds(group, 1), :, :].rearrange("a p c -> (a p) c")).then_inc(x_in[i], 16)

                sp.sem_inc(rows_free, DLANES)
                for i in L:
                    load(i, i)
                with sp.Fori(0, rounds) as it:
                    def put(k, tile, i):
                        sp.dma_start(rows[k][bass.ds(it * DLANES + i, 1), :, :].rearrange("a p c -> (a p) c"),
                                     flat(tile[i][:, :, :])).then_inc(stored[i], 16)
                    for i in L:
                        sp.wait_ge(r2_done, it * DLANES + i + 1)
                        sp.sem_inc(sp_tick, 1)
                        sp.wait_ge(ev[2], it * DLANES + i + 1)
                        sp.sem_inc(sp_tick, 1)
                        put(1, r2, i)
                    for i in L:
                        sp.wait_ge(ev[4], it * DLANES + i + 1)
                        sp.sem_inc(sp_tick, 1)
                        put(2, r3, i)
                        load(i, (it + 1) * DLANES + i)
                    for i in L:
                        sp.wait_ge(x1_done, it * DLANES + i + 1)
                        sp.sem_inc(sp_tick, 1)
                        put(3, x1, i)
                    for i in L:
                        sp.wait_ge(fin_done, it * DLANES + i + 1)
                        sp.sem_inc(sp_tick, 1)
                        put(4, fin, i)
                    for i in L:
                        sp.wait_ge(stored[i], (it + 1) * (16 * stores))
                        sp.sem_inc(rows_free, 1)
                for i in L:
                    sp.wait_ge(x_in[i], (rounds + 1) * 16)

            @block.tensor
            def _(pe):
                with pe.Fori(0, rounds) as it:
                    def each(stage):
                        for i in L:
                            stage(i, it * DLANES + i + 1)

                    def turn_x(i, n):
                        pe.wait_ge(x_in[i], (it + 1) * 16)
                        pe.wait_ge(ev[7], n)
                        for t in range(G):
                            ins = nc.tensor.transpose(pa[i][:, t * P:(t + 1) * P], x[i][:, t, :], K["ident"][:, :])
                        ins.then_inc(pe_s[0], 1)

                    def times_w1(i, n):
                        pe.wait_ge(ev[0], n)
                        nc.tensor.matmul(pb[i][:, :], K["W1"][:, :], fa[i][:, :], start=True, stop=True).then_inc(pe_s[1], 1)

                    def times_w2(i, n):
                        pe.wait_ge(ev[1], n)
                        add_bias(nc, K, pa[i], "b2")
                        for t in range(G):
                            h = fb[i][:, t * P:(t + 1) * P]
                            nc.tensor.matmul(pa[i][:, t * P:(t + 1) * P], h, K["W2"][:, :], start=False, stop=(t == G - 1))
                            ins = nc.tensor.matmul(pb[i][:, t * 2 * H:(t + 1) * 2 * H], h, K["A2"][:, :], start=True, stop=True)
                        ins.then_inc(pe_s[2], 1)

                    def turn_h2(i, n):
                        pe.wait_ge(h2_done, n)
                        pe.wait_ge(ev[2], n)
                        for t in range(G):
                            ins = nc.tensor.transpose(pb[i][:, t * P:(t + 1) * P], r3[i][:, t, 0:P], K["ident"][:, :])
                        ins.then_inc(pe_s[3], 1)

                    def times_w3(i, n):
                        pe.wait_ge(ev[3], n)
                        pe.wait_ge(r2_done, n)
                        add_bias(nc, K, pa[i], "b3")
                        for t in range(G):
                            h = fa[i][:, t * P:(t + 1) * P]
                            nc.tensor.matmul(pa[i][:, t * P:(t + 1) * P], h, K["W3m"][:, :], start=False, stop=(t == G - 1))
                            ins = nc.tensor.matmul(pb[i][:, t * 2 * H:(t + 1) * 2 * H], h, K["A3"][:, :], start=True, stop=True)
                        ins.then_inc(pe_s[4], 1)

                    def turn_x1(i, n):
                        pe.wait_ge(x1_done, n)
                        for t in range(G):
                            ins = nc.tensor.transpose(pa[i][:, t * P:(t + 1) * P], x1[i][:, t, :], K["ident"][:, :])
                        ins.then_inc(pe_s[5], 1)

                    def times_u1(i, n):
                        pe.wait_ge(ev[5], n)
                        nc.tensor.matmul(pb[i][:, :], K["U1a"][:, :], fb[i][:, :], start=True, stop=True).then_inc(pe_s[6], 1)

                    def times_u2(i, n):
                        pe.wait_ge(ev[6], n)
                        add_bias(nc, K, pa[i], "c2")
                        for t in range(G):
                            ins = nc.tensor.matmul(pa[i][:, t * P:(t + 1) * P], fa[i][:, t * P:(t + 1) * P], K["U2"][:, :],
                                                   start=False, stop=(t == G - 1))
                        ins.then_inc(pe_s[7], 1)

                    for stage in (turn_x, times_w1, times_w2, turn_h2, times_w3, turn_x1, times_u1, times_u2):
                        each(stage)

            @block.scalar
            def _(act):
                with act.Fori(0, rounds) as it:
                    def each(stage):
                        for i in L:
                            stage(i, it * DLANES + i + 1)

                    def take_x(i, n):
                        act.wait_ge(pe_s[0], n)
                        nc.scalar.activation(fa[i][:, :], pa[i][:, :], ACT.Copy).then_inc(ev[0], 1)

                    def take_h1(i, n):
                        act.wait_ge(pe_s[1], n)
                        nc.scalar.activation(fb[i][:, :], pb[i][:, :], ACT.Relu, bias=K["b1"][:, :]).then_inc(ev[1], 1)

                    def relu_h2(i, n):
                        act.wait_ge(rows_free, n)
                        act.wait_ge(pe_s[2], n)
                        psum = pa[i][:, :].rearrange("p (t c) -> p t c", t=G)
                        nc.scalar.activation(r3[i][:, :, 0:P], psum, ACT.Relu).then_inc(h2_done, 1)
                        nc.scalar.activation(r2[i][:, :, 0:P], psum, ACT.Copy).then_inc(r2_done, 1)

                    def take_h2(i, n):
                        act.wait_ge(pe_s[3], n)
                        nc.scalar.activation(fa[i][:, :], pb[i][:, :], ACT.Copy).then_inc(ev[3], 1)

                    def root(i, n, ready, done):
                        act.wait_ge(ready, n)
                        nc.scalar.activation(rstd[i][:, 0, :], aggr[i][:, :, 1], ACT.Sqrt, bias=K["eps"][:, :]).then_inc(done, 1)

                    def take_x1(i, n):
                        act.wait_ge(pe_s[5], n)
                        nc.scalar.activation(fb[i][:, :], pa[i][:, :], ACT.Copy).then_inc(ev[5], 1)

                    def take_u(i, n):
                        act.wait_ge(pe_s[6], n)
                        nc.scalar.activation(fa[i][:, :], pb[i][:, :], ACT.Relu, bias=K["c1"][:, :]).then_inc(ev[6], 1)

                    each(take_x)
                    each(take_h1)
                    each(relu_h2)
                    each(take_h2)
                    each(lambda i, n: root(i, n, var1, root1))
                    each(take_x1)
                    each(take_u)
                    each(lambda i, n: root(i, n, var2, root2))

            @block.vector
            def _(v):
                v.sem_inc(ev[7], DLANES)
                with v.Fori(0, rounds) as it:
                    def each(stage):
                        for i in L:
                            stage(i, it * DLANES + i + 1)

                    def take_xp2(i, n):
                        v.wait_ge(rows_free, n)
                        v.wait_ge(pe_s[2], n)
                        nc.vector.tensor_copy(r2[i][:, :, P:ROW], pb[i][:, 0:G * 2 * H].rearrange("p (t c) -> p t c", t=G)).then_inc(ev[2], 1)

                    def residual(i, n):
                        v.wait_ge(pe_s[4], n)
                        nc.vector.tensor_copy(r3[i][:, :, P:ROW], pb[i][:, 0:G * 2 * H].rearrange("p (t c) -> p t c", t=G))
                        nc.vector.tensor_tensor(y[i][:, :, :], pa[i][:, :].rearrange("p (t c) -> p t c", t=G), x[i][:, :, :], ALU.add)
                        v.drain().then_inc(ev[4], 1)
                        layer_norm_dve(nc, v, y[i], None, stats[i], aggr[i], None, G)
                        v.sem_inc(var1, 1)

                    def norm1(i, n):
                        v.wait_ge(root1, n)
                        layer_norm_apply(nc, v, y[i], x1[i], aggr[i], rstd[i], G)
                        v.drain().then_inc(x1_done, 1)

                    def residual2(i, n):
                        v.wait_ge(pe_s[7], n)
                        nc.vector.tensor_tensor(y[i][:, :, :], pa[i][:, :].rearrange("p (t c) -> p t c", t=G), x1[i][:, :, :], ALU.add)
                        v.drain().then_inc(ev[7], 1)
                        layer_norm_dve(nc, v, y[i], None, stats[i], aggr[i], None, G)
                        v.sem_inc(var2, 1)

                    def norm2(i, n):
                        v.wait_ge(root2, n)
                        layer_norm_apply(nc, v, y[i], fin[i], aggr[i], rstd[i], G)
                        v.drain().then_inc(fin_done, 1)

                    for stage in (take_xp2, residual, norm1, residual2, norm2):
                        each(stage)

        clear_semaphores(nc, used)


def attend(nc, A, K, T, layer):
    wd, nacc = WIDE[layer], ACC[layer]
    sw = STATE[layer]
    lanes = range(2)
    with ExitStack() as ctx:
        def name_of(name):
            return f"a{layer}_{name}"

        def sb(name, shape, dt=FP32):
            return ctx.enter_context(nc.sbuf_tensor(name_of(name), shape, dt))

        used = []

        def sem(name):
            used.append(ctx.enter_context(nc.semaphore(name_of(name))))
            return used[-1]

        def bank(name):
            return ctx.enter_context(nc.psum_tensor(name_of(name), [P, G * P], FP32))

        in_w = P if layer == 1 else ROW
        out_w = P if layer == 3 else ROW
        S = [sb(f"src{b}", [P, G, in_w]) for b in lanes]
        D = [sb(f"dst{b}", [P, G, in_w]) for b in lanes]
        idx = [sb(f"idx{b}", [P, G], I32) for b in lanes]
        idd = [sb(f"idd{b}", [P, G], I32) for b in lanes]
        fresh = [sb(f"fresh{b}", [P, G]) for b in lanes]
        st = [sb(f"st{b}", [P, G, sw]) for b in lanes]
        m = [sb(f"m{b}", [P, G + 1, H]) for b in lanes]
        lg = [sb(f"lg{b}", [P, 2, G, H]) for b in lanes]
        lr = [sb(f"lr{b}", [P, 2, G, H]) for b in lanes]
        q = [sb(f"q{b}", [P, G, H]) for b in lanes]
        dd = [sb(f"dd{b}", [P, 3, G, H]) for b in lanes]
        wt = [sb(f"wt{b}", [P, 3, G, H]) for b in lanes]
        msg = [sb(f"msg{b}", [P, G, H, wd + 1]) for b in lanes]
        den = [sb(f"den{b}", [P, 2, G, H]) for b in lanes]
        o = [sb(f"o{b}", [P, G, H, wd]) for b in lanes]
        if layer == 1:
            hf = [sb(f"hf{b}", [P, G, P]) for b in lanes]
        r = [sb(f"r{b}", [P, G, out_w]) for b in lanes]
        pm = [[bank(f"p{b}{k}") for k in range(4)] for b in lanes]
        arrived = [K["dma_sem"](name_of(f"arrived{b}")) for b in lanes]
        d_in = [sem(f"d_in{b}") for b in lanes]
        in_free, tick, sp_tick, staged = sem("in_free"), sem("tick"), sem("sp_tick"), sem("staged")
        f1, expd, f2, o_done, h_done = (sem(s) for s in ("f1", "expd", "f2", "o_done", "h_done"))
        turned_h, took_h, times, rows_done = (sem(s) for s in ("turned_h", "took_h", "times", "rows_done"))
        st_stored, r_stored = ([sem(f"{s}{b}") for b in lanes] for s in ("st_stored", "r_stored"))
        st_free, r_free = sem("st_free"), sem("r_free")
        if layer == 1:
            fT = [sb(f"fT{b}", [P, 2, G * P]) for b in lanes]
            al = [sb(f"al{b}", [P, 2, G, 2 * H]) for b in lanes]
            xd_stored = [sem(f"xd_stored{b}") for b in lanes]
            turned, took, proj, took_al, took_r = (sem(s) for s in ("turned", "took", "proj", "took_al", "took_r"))
        if layer < 3:
            hT = [sb(f"hT{b}", [P, G * P]) for b in lanes]
        else:
            zT = [sb(f"zT{b}", [P, H, G * P]) for b in lanes]
            xr = [sb(f"xr{b}", [P, G, P]) for b in lanes]
            xr_in = [sem(f"xr_in{b}") for b in lanes]
            stats = [sb(f"stats{b}", [P, G, 6]) for b in lanes]
            aggr = [sb(f"aggr{b}", [P, G, 2]) for b in lanes]
            rstd = [sb(f"rstd{b}", [P, 2, G]) for b in lanes]
            y = [sb(f"y{b}", [P, G, P]) for b in lanes]
            var, root, weighted, summed = sem("var"), sem("root"), sem("weighted"), sem("summed")

        iters = EG // 2
        flat = lambda ap: ap.rearrange("p t c -> p (t c)")
        slots = lambda ap: ap.rearrange("(p j) c -> p j c", p=P)
        st_rows = slots(T["st", layer])
        next_rows = slots(T[layer + 1][NP:NP + EP, :])
        xd_rows = slots(T["xd"])

        def cols(it, b):
            return bass.ds((it * 2 + b) * G, G)

        per_group = 2 * G if layer == 1 else G
        logit_at = 256
        tT = [pm[b][3] if layer == 1 else pm[b][2] for b in lanes]

        with nc.Block() as block:
            @block.gpsimd
            def _(g):
                def gather(it, b):
                    n = it * 2 + b + 1
                    if layer < 3:
                        g.wait_ge(in_free, n)
                        g.sem_inc(tick, 1)
                    if layer == 1:
                        nc.gpsimd.tensor_copy(idx[b][:, :], K["src_i"][:, cols(it, b)]).then_inc(staged, 1)
                        nc.gpsimd.tensor_copy(idd[b][:, :], K["dst_i"][:, cols(it, b)]).then_inc(staged, 1)
                        g.wait_ge(staged, it * 4 + 2 * b + 2)
                        g.sem_inc(tick, 1)
                        for t in range(G):
                            for rows, at in ((S, idx), (D, idd)):
                                g.indirect_dma_start(rows[b][:, t, :], None, A["x"][:, :],
                                                     bass.IndirectOffsetOnAxis(ap=at[b][:, t:t + 1], axis=0)).then_inc(arrived[b], 16)
                    else:
                        nc.gpsimd.tensor_copy(idx[b][:, :], K["gsrc_i"][:, cols(it, b)]).then_inc(staged, 1)
                        g.wait_ge(staged, it * 2 + b + 1)
                        g.sem_inc(tick, 1)
                        for t in range(G):
                            g.indirect_dma_start(S[b][:, t, :], None, T[layer][:, :],
                                                 bass.IndirectOffsetOnAxis(ap=idx[b][:, t:t + 1], axis=0)).then_inc(arrived[b], 16)

                def weigh(it, b):
                    n = it * 2 + b + 1
                    g.wait_ge(expd, n)
                    g.sem_inc(tick, 1)
                    for t in range(G):
                        ins = nc.gpsimd.tensor_tensor(msg[b][:, t, :, 0:P], S[b][:, t, 0:P].unsqueeze(1).to_broadcast([P, H, P]),
                                                      wt[b][:, 1, t, :].unsqueeze(2).to_broadcast([P, H, P]), ALU.mult)
                    ins.then_inc(weighted, 1)

                with g.Fori(0, iters) as it:
                    for b in lanes:
                        gather(it, b)
                    if layer == 3:
                        for b in lanes:
                            weigh(it, b)

            @block.sync
            def _(sp):
                def inputs(it):
                    for b in lanes:
                        n = it * 2 + b + 1
                        if layer == 1:
                            sp.wait_ge(arrived[b], (it + 1) * (16 * per_group))
                            sp.sem_inc(sp_tick, 1)
                            sp.dma_start(xd_rows[:, cols(it, b), :], D[b][:, :, :]).then_inc(xd_stored[b], 16)
                        else:
                            sp.wait_ge(in_free, n)
                            sp.sem_inc(sp_tick, 1)
                            sp.dma_start(D[b][:, :, :], slots(T[layer][NP:NP + EP, :])[:, cols(it, b), :]).then_inc(d_in[b], 16)
                    if layer == 1:
                        for b in lanes:
                            sp.wait_ge(xd_stored[b], (it + 1) * 16)
                            sp.sem_inc(sp_tick, 1)
                            sp.wait_ge(took, it * 2 + b + 1)
                            sp.sem_inc(in_free, 1)

                def residual_rows(it):
                    for b in lanes:
                        sp.dma_start(xr[b][:, :, :], xd_rows[:, cols(it, b), :]).then_inc(xr_in[b], 16)

                def store_rows(it):
                    for b in lanes:
                        n = it * 2 + b + 1
                        sp.wait_ge(rows_done, n)
                        sp.sem_inc(sp_tick, 1)
                        if layer == 1:
                            sp.wait_ge(took_r, n)
                            sp.sem_inc(sp_tick, 1)
                        sp.dma_start(next_rows[:, cols(it, b), :], r[b][:, :, :]).then_inc(r_stored[b], 16)

                def store_states(it):
                    for b in lanes:
                        sp.wait_ge(f2, it * 2 + b + 1)
                        sp.sem_inc(sp_tick, 1)
                        sp.dma_start(st_rows[:, cols(it, b), :], st[b][:, :, :]).then_inc(st_stored[b], 16)

                def free_rows(it):
                    for b in lanes:
                        sp.wait_ge(r_stored[b], (it + 1) * 16)
                        sp.sem_inc(r_free, 1)

                def free_states(it):
                    for b in lanes:
                        sp.wait_ge(st_stored[b], (it + 1) * 16)
                        sp.sem_inc(st_free, 1)

                sp.sem_inc(st_free, 2)
                sp.sem_inc(r_free, 2)
                if layer == 1:
                    sp.sem_inc(in_free, 2)
                inputs(0)
                if layer == 3:
                    residual_rows(0)
                store_states(0)
                free_states(0)
                with sp.Fori(1, iters) as it:
                    inputs(it)
                    if layer < 3:
                        store_rows(it - 1)
                        store_states(it)
                        free_rows(it - 1)
                    else:
                        store_states(it)
                        store_rows(it - 1)
                        residual_rows(it)
                        free_rows(it - 1)
                    free_states(it)
                store_rows(iters - 1)
                free_rows(iters - 1)

            @block.tensor
            def _(pe):
                def turn_in(it, b):
                    pe.wait_ge(arrived[b], (it + 1) * (16 * per_group))
                    if not (isinstance(it, int) and it == 0):
                        pe.wait_ge(f2, it * 2 + b - 1)
                    for k, rows in enumerate((S, D)):
                        for t in range(G):
                            ins = nc.tensor.transpose(pm[b][k][:, t * P:(t + 1) * P], rows[b][:, t, :], K["ident"][:, :])
                    ins.then_inc(turned, 1)

                def project(it, b):
                    pe.wait_ge(took, it * 2 + b + 1)
                    for k in range(2):
                        add_bias(nc, K, pm[b][k], "b1")
                        for t in range(G):
                            f = fT[b][:, k, t * P:(t + 1) * P]
                            nc.tensor.matmul(pm[b][k][:, t * P:(t + 1) * P], f, K["W1"][:, :], start=False, stop=(t == G - 1))
                            at = (k * G + t) * 2 * H
                            ins = nc.tensor.matmul(pm[b][2][:, at:at + 2 * H], f, K["A1"][:, :], start=True, stop=True)
                    ins.then_inc(proj, 1)

                def turn_out(it, b):
                    n = it * 2 + b + 1
                    if layer < 3:
                        pe.wait_ge(h_done, n)
                        for t in range(G):
                            h = hf[b][:, t, :] if layer == 1 else r[b][:, t, 0:P]
                            ins = nc.tensor.transpose(tT[b][:, t * P:(t + 1) * P], h, K["ident"][:, :])
                    else:
                        pe.wait_ge(o_done, n)
                        for h in range(H):
                            for t in range(G):
                                ins = nc.tensor.transpose(pm[b][h][:, t * P:(t + 1) * P], o[b][:, t, h, :], K["ident"][:, :])
                    ins.then_inc(turned_h, 1)

                def multiply(it, b):
                    n = it * 2 + b + 1
                    pe.wait_ge(took_h, n)
                    if layer == 3:
                        add_bias(nc, K, pm[b][0], "b3")
                        for t in range(G):
                            for h in range(H):
                                ins = nc.tensor.matmul(pm[b][0][:, t * P:(t + 1) * P], zT[b][:, h, t * P:(t + 1) * P],
                                                       K["W3"][:, h * P:(h + 1) * P], start=False,
                                                       stop=(t == G - 1 and h == H - 1))
                    else:
                        if layer == 1:
                            add_bias(nc, K, tT[b], "b2")
                        for t in range(G):
                            h = hT[b][:, t * P:(t + 1) * P]
                            if layer == 1:
                                nc.tensor.matmul(tT[b][:, t * P:(t + 1) * P], h, K["W2"][:, :], start=False, stop=(t == G - 1))
                            at = logit_at + t * 2 * H
                            ins = nc.tensor.matmul(pm[b][2][:, at:at + 2 * H], h, K[f"A{layer + 1}"][:, :], start=True, stop=True)
                    ins.then_inc(times, 1)

                def both(stage, it):
                    for b in lanes:
                        stage(it, b)

                if layer == 1:
                    both(turn_in, 0)
                    both(project, 0)
                with pe.Fori(1, iters) as it:
                    if layer == 1:
                        both(turn_in, it)
                    both(turn_out, it - 1)
                    if layer == 1:
                        both(project, it)
                        pe.wait_ge(took_al, it * 2 + 2)
                    both(multiply, it - 1)
                both(turn_out, iters - 1)
                both(multiply, iters - 1)

            @block.scalar
            def _(act):
                def take_in(it, b):
                    act.wait_ge(turned, it * 2 + b + 1)
                    for k in range(2):
                        ins = nc.scalar.activation(fT[b][:, k, :], pm[b][k][:, :], ACT.Copy)
                    ins.then_inc(took, 1)

                def take_projections(it, b):
                    n = it * 2 + b + 1
                    act.wait_ge(st_free, n)
                    act.wait_ge(proj, n)
                    nc.scalar.activation(al[b][:, :, :, :].rearrange("p k t c -> p (k t c)"), pm[b][2][:, 0:2 * G * 2 * H], ACT.Copy)
                    nc.scalar.activation(st[b][:, :, sw - P:sw], pm[b][1][:, :].rearrange("p (t c) -> p t c", t=G),
                                         ACT.Copy).then_inc(took_al, 1)

                def exponentials(it, b):
                    act.wait_ge(f1, it * 2 + b + 1)
                    nc.scalar.activation(wt[b][:, :, :, :].rearrange("p k t h -> p (k t h)"),
                                         dd[b][:, :, :, :].rearrange("p k t h -> p (k t h)"), ACT.Exp).then_inc(expd, 1)

                def finish(it, b):
                    n = it * 2 + b + 1
                    if layer == 1:
                        act.wait_ge(o_done, n)
                        nc.scalar.activation(flat(hf[b][:, :, :]), o[b][:, :, :, :].rearrange("p t h c -> p (t h c)"), ACT.Relu).then_inc(h_done, 1)
                    elif layer == 2:
                        act.wait_ge(r_free, n)
                        act.wait_ge(o_done, n)
                        nc.scalar.activation(r[b][:, :, 0:P], o[b][:, :, :, :].rearrange("p t h c -> p t (h c)"), ACT.Relu).then_inc(h_done, 1)
                    else:
                        act.wait_ge(summed, n)
                        for t in range(G):
                            for h in range(H):
                                ins = nc.scalar.activation(o[b][:, t, h, :], o[b][:, t, h, :], ACT.Copy, scale=den[b][:, 1, t, h:h + 1])
                        ins.then_inc(o_done, 1)

                def take_out(it, b):
                    act.wait_ge(turned_h, it * 2 + b + 1)
                    if layer < 3:
                        nc.scalar.activation(hT[b][:, :], tT[b][:, :], ACT.Copy).then_inc(took_h, 1)
                    else:
                        for h in range(H):
                            ins = nc.scalar.activation(zT[b][:, h, :], pm[b][h][:, :], ACT.Copy)
                        ins.then_inc(took_h, 1)

                def take_rows(it, b):
                    n = it * 2 + b + 1
                    act.wait_ge(r_free, n)
                    act.wait_ge(times, n)
                    nc.scalar.activation(r[b][:, :, 0:P], tT[b][:, :].rearrange("p (t c) -> p t c", t=G), ACT.Copy).then_inc(took_r, 1)

                def roots(it, b):
                    act.wait_ge(var, it * 2 + b + 1)
                    nc.scalar.activation(rstd[b][:, 0, :], aggr[b][:, :, 1], ACT.Sqrt, bias=K["eps"][:, :]).then_inc(root, 1)

                def both(stage, it):
                    for b in lanes:
                        stage(it, b)

                if layer == 1:
                    both(take_in, 0)
                    both(take_projections, 0)
                both(exponentials, 0)
                both(finish, 0)
                with act.Fori(1, iters) as it:
                    if layer == 1:
                        both(take_in, it)
                    both(take_out, it - 1)
                    if layer == 1:
                        both(take_projections, it)
                    both(exponentials, it)
                    if layer == 1:
                        both(take_rows, it - 1)
                    if layer == 3:
                        both(roots, it - 1)
                    both(finish, it)
                both(take_out, iters - 1)
                if layer == 1:
                    both(take_rows, iters - 1)
                if layer == 3:
                    both(roots, iters - 1)

            @block.vector
            def _(v):
                def weights(it, b):
                    n = it * 2 + b + 1
                    v.wait_ge(st_free, n)
                    nc.vector.tensor_copy(fresh[b][:, :], K["fresh"][:, cols(it, b)])
                    if layer == 1:
                        v.wait_ge(took_al, n)
                        nc.vector.tensor_tensor(lg[b][:, 0, :, :], al[b][:, 0, :, 0:H], al[b][:, 1, :, H:2 * H], ALU.add)
                        nc.vector.tensor_tensor(lg[b][:, 1, :, :], al[b][:, 1, :, 0:H], al[b][:, 1, :, H:2 * H], ALU.add)
                    else:
                        v.wait_ge(arrived[b], (it + 1) * (16 * per_group))
                        held = K["held"][:, :, cols(it, b)].rearrange("p c t -> p t c")
                        nc.vector.tensor_tensor(lg[b][:, 0, :, :], S[b][:, :, P:P + H], held[:, :, H:2 * H], ALU.add)
                        nc.vector.tensor_tensor(lg[b][:, 1, :, :], held[:, :, 0:H], held[:, :, H:2 * H], ALU.add)
                    nc.vector.tensor_copy(m[b][:, 0, :], m[1 - b][:, G, :])
                    v.drain()
                    logits, leaky = (z[b][:, :, :, :].rearrange("p k t h -> p (k t h)") for z in (lg, lr))
                    nc.vector.scalar_tensor_tensor(leaky, logits, SLOPE, logits, ALU.mult, ALU.max)
                    v.drain()
                    nc.vector.tensor_tensor(q[b][:, :, :], lr[b][:, 0, :, :], lr[b][:, 1, :, :], ALU.max)
                    v.drain()
                    for t in range(G):
                        nc.vector.scalar_tensor_tensor(m[b][:, t + 1, :], m[b][:, t, :], fresh[b][:, t:t + 1],
                                                       q[b][:, t, :], ALU.add, ALU.max)
                        v.drain()
                    now = m[b][:, 1:G + 1, :]
                    nc.vector.tensor_tensor(dd[b][:, 0, :, :], m[b][:, 0:G, :], now, ALU.subtract)
                    nc.vector.tensor_tensor(dd[b][:, 1, :, :], lr[b][:, 0, :, :], now, ALU.subtract)
                    nc.vector.tensor_tensor(dd[b][:, 2, :, :], lr[b][:, 1, :, :], now, ALU.subtract)
                    nc.vector.tensor_copy(st[b][:, :, nacc:nacc + H], now)
                    nc.vector.tensor_copy(st[b][:, :, nacc + H:nacc + 2 * H], lr[b][:, 1, :, :])
                    v.drain()
                    nc.vector.tensor_tensor(dd[b][:, 0, :, :], dd[b][:, 0, :, :],
                                            fresh[b][:, :].unsqueeze(2).to_broadcast([P, G, H]), ALU.add)
                    v.drain().then_inc(f1, 1)

                def sums(it, b):
                    n = it * 2 + b + 1
                    v.wait_ge(expd, n)
                    w, ws = wt[b][:, 1, :, :], wt[b][:, 2, :, :]
                    nc.vector.tensor_copy(msg[b][:, :, :, wd:wd + 1].rearrange("p t h a -> p t (h a)"), w)
                    if layer == 2:
                        v.wait_ge(d_in[b], (it + 1) * 16)
                    if layer < 3:
                        if layer == 1:
                            src = pm[b][0][:, :].rearrange("p (t h c) -> p t h c", t=G, h=H)
                            own = st[b][:, :, sw - P:sw].rearrange("p t (h c) -> p t h c", h=H)
                        else:
                            src, own = (z[b][:, :, 0:P].rearrange("p t (h c) -> p t h c", h=H) for z in (S, D))
                        nc.vector.tensor_tensor(msg[b][:, :, :, 0:wd], src, w.unsqueeze(3).to_broadcast([P, G, H, wd]), ALU.mult)
                        nc.vector.tensor_tensor(o[b][:, :, :, :], own, ws.unsqueeze(3).to_broadcast([P, G, H, wd]), ALU.mult)
                    v.drain()
                    if layer == 3:
                        v.wait_ge(weighted, n)
                    acc = st[b][:, :, 0:nacc].rearrange("p t (h c) -> p t h c", h=H)
                    before = st[1 - b][:, G - 1, 0:nacc].rearrange("p (h c) -> p h c", h=H)
                    for t in range(G):
                        for h in range(H):
                            old = before[:, h, :] if t == 0 else acc[:, t - 1, h, :]
                            nc.vector.scalar_tensor_tensor(acc[:, t, h, :], old, wt[b][:, 0, t, h:h + 1],
                                                           msg[b][:, t, h, :], ALU.mult, ALU.add)
                        v.drain()
                    v.sem_inc(f2, 1)
                    nc.vector.tensor_tensor(den[b][:, 0, :, :], acc[:, :, :, wd:wd + 1].rearrange("p t h a -> p t (h a)"), ws, ALU.add)
                    if layer < 3:
                        nc.vector.tensor_tensor(o[b][:, :, :, :], o[b][:, :, :, :], acc[:, :, :, 0:wd], ALU.add)
                    v.drain()
                    nc.vector.reciprocal(den[b][:, 1, :, :], den[b][:, 0, :, :])
                    if layer < 3:
                        v.drain()
                        if layer > 1:
                            v.sem_inc(in_free, 1)
                        nc.vector.tensor_tensor(o[b][:, :, :, :], o[b][:, :, :, :],
                                                den[b][:, 1, :, :].unsqueeze(3).to_broadcast([P, G, H, wd]), ALU.mult)
                        v.drain().then_inc(o_done, 1)
                    else:
                        v.wait_ge(d_in[b], (it + 1) * 16)
                        for t in range(G):
                            for h in range(H):
                                nc.vector.scalar_tensor_tensor(o[b][:, t, h, :], D[b][:, t, 0:P], wt[b][:, 2, t, h:h + 1],
                                                               acc[:, t, h, 0:P], ALU.mult, ALU.add)
                        v.drain().then_inc(summed, 1)
                        v.sem_inc(in_free, 1)

                def logits_out(it, b):
                    n = it * 2 + b + 1
                    v.wait_ge(r_free, n)
                    v.wait_ge(times, n)
                    logits = pm[b][2][:, logit_at:logit_at + G * 2 * H].rearrange("p (t c) -> p t c", t=G)
                    nc.vector.tensor_copy(r[b][:, :, P:ROW], logits)
                    nc.vector.tensor_copy(K["held"][:, :, cols(it, b)].rearrange("p c t -> p t c"), logits)
                    v.drain().then_inc(rows_done, 1)

                def residual(it, b):
                    v.wait_ge(times, it * 2 + b + 1)
                    v.wait_ge(xr_in[b], (it + 1) * 16)
                    nc.vector.tensor_tensor(y[b][:, :, :], pm[b][0][:, :].rearrange("p (t c) -> p t c", t=G), xr[b][:, :, :], ALU.add)
                    v.drain()
                    layer_norm_dve(nc, v, y[b], None, stats[b], aggr[b], None, G)
                    v.sem_inc(var, 1)

                def norm(it, b):
                    n = it * 2 + b + 1
                    v.wait_ge(r_free, n)
                    v.wait_ge(root, n)
                    layer_norm_apply(nc, v, y[b], r[b], aggr[b], rstd[b], G)
                    v.drain().then_inc(rows_done, 1)

                def both(stage, it):
                    for b in lanes:
                        stage(it, b)

                if layer > 1:
                    v.sem_inc(in_free, 2)
                nc.vector.memset(m[1][:, :, :], 0.0)
                nc.vector.memset(st[1][:, G - 1, 0:nacc], 0.0)
                v.drain()
                both(weights, 0)
                both(sums, 0)
                with v.Fori(1, iters) as it:
                    both(weights, it)
                    if layer == 3:
                        both(residual, it - 1)
                    else:
                        both(logits_out, it - 1)
                    both(sums, it)
                    if layer == 3:
                        both(norm, it - 1)
                if layer == 3:
                    both(residual, iters - 1)
                    both(norm, iters - 1)
                else:
                    both(logits_out, iters - 1)
                nc.vector.tensor_copy(K["carry_m"][:, :], m[1][:, G, :])
                nc.vector.tensor_copy(K["carry_acc"][:, 0:nacc], st[1][:, G - 1, 0:nacc])

        clear_semaphores(nc, used)


def seam_attend(nc, K, T, layer):
    wd, nacc, sw = WIDE[layer], ACC[layer], STATE[layer]
    blocks = 1 if layer < 3 else H
    hb = H // blocks
    with ExitStack() as ctx:
        def sb(name, shape, dt=FP32):
            return ctx.enter_context(nc.sbuf_tensor(f"s{layer}_{name}", shape, dt))

        used = []

        def sem(name):
            used.append(ctx.enter_context(nc.semaphore(f"s{layer}_{name}")))
            return used[-1]

        def bank(name):
            return ctx.enter_context(nc.psum_tensor(f"s{layer}_{name}", [P, 512], FP32))

        out_w = P if layer == 3 else ROW
        head = sb("head", [P, sw])
        xrow = sb("xrow", [P, ROW])
        tin = [sb(f"tin{k}", [P, 3, P]) for k in range(blocks)]
        tT = sb("tT", [P, 3, P])
        run = sb("run", [P, 3, P + 1])
        ex = sb("ex", [P, 2, P])
        we = sb("we", [P, 2, P])
        tw = sb("tw", [P, 2, P])
        cin = sb("cin", [P, 3, P])
        hm = sb("hm", [P, 4, P])
        e3 = sb("e3", [P, 3, P])
        w3 = sb("w3", [P, 3, P])
        u = sb("u", [P, 5, P])
        z = sb("z", [P, H, P] if layer == 3 else [P, 1, P])
        zT = sb("zT", [P, H, P] if layer == 3 else [P, 1, P])
        r = sb("r", [P, out_w])
        xr = sb("xr", [P, P])
        y = sb("y", [P, 1, P])
        stats, aggr, rstd = sb("stats", [P, 1, 6]), sb("aggr", [P, 1, 2]), sb("rstd", [P, 2, 1])
        val = sb("val", [P, 2 * H])
        pt, pback, ph, pr, pa = bank("pt"), bank("pback"), bank("ph"), bank("pr"), bank("pa")
        got, put = K["dma_sem"](f"s{layer}_got"), K["dma_sem"](f"s{layer}_put")
        packed, turned, f1, x1, carried, back, f2, x2, zdone, zturn, ztook, prod, rdone, var, root = (
            sem(s) for s in ("packed", "turned", "f1", "x1", "carried", "back", "f2", "x2", "zdone",
                             "zturn", "ztook", "prod", "rdone", "var", "root"))

        with nc.Block() as block:
            @block.gpsimd
            def _(g):
                at = bass.IndirectOffsetOnAxis(ap=K["head_slot_i"][:, :], axis=0)
                g.indirect_dma_start(head[:, :], None, T["st", layer][:, :], at).then_inc(got, 16)
                if layer > 1:
                    g.indirect_dma_start(xrow[:, :], None, T[layer][:, :],
                                         bass.IndirectOffsetOnAxis(ap=K["head_read_i"][:, :], axis=0)).then_inc(got, 16)
                if layer == 3:
                    g.indirect_dma_start(xr[:, :], None, T["xd"][:, :], at).then_inc(got, 16)
                g.wait_ge(rdone, 1)
                g.indirect_dma_start(T[layer + 1][:, :], bass.IndirectOffsetOnAxis(ap=K["head_row_i"][:, :], axis=0),
                                     r[:, :], None, bounds_check=NP + EP - 1, oob_is_err=False).then_inc(put, 16)
                g.wait_ge(put, 16)

            n_got = 16 * (1 + (layer > 1) + (layer == 3))

            @block.tensor
            def _(pe):
                for k in range(blocks):
                    pe.wait_ge(packed, k + 1)
                    for i in range(3):
                        ins = nc.tensor.transpose(pt[:, i * P:(i + 1) * P], tin[k][:, i, :], K["ident"][:, :])
                    ins.then_inc(turned, 1)
                    pe.wait_ge(carried, k + 1)
                    for i in range(3):
                        ins = nc.tensor.transpose(pback[:, i * P:(i + 1) * P], run[:, i, 0:P], K["ident"][:, :])
                    ins.then_inc(back, 1)
                pe.wait_ge(zdone, 1)
                for k in range(blocks):
                    ins = nc.tensor.transpose(ph[:, k * P:(k + 1) * P], z[:, k, :], K["ident"][:, :])
                ins.then_inc(zturn, 1)
                pe.wait_ge(ztook, 1)
                if layer == 3:
                    for k in range(H):
                        ins = nc.tensor.matmul(pr[:, 0:P], zT[:, k, :], K["W3"][:, k * P:(k + 1) * P], start=(k == 0), stop=(k == H - 1))
                else:
                    if layer == 1:
                        nc.tensor.matmul(pr[:, 0:P], zT[:, 0, :], K["W2"][:, :], start=True, stop=True)
                    ins = nc.tensor.matmul(pa[:, 0:2 * H], zT[:, 0, :], K[f"A{layer + 1}"][:, :], start=True, stop=True)
                ins.then_inc(prod, 1)

            @block.scalar
            def _(act):
                for k in range(blocks):
                    act.wait_ge(f1, k + 1)
                    nc.scalar.activation(we[:, :, :], ex[:, :, :], ACT.Exp).then_inc(x1, 1)
                    act.wait_ge(f2, k + 1)
                    nc.scalar.activation(w3[:, :, :], e3[:, :, :], ACT.Exp).then_inc(x2, 1)
                act.wait_ge(zturn, 1)
                nc.scalar.activation(zT[:, :, :].rearrange("p k c -> p (k c)"), ph[:, 0:blocks * P], ACT.Copy).then_inc(ztook, 1)
                if layer == 3:
                    act.wait_ge(var, 1)
                    nc.scalar.activation(rstd[:, 0, :], aggr[:, :, 1], ACT.Sqrt, bias=K["eps"][:, :]).then_inc(root, 1)

            @block.vector
            def _(v):
                def of_heads(ap, k):
                    return ap[:, k * hb:(k + 1) * hb].unsqueeze(2).to_broadcast([P, hb, wd])

                def heads(ap):
                    return ap.rearrange("p (h c) -> p h c", h=hb)

                tail_acc = K["carry_acc"][:, 0:nacc].rearrange("p (h c) -> p h c", h=H)
                head_acc = head[:, 0:nacc].rearrange("p (h c) -> p h c", h=H)
                nc.vector.memset(run[:, :, :], 0.0)
                v.wait_ge(got, n_got)
                for k in range(blocks):
                    hs = slice(k * hb, (k + 1) * hb)
                    nc.vector.tensor_copy(heads(tin[k][:, 0, :]), of_heads(K["carry_m"][:, :], k))
                    nc.vector.tensor_copy(heads(tin[k][:, 1, :]), tail_acc[:, hs, wd:wd + 1].to_broadcast([P, hb, wd]))
                    nc.vector.tensor_copy(heads(tin[k][:, 2, :]), tail_acc[:, hs, 0:wd])
                    v.drain().then_inc(packed, 1)
                    v.wait_ge(turned, k + 1)
                    nc.vector.tensor_copy(tT[:, :, :].rearrange("p i c -> p (i c)"), pt[:, 0:3 * P])
                    v.drain()
                    nc.vector.tensor_tensor_scan(run[:, 0, 1:P + 1], K["chain"][:, :], tT[:, 0, :], 0.0, ALU.add, ALU.max)
                    v.drain()
                    nc.vector.tensor_tensor(ex[:, 0, :], run[:, 0, 0:P], run[:, 0, 1:P + 1], ALU.subtract)
                    nc.vector.tensor_tensor(ex[:, 1, :], tT[:, 0, :], run[:, 0, 1:P + 1], ALU.subtract)
                    v.drain()
                    nc.vector.tensor_tensor(ex[:, 0, :], ex[:, 0, :], K["chain"][:, :], ALU.add)
                    v.drain().then_inc(f1, 1)
                    v.wait_ge(x1, k + 1)
                    for i in range(2):
                        nc.vector.tensor_tensor(tw[:, i, :], tT[:, i + 1, :], we[:, 1, :], ALU.mult)
                    v.drain()
                    for i in range(2):
                        nc.vector.tensor_tensor_scan(run[:, i + 1, 1:P + 1], we[:, 0, :], tw[:, i, :], 0.0, ALU.mult, ALU.add)
                    v.drain().then_inc(carried, 1)
                    v.wait_ge(back, k + 1)
                    nc.vector.tensor_copy(cin[:, :, :].rearrange("p i c -> p (i c)"), pback[:, 0:3 * P])
                    nc.vector.tensor_copy(heads(hm[:, 0, :]), of_heads(head[:, nacc:nacc + H], k))
                    nc.vector.tensor_copy(heads(hm[:, 1, :]), head_acc[:, hs, wd:wd + 1].to_broadcast([P, hb, wd]))
                    nc.vector.tensor_copy(heads(hm[:, 2, :]), of_heads(head[:, nacc + H:nacc + 2 * H], k))
                    v.drain()
                    nc.vector.tensor_scalar(cin[:, 0, :], cin[:, 0, :], K["joins"][:, :], None, ALU.add)
                    v.drain()
                    nc.vector.tensor_tensor(hm[:, 3, :], cin[:, 0, :], hm[:, 0, :], ALU.max)
                    v.drain()
                    nc.vector.tensor_tensor(e3[:, 0, :], cin[:, 0, :], hm[:, 3, :], ALU.subtract)
                    nc.vector.tensor_tensor(e3[:, 1, :], hm[:, 0, :], hm[:, 3, :], ALU.subtract)
                    nc.vector.tensor_tensor(e3[:, 2, :], hm[:, 2, :], hm[:, 3, :], ALU.subtract)
                    v.drain().then_inc(f2, 1)
                    v.wait_ge(x2, k + 1)
                    nc.vector.tensor_tensor(u[:, 0, :], cin[:, 1, :], w3[:, 0, :], ALU.mult)
                    nc.vector.tensor_tensor(u[:, 1, :], hm[:, 1, :], w3[:, 1, :], ALU.mult)
                    nc.vector.tensor_tensor(u[:, 2, :], cin[:, 2, :], w3[:, 0, :], ALU.mult)
                    nc.vector.tensor_tensor(heads(u[:, 3, :]), head_acc[:, hs, 0:wd], heads(w3[:, 1, :]), ALU.mult)
                    xd = head[:, sw - P:sw] if layer == 1 else xrow[:, 0:P]
                    nc.vector.tensor_tensor(u[:, 4, :], xd, w3[:, 2, :], ALU.mult)
                    v.drain()
                    nc.vector.tensor_tensor(u[:, 0, :], u[:, 0, :], u[:, 1, :], ALU.add)
                    nc.vector.tensor_tensor(u[:, 2, :], u[:, 2, :], u[:, 3, :], ALU.add)
                    v.drain()
                    nc.vector.tensor_tensor(u[:, 0, :], u[:, 0, :], w3[:, 2, :], ALU.add)
                    nc.vector.tensor_tensor(u[:, 2, :], u[:, 2, :], u[:, 4, :], ALU.add)
                    v.drain()
                    nc.vector.reciprocal(u[:, 1, :], u[:, 0, :])
                    v.drain()
                    nc.vector.tensor_tensor(z[:, k, :], u[:, 2, :], u[:, 1, :], ALU.mult)
                    v.drain()
                if layer < 3:
                    nc.vector.tensor_scalar(z[:, 0, :], z[:, 0, :], 0.0, None, ALU.max)
                    v.drain()
                v.sem_inc(zdone, 1)
                v.wait_ge(prod, 1)
                if layer < 3:
                    if layer == 1:
                        nc.vector.tensor_tensor(r[:, 0:P], pr[:, 0:P], K["b2r"][:, :], ALU.add)
                    else:
                        nc.vector.tensor_copy(r[:, 0:P], z[:, 0, :])
                    nc.vector.tensor_copy(r[:, P:ROW], pa[:, 0:2 * H])
                    nc.vector.tensor_copy(val[:, :], pa[:, 0:2 * H])
                    v.drain().then_inc(rdone, 1)
                    for c in range(2 * H):
                        old = K["held"][:, c, :]
                        nc.vector.tensor_tensor(old, old, K["not_headend"][:, :], ALU.mult)
                    v.drain()
                    for c in range(2 * H):
                        old = K["held"][:, c, :]
                        nc.vector.scalar_tensor_tensor(old, K["headend"][:, :], val[:, c:c + 1], old, ALU.mult, ALU.add)
                else:
                    nc.vector.tensor_tensor(y[:, 0, :], pr[:, 0:P], xr[:, :], ALU.add)
                    v.drain()
                    nc.vector.tensor_tensor(y[:, 0, :], y[:, 0, :], K["b3r"][:, :], ALU.add)
                    v.drain()
                    layer_norm_dve(nc, v, y, None, stats, aggr, None, 1)
                    v.sem_inc(var, 1)
                    v.wait_ge(root, 1)
                    layer_norm_apply(nc, v, y, r[:, :].unsqueeze(1), aggr, rstd, 1)
                    v.drain().then_inc(rdone, 1)

        clear_semaphores(nc, used)


def hold_logits(nc, K, T, layer):
    with ExitStack() as ctx:
        tail = ctx.enter_context(nc.sbuf_tensor(f"h{layer}_tail", [P, ROW], FP32))
        masked = ctx.enter_context(nc.sbuf_tensor(f"h{layer}_masked", [P, 2 * H, COLS], FP32))
        got = K["dma_sem"](f"h{layer}_got")
        with nc.Block() as block:
            @block.gpsimd
            def _(g):
                g.indirect_dma_start(tail[:, :], None, T[layer][:, :],
                                     bass.IndirectOffsetOnAxis(ap=K["tail_row_i"][:, :], axis=0)).then_inc(got, 16)

            @block.vector
            def _(v):
                for c in range(2 * H):
                    nc.vector.tensor_tensor(masked[:, c, :], K["held"][:, c, :], K["last"][:, :], ALU.mult)
                v.wait_ge(got, 16)
                v.drain()
                for c in range(2 * H):
                    nc.vector.tensor_tensor_scan(K["held"][:, c, ::-1], K["goes_on"][:, ::-1], masked[:, c, ::-1],
                                                 tail[:, P + c:P + c + 1], ALU.mult, ALU.add)

def message(nc, A, K, T, out):
    lanes = range(2)
    with ExitStack() as ctx:
        def sb(name, shape, dt=FP32):
            return ctx.enter_context(nc.sbuf_tensor("e_" + name, shape, dt))

        used = []

        def sem(name):
            used.append(ctx.enter_context(nc.semaphore("e_" + name)))
            return used[-1]

        S = [sb(f"src{b}", [P, G, P]) for b in lanes]
        D = [sb(f"dst{b}", [P, G, P]) for b in lanes]
        idx = [sb(f"idx{b}", [P, 3, G], I32) for b in lanes]
        wrow = [sb(f"wrow{b}", [1, G * P]) for b in lanes]
        fresh = [sb(f"fresh{b}", [P, G]) for b in lanes]
        sT = [sb(f"sT{b}", [P, G * P]) for b in lanes]
        dT = [sb(f"dT{b}", [P, G * P]) for b in lanes]
        rT = [sb(f"rT{b}", [P, G * P]) for b in lanes]
        gT = [sb(f"gT{b}", [P, G * P]) for b in lanes]
        uT = [sb(f"uT{b}", [P, G * P]) for b in lanes]
        agg = [sb(f"agg{b}", [P, G, P]) for b in lanes]
        xnew = [sb(f"xnew{b}", [P, G, P]) for b in lanes]
        xres = [sb(f"xres{b}", [P, G, P]) for b in lanes]
        y = [sb(f"y{b}", [P, G, P]) for b in lanes]
        fin = [sb(f"fin{b}", [P, G, P]) for b in lanes]
        to = [sb(f"to{b}", [P, G], I32) for b in lanes]
        stats = [sb(f"stats{b}", [P, G, 6]) for b in lanes]
        aggr = [sb(f"aggr{b}", [P, G, 2]) for b in lanes]
        rstd = [sb(f"rstd{b}", [P, 2, G]) for b in lanes]
        pm = [[ctx.enter_context(nc.psum_tensor(f"e_p{b}{k}", [P, G * P], FP32)) for k in range(4)] for b in lanes]
        w_in, agg_stored = ([sem(f"{s}{b}") for b in lanes] for s in ("w_in", "agg_stored"))
        arrived, sent = ([K["dma_sem"](f"e_{s}{b}") for b in lanes] for s in ("arrived", "sent"))
        (in_free, tick, staged, turned, took, pre, took_r, msgs, maxed, turned_g, took_g, upd, took_u, last_mm,
         var, root, fin_done, out_free, agg_free, y_read, msg_read) = (
            sem(s) for s in ("in_free", "tick", "staged", "turned", "took", "pre", "took_r", "msgs", "maxed",
                             "turned_g", "took_g", "upd", "took_u", "last_mm", "var", "root", "fin_done", "out_free",
                             "agg_free", "y_read", "msg_read"))
        sp_tick = sem("sp_tick")
        iters = EG // 2

        def cols(it, b):
            return bass.ds((it * 2 + b) * G, G)

        w_rows = A["w"].rearrange("(g t) p -> g (t p)", t=G)
        agg_rows = T["st", 4].rearrange("(p j) c -> p j c", p=P)

        def both(stage, it):
            for b in lanes:
                stage(it, b)

        with nc.Block() as block:
            @block.gpsimd
            def _(g):
                def gather(it, b, staged_before):
                    g.wait_ge(in_free, it * 2 + b + 1)
                    g.sem_inc(tick, 1)
                    nc.gpsimd.tensor_copy(idx[b][:, 0, :], K["gsrc_i"][:, cols(it, b)]).then_inc(staged, 1)
                    nc.gpsimd.tensor_copy(idx[b][:, 1, :], K["gdst_i"][:, cols(it, b)]).then_inc(staged, 1)
                    g.wait_ge(staged, staged_before + 2)
                    g.sem_inc(tick, 1)
                    for t in range(G):
                        for k, rows in enumerate((S, D)):
                            g.indirect_dma_start(rows[b][:, t, :], None, T[4][:, :],
                                                 bass.IndirectOffsetOnAxis(ap=idx[b][:, k, t:t + 1], axis=0)).then_inc(arrived[b], 16)

                def scatter(it, staged_before):
                    for b in lanes:
                        nc.gpsimd.tensor_copy(to[b][:, :], K["scat_i"][:, cols(it, b)]).then_inc(staged, 1)
                    g.wait_ge(staged, staged_before + 2)
                    g.sem_inc(tick, 1)
                    for b in lanes:
                        g.wait_ge(fin_done, it * 2 + b + 1)
                        g.sem_inc(tick, 1)
                        for t in range(G):
                            g.indirect_dma_start(out[:, :], bass.IndirectOffsetOnAxis(ap=to[b][:, t:t + 1], axis=0),
                                                 fin[b][:, t, :], None, bounds_check=NP - 1, oob_is_err=False).then_inc(sent[b], 16)
                    for b in lanes:
                        g.wait_ge(sent[b], (it + 1) * (16 * G))
                        g.sem_inc(out_free, 1)

                g.sem_inc(out_free, 2)
                for r in range(2):
                    for b in lanes:
                        gather(r, b, 4 * r + 2 * b)
                with g.Fori(1, iters - 1) as it:
                    for b in lanes:
                        gather(it + 1, b, it * 6 + 2 * b + 2)
                    scatter(it - 1, it * 6 + 6)
                scatter(iters - 2, iters * 6 - 4)
                scatter(iters - 1, iters * 6 - 2)

            @block.sync
            def _(sp):
                sp.sem_inc(agg_free, 2)
                for b in lanes:
                    sp.dma_start(wrow[b][:, :], w_rows[b:b + 1, :]).then_inc(w_in[b], 16)
                with sp.Fori(0, iters) as it:
                    for b in lanes:
                        sp.wait_ge(maxed, it * 2 + b + 1)
                        sp.sem_inc(sp_tick, 1)
                        sp.dma_start(agg_rows[:, cols(it, b), :], agg[b][:, :, :]).then_inc(agg_stored[b], 16)
                        sp.dma_start(wrow[b][:, :], w_rows[bass.ds(it * 2 + b + 2, 1), :]).then_inc(w_in[b], 16)
                    for b in lanes:
                        sp.wait_ge(agg_stored[b], (it + 1) * 16)
                        sp.sem_inc(agg_free, 1)
                for b in lanes:
                    sp.wait_ge(w_in[b], (iters + 1) * 16)

            @block.tensor
            def _(pe):
                def turn_in(it, b):
                    pe.wait_ge(arrived[b], (it + 1) * (16 * 2 * G))
                    pe.wait_ge(msg_read, it * 2 + b + 1)
                    for k, rows in enumerate((S, D)):
                        for t in range(G):
                            ins = nc.tensor.transpose(pm[b][k][:, t * P:(t + 1) * P], rows[b][:, t, :], K["ident"][:, :])
                    ins.then_inc(turned, 1)

                def edge_in(it, b):
                    pe.wait_ge(took, it * 2 + b + 1)
                    pe.wait_ge(w_in[b], (it + 1) * 16)
                    nc.tensor.matmul(pm[b][0][:, :], K["M1a"][:, :], sT[b][:, :], start=True, stop=False)
                    nc.tensor.matmul(pm[b][0][:, :], K["M1b"][:, :], dT[b][:, :], start=False, stop=False)
                    nc.tensor.matmul(pm[b][0][:, :], K["w1c"][:, :], wrow[b][:, :], start=False, stop=True).then_inc(pre, 1)

                def edge_out(it, b):
                    pe.wait_ge(took_r, it * 2 + b + 1)
                    add_bias(nc, K, pm[b][1], "m2")
                    for t in range(G):
                        ins = nc.tensor.matmul(pm[b][1][:, t * P:(t + 1) * P], rT[b][:, t * P:(t + 1) * P], K["M2"][:, :],
                                               start=False, stop=(t == G - 1))
                    ins.then_inc(msgs, 1)

                def own_part(it, b):
                    nc.tensor.matmul(pm[b][2][:, :], K["U1a"][:, :], dT[b][:, :], start=True, stop=False)

                def turn_max(it, b):
                    pe.wait_ge(y_read, it * 2 + b + 1)
                    pe.wait_ge(maxed, it * 2 + b + 1)
                    for t in range(G):
                        ins = nc.tensor.transpose(pm[b][3][:, t * P:(t + 1) * P], agg[b][:, t, :], K["ident"][:, :])
                    ins.then_inc(turned_g, 1)

                def node_in(it, b):
                    pe.wait_ge(took_g, it * 2 + b + 1)
                    nc.tensor.matmul(pm[b][2][:, :], K["U1b"][:, :], gT[b][:, :], start=False, stop=True).then_inc(upd, 1)

                def node_out(it, b):
                    pe.wait_ge(took_u, it * 2 + b + 1)
                    add_bias(nc, K, pm[b][3], "c2")
                    for t in range(G):
                        ins = nc.tensor.matmul(pm[b][3][:, t * P:(t + 1) * P], uT[b][:, t * P:(t + 1) * P], K["U2"][:, :],
                                               start=False, stop=(t == G - 1))
                    ins.then_inc(last_mm, 1)

                for stage in (turn_in, edge_in, edge_out, own_part):
                    both(stage, 0)
                with pe.Fori(1, iters) as it:
                    both(turn_in, it)
                    both(turn_max, it - 1)
                    both(edge_in, it)
                    both(node_in, it - 1)
                    both(edge_out, it)
                    both(node_out, it - 1)
                    both(own_part, it)
                for stage in (turn_max, node_in, node_out):
                    both(stage, iters - 1)

            @block.scalar
            def _(act):
                def take_in(it, b):
                    act.wait_ge(turned, it * 2 + b + 1)
                    nc.scalar.activation(sT[b][:, :], pm[b][0][:, :], ACT.Copy)
                    nc.scalar.activation(dT[b][:, :], pm[b][1][:, :], ACT.Copy).then_inc(took, 1)

                def take_edge(it, b):
                    act.wait_ge(pre, it * 2 + b + 1)
                    nc.scalar.activation(rT[b][:, :], pm[b][0][:, :], ACT.Relu, bias=K["mb1"][:, :]).then_inc(took_r, 1)

                def take_max(it, b):
                    act.wait_ge(turned_g, it * 2 + b + 1)
                    nc.scalar.activation(gT[b][:, :], pm[b][3][:, :], ACT.Copy).then_inc(took_g, 1)

                def take_node(it, b):
                    act.wait_ge(upd, it * 2 + b + 1)
                    nc.scalar.activation(uT[b][:, :], pm[b][2][:, :], ACT.Relu, bias=K["c1"][:, :]).then_inc(took_u, 1)

                def roots(it, b):
                    act.wait_ge(var, it * 2 + b + 1)
                    nc.scalar.activation(rstd[b][:, 0, :], aggr[b][:, :, 1], ACT.Sqrt, bias=K["eps"][:, :]).then_inc(root, 1)

                both(take_in, 0)
                both(take_edge, 0)
                with act.Fori(1, iters) as it:
                    both(take_in, it)
                    both(take_max, it - 1)
                    both(take_edge, it)
                    both(take_node, it - 1)
                    both(roots, it - 1)
                for stage in (take_max, take_node, roots):
                    both(stage, iters - 1)

            @block.vector
            def _(v):
                def keep(it, b):
                    v.wait_ge(turned, it * 2 + b + 1)
                    nc.vector.tensor_copy(xnew[b][:, :, :], D[b][:, :, :])
                    nc.vector.tensor_copy(fresh[b][:, :], K["fresh"][:, cols(it, b)])
                    v.drain().then_inc(in_free, 1)

                def pass_on(it, b):
                    nc.vector.tensor_copy(xres[b][:, :, :], xnew[b][:, :, :])

                def maximum(it, b):
                    n = it * 2 + b + 1
                    v.wait_ge(agg_free, n)
                    v.wait_ge(msgs, n)
                    for t in range(G):
                        old = agg[1 - b][:, G - 1, :] if t == 0 else agg[b][:, t - 1, :]
                        nc.vector.scalar_tensor_tensor(agg[b][:, t, :], old, fresh[b][:, t:t + 1],
                                                       pm[b][1][:, t * P:(t + 1) * P], ALU.add, ALU.max)
                        v.drain()
                    v.sem_inc(maxed, 1)
                    v.sem_inc(msg_read, 1)

                def residual(it, b):
                    v.wait_ge(last_mm, it * 2 + b + 1)
                    nc.vector.tensor_tensor(y[b][:, :, :], pm[b][3][:, :].rearrange("p (t c) -> p t c", t=G), xres[b][:, :, :], ALU.add)
                    v.drain().then_inc(y_read, 1)
                    layer_norm_dve(nc, v, y[b], None, stats[b], aggr[b], None, G)
                    v.sem_inc(var, 1)

                def norm(it, b):
                    n = it * 2 + b + 1
                    v.wait_ge(out_free, n)
                    v.wait_ge(root, n)
                    layer_norm_apply(nc, v, y[b], fin[b], aggr[b], rstd[b], G)
                    v.drain().then_inc(fin_done, 1)

                nc.vector.memset(agg[1][:, :, :], 0.0)
                v.drain()
                v.sem_inc(y_read, 2)
                v.sem_inc(msg_read, 2)
                v.sem_inc(in_free, 2)
                both(keep, 0)
                both(maximum, 0)
                both(pass_on, 0)
                v.drain()
                with v.Fori(1, iters) as it:
                    both(keep, it)
                    both(maximum, it)
                    both(residual, it - 1)
                    both(norm, it - 1)
                    both(pass_on, it)
                    v.drain()
                both(residual, iters - 1)
                both(norm, iters - 1)
                nc.vector.tensor_copy(K["carry_acc"][:, 0:P], agg[1][:, G - 1, :])

        clear_semaphores(nc, used)


def seam_message(nc, K, T, out):
    with ExitStack() as ctx:
        def sb(name, shape, dt=FP32):
            return ctx.enter_context(nc.sbuf_tensor("z_" + name, shape, dt))

        used = []

        def sem(name):
            used.append(ctx.enter_context(nc.semaphore("z_" + name)))
            return used[-1]

        head, xd, g, y, r = sb("head", [P, P]), sb("xd", [P, P]), sb("g", [P, P]), sb("y", [P, 1, P]), sb("r", [P, 1, P])
        tT, run, cin = sb("tT", [P, P]), sb("run", [P, P + 1]), sb("cin", [P, P])
        xT, gT, uT = sb("xT", [P, P]), sb("gT", [P, P]), sb("uT", [P, P])
        stats, aggr, rstd = sb("stats", [P, 1, 6]), sb("aggr", [P, 1, 2]), sb("rstd", [P, 2, 1])
        ps = [ctx.enter_context(nc.psum_tensor(f"z_p{k}", [P, 512], FP32)) for k in range(6)]
        s, a, d = sem("pe"), sem("act"), sem("dve")
        got, put = K["dma_sem"]("z_got"), K["dma_sem"]("z_put")

        with nc.Block() as block:
            @block.gpsimd
            def _(p):
                p.indirect_dma_start(head[:, :], None, T["st", 4][:, :],
                                     bass.IndirectOffsetOnAxis(ap=K["head_slot_i"][:, :], axis=0)).then_inc(got, 16)
                p.indirect_dma_start(xd[:, :], None, T[4][:, :],
                                     bass.IndirectOffsetOnAxis(ap=K["head_read_i"][:, :], axis=0)).then_inc(got, 16)
                p.wait_ge(d, 4)
                p.indirect_dma_start(out[:, :], bass.IndirectOffsetOnAxis(ap=K["head_out_i"][:, :], axis=0),
                                     r[:, 0, :], None, bounds_check=NP - 1, oob_is_err=False).then_inc(put, 16)
                p.wait_ge(put, 16)

            @block.tensor
            def _(pe):
                nc.tensor.transpose(ps[0][:, 0:P], K["carry_acc"][:, 0:P], K["ident"][:, :])
                pe.wait_ge(got, 32)
                nc.tensor.transpose(ps[1][:, 0:P], xd[:, :], K["ident"][:, :]).then_inc(s, 1)
                pe.wait_ge(d, 1)
                nc.tensor.transpose(ps[2][:, 0:P], run[:, 0:P], K["ident"][:, :]).then_inc(s, 1)
                pe.wait_ge(d, 2)
                nc.tensor.transpose(ps[3][:, 0:P], g[:, :], K["ident"][:, :]).then_inc(s, 1)
                pe.wait_ge(a, 2)
                nc.tensor.matmul(ps[4][:, 0:P], K["U1a"][:, :], xT[:, :], start=True, stop=False)
                nc.tensor.matmul(ps[4][:, 0:P], K["U1b"][:, :], gT[:, :], start=False, stop=True).then_inc(s, 1)
                pe.wait_ge(a, 3)
                nc.tensor.matmul(ps[5][:, 0:P], uT[:, :], K["U2"][:, :], start=True, stop=True).then_inc(s, 1)

            @block.scalar
            def _(act):
                act.wait_ge(s, 1)
                nc.scalar.activation(xT[:, :], ps[1][:, 0:P], ACT.Copy).then_inc(a, 1)
                act.wait_ge(s, 3)
                nc.scalar.activation(gT[:, :], ps[3][:, 0:P], ACT.Copy).then_inc(a, 1)
                act.wait_ge(s, 4)
                nc.scalar.activation(uT[:, :], ps[4][:, 0:P], ACT.Relu, bias=K["c1"][:, :]).then_inc(a, 1)
                act.wait_ge(d, 3)
                nc.scalar.activation(rstd[:, 0, :], aggr[:, :, 1], ACT.Sqrt, bias=K["eps"][:, :]).then_inc(a, 1)

            @block.vector
            def _(v):
                nc.vector.memset(run[:, :], 0.0)
                v.wait_ge(s, 1)
                nc.vector.tensor_copy(tT[:, :], ps[0][:, 0:P])
                v.drain()
                nc.vector.tensor_tensor_scan(run[:, 1:P + 1], K["chain"][:, :], tT[:, :], 0.0, ALU.add, ALU.max)
                v.drain().then_inc(d, 1)
                v.wait_ge(s, 2)
                nc.vector.tensor_scalar(cin[:, :], ps[2][:, 0:P], K["joins"][:, :], None, ALU.add)
                v.drain()
                nc.vector.tensor_tensor(g[:, :], cin[:, :], head[:, :], ALU.max)
                v.drain().then_inc(d, 1)
                v.wait_ge(s, 5)
                nc.vector.tensor_tensor(y[:, 0, :], ps[5][:, 0:P], xd[:, :], ALU.add)
                v.drain()
                nc.vector.tensor_tensor(y[:, 0, :], y[:, 0, :], K["c2r"][:, :], ALU.add)
                v.drain()
                layer_norm_dve(nc, v, y, None, stats, aggr, None, 1)
                v.sem_inc(d, 1)
                v.wait_ge(a, 4)
                layer_norm_apply(nc, v, y, r, aggr, rstd, 1)
                v.drain().then_inc(d, 1)

        clear_semaphores(nc, used)



TABLE_KIND = "Internal"



def kernel(**inputs):
    import numpy as _np
    import concourse.bacc as _bacc
    from concourse import mybir as _mybir
    from concourse.bass_utils import run_bass_kernel_spmd as _run

    nc = _bacc.Bacc("TRN2", target_bir_lowering=False, num_devices=1)
    inputs = {k: _np.ascontiguousarray(v) for k, v in inputs.items()}
    x = _np.zeros((NP + DLANES * G * P, P), inputs["x"].dtype)
    x[:N] = inputs["x"]
    pad = EP - E
    src = _np.concatenate([inputs["src"], _np.zeros(pad, inputs["src"].dtype)])
    dst = _np.concatenate([inputs["dst"], _np.full(pad, N, inputs["dst"].dtype)])
    w = _np.concatenate([inputs["edge_weight"], _np.zeros(pad, inputs["edge_weight"].dtype)])
    edge = _np.full(1, -1, dst.dtype)
    arrays = {
        "x": x, "src": src.reshape(P, COLS), "dst": dst.reshape(P, COLS),
        "dst_before": _np.concatenate([edge, dst[:-1]]).reshape(P, COLS),
        "dst_after": _np.concatenate([dst[1:], edge]).reshape(P, COLS),
        "w": _np.concatenate([w.reshape(P, COLS).T, _np.zeros((2 * G, P), w.dtype)]),
        "node_ids": _np.arange(NP, dtype=_np.int32).reshape(NP, 1),
        "slot_ids": (NP + _np.arange(EP, dtype=_np.int32)).reshape(P, COLS),
        "eye": _np.eye(P, dtype=_np.float32),
    }
    for name, value in inputs.items():
        if name.startswith(("L0_", "L1_")):
            arrays[name] = value
    feeds, aps = {}, {}
    for name, a in arrays.items():
        feeds["in_" + name] = a
        aps[name] = nc.dram_tensor("in_" + name, a.shape, _mybir.dt.from_np(a.dtype), kind="ExternalInput").ap()
    out = nc.dram_tensor("out_rows", (NP, P), _mybir.dt.float32, kind="ExternalOutput").ap()
    build(nc, aps, out)
    r = _run(nc, [feeds], core_ids=[0])
    return r.results[0]["out_rows"][:N]
```

```python
import concourse.bass as bass
from concourse import mybir
from contextlib import ExitStack

FP32 = mybir.dt.float32
BF16 = mybir.dt.bfloat16
I32 = mybir.dt.int32
ALU = mybir.AluOpType
ACT = mybir.ActivationFunctionType
AX = mybir.AxisListType

P = 128
N = 100000
E = 50000
H = 4
C = P // H
G = 4
COLS = 392
EP = P * COLS
EG = COLS // G
NG = (N + G * P - 1) // (G * P)
NP = NG * G * P
FAR = float(1 << 22)
BIG = 1e30
ROW = P + 2 * H
SLOPE = 0.2
EPS = 1e-5
DLANES = 4
MG = 8
LAYERS = (1, 2, 3)
BIASES = ("b1", "b2", "b3", "m2", "c2")
WIDE = {1: C, 2: C, 3: P}
ACC = {l: H * (WIDE[l] + 1) for l in LAYERS}
STATE = {1: ACC[1] + 2 * H + P, 2: ACC[2] + 2 * H, 3: ACC[3] + 2 * H, 4: P}


def build(nc, A, out):
    ctx = ExitStack()
    with ctx:
        def sb(name, shape, dt=FP32):
            return ctx.enter_context(nc.sbuf_tensor(name, shape, dt))

        K = {}
        for name in ("ident", "W1", "W2", "W3m", "U1a", "U1b", "U2", "M1a", "M1b", "M2",
                     "b2r", "b3r", "c2r"):
            K[name] = sb("k_" + name, [P, P])
        K["W3"] = sb("k_W3", [P, H * P])
        K["w1c"] = sb("k_w1c", [1, P])
        K["ones"] = sb("k_ones", [P, P], BF16)
        K["parts"] = sb("k_parts", [P, len(BIASES), G, P], BF16)
        for name in ("b1", "b2", "mb1", "c1", "eps"):
            K[name] = sb("k_" + name + "_col", [P, 1])
        for name in ("A1", "A2", "A3"):
            K[name] = sb("k_" + name, [P, 2 * H])
        for name in ("src_i", "dst_i", "scat_i", "slot_i", "gsrc_i", "gdst_i"):
            K[name] = sb("k_" + name, [P, COLS], I32)
        K["fresh"] = sb("k_fresh", [P, COLS])
        K["last"] = sb("k_last", [P, COLS])
        K["goes_on"] = sb("k_goes_on", [P, COLS])
        K["headend"] = sb("k_headend", [P, COLS])
        K["joins"] = sb("k_joins", [P, 1])
        K["chain"] = sb("k_chain", [P, P])
        K["head_slot_i"] = sb("k_head_slot_i", [P, 1], I32)
        K["head_row_i"] = sb("k_head_row_i", [P, 1], I32)
        K["head_out_i"] = sb("k_head_out_i", [P, 1], I32)
        K["tail_row_i"] = sb("k_tail_row_i", [P, 1], I32)
        K["head_read_i"] = sb("k_head_read_i", [P, 1], I32)
        K["not_headend"] = sb("k_not_headend", [P, COLS])
        K["tail"] = sb("k_tail", [P, 1])
        K["held"] = sb("k_held", [P, 2 * H, COLS])
        K["carry_m"] = sb("k_carry_m", [P, H])
        K["carry_acc"] = sb("k_carry_acc", [P, ACC[3]])

        T = {l: nc.dram_tensor(f"table_{l}", [NP + EP, P if l == 4 else ROW], FP32, kind=TABLE_KIND).ap()
             for l in (2, 3, 4)}
        T["map"] = nc.dram_tensor("node_row", [NP, 1], I32, kind=TABLE_KIND).ap()
        T["xd"] = nc.dram_tensor("slot_x", [EP, P], FP32, kind="Internal").ap()
        for l in (1, 2, 3, 4):
            T["st", l] = nc.dram_tensor(f"slot_state_{l}", [EP, STATE[l]], FP32, kind="Internal").ap()

        K["dma_sem"] = lambda name: ctx.enter_context(nc.semaphore(name))

        prepare(nc, A, K, T)
        dense(nc, A, K, T, out)
        look_up_dst(nc, K, T)
        for layer in LAYERS:
            attend(nc, A, K, T, layer)
            seam_attend(nc, K, T, layer)
            if layer < 3:
                hold_logits(nc, K, T, layer + 1)
        message(nc, A, K, T, out)
        seam_message(nc, K, T, out)


def clear_semaphores(nc, used):
    with nc.Block() as block:
        @block.gpsimd
        def _(g):
            for s in used:
                g.sem_clear(s)


def prepare(nc, A, K, T):
    with ExitStack() as ctx:
        def sb(name, shape, dt=FP32):
            return ctx.enter_context(nc.sbuf_tensor(name, shape, dt))

        used = []

        def sem(name):
            used.append(ctx.enter_context(nc.semaphore(name)))
            return used[-1]

        att = {(k, l): sb(f"att_{k}{l}", [P, P if l < 3 else H * P]) for k in "sd" for l in LAYERS}
        prod = sb("prep_prod", [P, H * P])
        w3raw = sb("prep_w3", [P, H * P])
        prev_i = sb("prep_prev_i", [P, COLS], I32)
        next_i = sb("prep_next_i", [P, COLS], I32)
        dstf = sb("prep_dst", [P, COLS])
        prevf = sb("prep_prev", [P, COLS])
        nextf = sb("prep_next", [P, COLS])
        slotf = sb("prep_slot", [P, COLS])
        inhead = sb("prep_inhead", [P, COLS])
        work = sb("prep_work", [P, COLS])
        ends = sb("prep_ends", [P, 4])
        wide = sb("prep_wide", [P, P])
        ps = ctx.enter_context(nc.psum_tensor("prep_ps", [P, 512], FP32))
        loaded, built, turned, mapped = sem("p_loaded"), sem("p_built"), sem("p_turned"), sem("p_mapped")
        plain = [("ident", A["eye"][:, :]), ("W1", A["L0_gnn_W1"][:, :]), ("W2", A["L0_gnn_W2"][:, :]),
                 ("U1a", A["L1_gnn_U1"][0:P, :]), ("U1b", A["L1_gnn_U1"][P:2 * P, :]),
                 ("U2", A["L1_gnn_U2"][:, :]), ("M1a", A["L1_gnn_W1"][0:P, :]),
                 ("M1b", A["L1_gnn_W1"][P:2 * P, :]), ("w1c", A["L1_gnn_W1"][2 * P:2 * P + 1, :]),
                 ("M2", A["L1_gnn_W2"][:, :]), ("src_i", A["src"][:, :]), ("dst_i", A["dst"][:, :]),
                 ("slot_i", A["slot_ids"][:, :])]
        spread = [("b2r", "L0_gnn_b2"), ("b3r", "L0_gnn_b3"), ("c2r", "L1_gnn_c2")]
        rows = ("L0_gnn_b1", "L0_gnn_b2", "L0_gnn_b3", "L1_gnn_b2", "L1_gnn_c2")
        cols = [("b1", "L0_gnn_b1"), ("b2", "L0_gnn_b2"), ("mb1", "L1_gnn_b1"), ("c1", "L1_gnn_c1")]
        loads = len(plain) + len(spread) + len(cols) + len(rows) + 3 + 6
        nb = len(BIASES) * P
        brow = sb("prep_brow", [1, nb])
        left = sb("prep_left", [1, nb])
        part = sb("prep_part", [1, 3, nb], BF16)
        split, spread_out = sem("p_split"), sem("p_spread_out")

        with nc.Block() as block:
            @block.sync
            def _(sp):
                for name, src in plain:
                    sp.dma_start(K[name][:, :], src).then_inc(loaded, 16)
                sp.dma_start(w3raw[:, :], A["L0_gnn_W3"][:, :]).then_inc(loaded, 16)
                sp.dma_start(prev_i[:, :], A["dst_before"][:, :]).then_inc(loaded, 16)
                sp.dma_start(next_i[:, :], A["dst_after"][:, :]).then_inc(loaded, 16)
                for name, src in spread:
                    sp.dma_start(K[name][:, :], A[src].partition_broadcast(P)).then_inc(loaded, 16)
                for i, src in enumerate(rows):
                    sp.dma_start(brow[:, i * P:(i + 1) * P], A[src].rearrange("(a n) -> a n", a=1)).then_inc(loaded, 16)
                for name, src in cols:
                    sp.dma_start(K[name][:, :], A[src].rearrange("(p a) -> p a", a=1)).then_inc(loaded, 16)
                for l in LAYERS:
                    for k in "sd":
                        sp.dma_start(att[k, l][:, :], A[f"L0_gnn_a{k}{l}"].rearrange("h c -> (h c)")
                                     .partition_broadcast(P)).then_inc(loaded, 16)
                sp.dma_start(T["map"].rearrange("(p n) a -> p (n a)", p=P),
                             A["node_ids"].rearrange("(p n) a -> p (n a)", p=P)).then_inc(mapped, 16)
                sp.wait_ge(mapped, 16)
                sp.wait_ge(split, 1)
                for k in range(3):
                    for t in range(G):
                        sp.dma_start(K["parts"][k:k + 1, :, t, :], part[:, k, :].rearrange("a (b n) -> a b n", n=P)).then_inc(spread_out, 16)
                sp.wait_ge(spread_out, 16 * 3 * G)

            @block.vector
            def _(v):
                nc.vector.memset(K["eps"][:, :], EPS)
                nc.vector.memset(K["ones"][:, :], 1.0)
                nc.vector.memset(K["parts"][:, :, :, :], 0.0)
                v.wait_ge(loaded, 16 * loads)
                nc.vector.tensor_copy(left[:, :], brow[:, :])
                for k in range(3):
                    v.drain()
                    nc.vector.tensor_copy(part[:, k, :], left[:, :])
                    v.drain()
                    nc.vector.tensor_tensor(left[:, :], left[:, :], part[:, k, :], ALU.subtract)
                v.drain().then_inc(split, 1)
                nc.vector.tensor_scalar(K["W3"][:, :], w3raw[:, :], 1.0 / H, None, ALU.mult)
                for src, dst in ((K["dst_i"], dstf), (prev_i, prevf), (next_i, nextf), (K["slot_i"], slotf)):
                    nc.vector.tensor_copy(dst[:, :], src[:, :])
                v.drain()
                nc.vector.tensor_reduce(K["W3m"][:, :], K["W3"][:, :].rearrange("p (h c) -> p c h", h=H), AX.X, ALU.add)
                for l in LAYERS:
                    w = {1: K["W1"], 2: K["W2"], 3: w3raw}[l]
                    n = P if l < 3 else H * P
                    for i, k in enumerate("sd"):
                        nc.vector.tensor_tensor(prod[:, 0:n], w[:, :], att[k, l][:, :], ALU.mult)
                        v.drain()
                        nc.vector.tensor_reduce(K[f"A{l}"][:, i * H:i * H + H],
                                                prod[:, 0:n].rearrange("p (h c) -> p h c", h=H), AX.X, ALU.add)
                        v.drain()
                first = dstf[:, 0:1]
                nc.vector.tensor_tensor(work[:, :], dstf[:, :], prevf[:, :], ALU.is_equal)
                nc.vector.tensor_tensor(K["goes_on"][:, :], dstf[:, :], nextf[:, :], ALU.is_equal)
                nc.vector.tensor_scalar(inhead[:, :], dstf[:, :], first, None, ALU.is_equal)
                v.drain()
                nc.vector.tensor_scalar(K["fresh"][:, :], work[:, :], -1.0, BIG, ALU.add, ALU.mult)
                nc.vector.tensor_scalar(K["joins"][:, :], work[:, 0:1], -1.0, BIG, ALU.add, ALU.mult)
                nc.vector.tensor_scalar(K["last"][:, :], K["goes_on"][:, :], -1.0, 1.0, ALU.mult, ALU.add)
                nc.vector.tensor_tensor(ends[:, 0:1], work[:, 0:1], inhead[:, COLS - 1:COLS], ALU.mult)
                nc.vector.tensor_tensor(ends[:, 1:2], K["goes_on"][:, COLS - 1:COLS],
                                        inhead[:, COLS - 1:COLS], ALU.mult)
                v.drain()
                nc.vector.memset(K["fresh"][:, 0:1], -BIG)
                nc.vector.tensor_tensor(K["headend"][:, :], K["last"][:, :], inhead[:, :], ALU.mult)
                nc.vector.tensor_scalar(ends[:, 2:3], ends[:, 0:1], -1.0, BIG, ALU.add, ALU.mult)
                nc.vector.tensor_scalar(ends[:, 3:4], ends[:, 1:2], FAR, None, ALU.mult)
                nc.vector.scalar_tensor_tensor(work[:, :], K["goes_on"][:, :], FAR, dstf[:, :], ALU.mult, ALU.add)
                v.drain()
                nc.vector.tensor_copy(K["scat_i"][:, :], work[:, :])
                nc.vector.tensor_copy(wide[:, :], ends[:, 2:3].to_broadcast([P, P]))
                nc.vector.tensor_tensor(prevf[:, :], K["headend"][:, :], slotf[:, :], ALU.mult)
                nc.vector.tensor_tensor(nextf[:, 0:1], dstf[:, 0:1], ends[:, 3:4], ALU.add)
                v.drain()
                nc.vector.tensor_reduce(work[:, 0:1], prevf[:, :], AX.X, ALU.add)
                nc.vector.tensor_copy(K["head_out_i"][:, :], nextf[:, 0:1])
                v.drain().then_inc(built, 1)
                nc.vector.tensor_scalar(work[:, 1:2], work[:, 0:1], float(NP), float(NP), ALU.max, ALU.subtract)
                nc.vector.tensor_scalar(work[:, 3:4], work[:, 0:1], float(NP), None, ALU.max)
                nc.vector.tensor_scalar(K["not_headend"][:, :], K["headend"][:, :], -1.0, 1.0, ALU.mult, ALU.add)
                nc.vector.tensor_tensor(work[:, 2:3], work[:, 0:1], ends[:, 3:4], ALU.add)
                v.drain()
                nc.vector.tensor_copy(K["head_slot_i"][:, :], work[:, 1:2])
                nc.vector.tensor_copy(K["head_row_i"][:, :], work[:, 2:3])
                nc.vector.tensor_copy(K["head_read_i"][:, :], work[:, 3:4])
                v.wait_ge(turned, 1)
                nc.vector.tensor_copy(K["chain"][:, :], ps[:, 0:P])

            @block.tensor
            def _(pe):
                pe.wait_ge(built, 1)
                nc.tensor.transpose(ps[:, 0:P], wide[:, :], K["ident"][:, :]).then_inc(turned, 1)

        clear_semaphores(nc, used)


def look_up_dst(nc, K, T):
    with ExitStack() as ctx:
        work = ctx.enter_context(nc.sbuf_tensor("l_work", [P, COLS], FP32))
        slotf = ctx.enter_context(nc.sbuf_tensor("l_slot", [P, COLS], FP32))
        with nc.Block() as block:
            @block.vector
            def _(v):
                nc.vector.tensor_copy(K["tail"][:, :], K["tail_row_i"][:, :])
                nc.vector.tensor_copy(slotf[:, :], K["slot_i"][:, :])
                v.drain()
                nc.vector.tensor_tensor(work[:, :], slotf[:, :], K["last"][:, :], ALU.mult)
                v.drain()
                nc.vector.tensor_tensor_scan(slotf[:, ::-1], K["goes_on"][:, ::-1], work[:, ::-1],
                                             K["tail"][:, :], ALU.mult, ALU.add)
                v.drain()
                nc.vector.tensor_copy(K["gdst_i"][:, :], slotf[:, :])


def add_bias(nc, K, bank, name):
    nc.tensor.matmul(bank[:, :], K["ones"][:, :], K["parts"][:, BIASES.index(name), :, :].rearrange("p t c -> p (t c)"),
                     start=True, stop=False)


def layer_norm_moments(nc, v, y, stats, aggr, n):
    for t in range(n):
        nc.vector.bn_stats(stats[:, t, :], y[:, t, :])
    v.drain()
    for t in range(n):
        nc.vector.bn_aggr(aggr[:, t, :], stats[:, t, :])
    v.drain()


def layer_norm_apply(nc, v, y, y_out, aggr, rstd, n):
    nc.vector.reciprocal(rstd[:, 1, 0:n], rstd[:, 0, 0:n])
    v.drain()
    for t in range(n):
        ins = nc.vector.tensor_scalar(y_out[:, t, :], y[:, t, :], aggr[:, t, 0:1], rstd[:, 1, t:t + 1],
                                      ALU.subtract, ALU.mult)
    return ins


def over_tiles(ap, n=G):
    return ap.unsqueeze(1).to_broadcast([P, n, ap.shape[-1]])


def dense(nc, A, K, T, out):
    with ExitStack() as ctx:
        def sb(name, shape, dt=FP32):
            return ctx.enter_context(nc.sbuf_tensor(name, shape, dt))

        used = []

        def sem(name):
            used.append(ctx.enter_context(nc.semaphore(name)))
            return used[-1]

        L = range(DLANES)
        x = [sb(f"d_x{i}", [P, G, P]) for i in L]
        fa = [sb(f"d_fa{i}", [P, G * P]) for i in L]
        fb = [sb(f"d_fb{i}", [P, G * P]) for i in L]
        r2 = [sb(f"d_r2{i}", [P, G, ROW]) for i in L]
        r3 = [sb(f"d_r3{i}", [P, G, ROW]) for i in L]
        y = [sb(f"d_y{i}", [P, G, P]) for i in L]
        x1 = [sb(f"d_x1{i}", [P, G, P]) for i in L]
        fin = [sb(f"d_fin{i}", [P, G, P]) for i in L]
        stats = [sb(f"d_stats{i}", [P, G, 6]) for i in L]
        aggr = [sb(f"d_aggr{i}", [P, G, 2]) for i in L]
        rstd = [sb(f"d_rstd{i}", [P, 2, G]) for i in L]
        pa = [ctx.enter_context(nc.psum_tensor(f"d_pa{i}", [P, G * P], FP32)) for i in L]
        pb = [ctx.enter_context(nc.psum_tensor(f"d_pb{i}", [P, G * P], FP32)) for i in L]
        x_in = [sem(f"d_x_in{i}") for i in L]
        r2_done = sem("d_r2_done")
        stored = [sem(f"d_stored{i}") for i in L]
        fin_stored = [sem(f"d_fin_stored{i}") for i in L]
        rows_free = sem("d_rows_free")
        fin_free = sem("d_fin_free")
        tick, sp_tick = sem("d_tick"), sem("d_sp_tick")
        pe_s = [sem(f"d_pe{k}") for k in range(8)]
        ev = [sem(f"d_ev{k}") for k in range(8)]
        h2_done, var1, root1, x1_done, var2, root2, fin_done = (
            sem("d_" + s) for s in ("h2_done", "var1", "root1", "x1_done", "var2", "root2", "fin_done"))
        rounds = NG // DLANES
        to = [sb(f"map_to{b}", [P, MG], I32) for b in range(2)]
        val = [sb(f"map_val{b}", [P, MG], I32) for b in range(2)]
        tail_to = sb("map_tail_to", [P, 1], I32)
        staged, kept = sem("m_staged"), sem("m_kept")
        sent, fetched = ([K["dma_sem"](f"m_{s}{b}") for b in range(2)] for s in ("sent", "fetched"))
        tailed = K["dma_sem"]("m_tailed")
        groups = COLS // MG
        assert groups % 2 == 1

        def scatter(g, b, col, stage_no):
            nc.gpsimd.tensor_copy(to[b][:, :], K["scat_i"][:, col]).then_inc(staged, 1)
            nc.gpsimd.tensor_copy(val[b][:, :], K["slot_i"][:, col]).then_inc(staged, 1)
            g.wait_ge(staged, stage_no)
            g.sem_inc(tick, 1)
            for t in range(MG):
                g.indirect_dma_start(T["map"][:, :], bass.IndirectOffsetOnAxis(ap=to[b][:, t:t + 1], axis=0),
                                     val[b][:, t:t + 1], None, bounds_check=NP - 1,
                                     oob_is_err=False).then_inc(sent[b], 16)

        def gather(g, b, col, stage_no):
            nc.gpsimd.tensor_copy(to[b][:, :], K["src_i"][:, col]).then_inc(staged, 1)
            g.wait_ge(staged, stage_no)
            g.sem_inc(tick, 1)
            for t in range(MG):
                g.indirect_dma_start(val[b][:, t:t + 1], None, T["map"][:, :],
                                     bass.IndirectOffsetOnAxis(ap=to[b][:, t:t + 1], axis=0)).then_inc(fetched[b], 16)

        rows = [t.rearrange("(g p t) c -> g p (t c)", p=P, t=G)
                for t in (A["x"], T[2][0:NP, :], T[3][0:NP, :], T[4][0:NP, :], out)]
        flat = lambda ap: ap.rearrange("p t c -> p (t c)")
        stores = 3
        pairs = (tuple(L)[:DLANES // 2], tuple(L)[DLANES // 2:])

        def run(stage, lanes, round_no):
            if round_no is not None:
                for i in lanes:
                    stage(i, round_no, round_no * DLANES + i + 1)

        def walk(engine, half):
            one, two = pairs
            half(one, 0, two, None, None)
            half(two, 0, one, 0, None)
            with engine.Fori(1, rounds) as it:
                half(one, it, two, it - 1, it - 1)
                half(two, it, one, it, it - 1)
            half(one, None, two, rounds - 1, rounds - 1)
            half(two, None, one, None, rounds - 1)

        with nc.Block() as block:
            @block.gpsimd
            def _(g):
                with g.Fori(0, groups // 2) as it:
                    for b in range(2):
                        scatter(g, b, bass.ds((it * 2 + b) * MG, MG), it * 4 + 2 * b + 2)
                    for b in range(2):
                        g.wait_ge(sent[b], (it + 1) * (16 * MG))
                        g.sem_inc(tick, 1)
                pairs_of_groups = groups // 2
                scatter(g, 0, slice(COLS - MG, COLS), pairs_of_groups * 4 + 2)
                g.wait_ge(sent[0], (pairs_of_groups + 1) * 16 * MG)
                n0 = pairs_of_groups * 4 + 2
                with g.Fori(0, pairs_of_groups) as it:
                    for b in range(2):
                        gather(g, b, bass.ds((it * 2 + b) * MG, MG), it * 4 + 2 * b + (n0 + 1))
                        g.wait_ge(fetched[b], (it + 1) * (16 * MG))
                        g.sem_inc(tick, 1)
                        nc.gpsimd.tensor_copy(K["gsrc_i"][:, bass.ds((it * 2 + b) * MG, MG)], val[b][:, :]).then_inc(staged, 1)
                        g.wait_ge(staged, it * 4 + 2 * b + (n0 + 2))
                        g.sem_inc(tick, 1)
                gather(g, 0, slice(COLS - MG, COLS), n0 + 4 * pairs_of_groups + 1)
                g.wait_ge(fetched[0], (pairs_of_groups + 1) * 16 * MG)
                nc.gpsimd.tensor_copy(K["gsrc_i"][:, COLS - MG:COLS], val[0][:, :]).then_inc(staged, 1)
                nc.gpsimd.tensor_copy(tail_to[:, :], K["dst_i"][:, COLS - 1:COLS]).then_inc(kept, 1)
                g.wait_ge(kept, 1)
                g.indirect_dma_start(K["tail_row_i"][:, :], None, T["map"][:, :],
                                     bass.IndirectOffsetOnAxis(ap=tail_to[:, :], axis=0)).then_inc(tailed, 16)
                g.wait_ge(tailed, 16)

            @block.sync
            def _(sp):
                def load(i, group):
                    sp.dma_start(flat(x[i][:, :, :]), rows[0][bass.ds(group, 1), :, :].rearrange("a p c -> (a p) c")).then_inc(x_in[i], 16)

                def put(k, tile, i, round_no, done):
                    sp.dma_start(rows[k][bass.ds(round_no * DLANES + i, 1), :, :].rearrange("a p c -> (a p) c"),
                                 flat(tile[i][:, :, :])).then_inc(done[i], 16)

                def free_rows(i, it, n):
                    sp.wait_ge(stored[i], it * (16 * stores))
                    sp.sem_inc(rows_free, 1)

                def put_x1(i, it, n):
                    sp.wait_ge(x1_done, n)
                    sp.sem_inc(sp_tick, 1)
                    put(3, x1, i, it, stored)

                def put_fin(i, it, n):
                    sp.wait_ge(fin_done, n)
                    sp.sem_inc(sp_tick, 1)
                    put(4, fin, i, it, fin_stored)

                def put_r2(i, it, n):
                    sp.wait_ge(r2_done, n)
                    sp.sem_inc(sp_tick, 1)
                    sp.wait_ge(ev[2], n)
                    sp.sem_inc(sp_tick, 1)
                    put(1, r2, i, it, stored)

                def put_r3(i, it, n):
                    sp.wait_ge(ev[4], n)
                    sp.sem_inc(sp_tick, 1)
                    put(2, r3, i, it, stored)
                    load(i, (it + 1) * DLANES + i)

                def free_fin(i, it, n):
                    sp.wait_ge(fin_stored[i], (it + 1) * 16)
                    sp.sem_inc(fin_free, 1)

                def half(front, f, back, b, p):
                    if p is not None:
                        run(free_rows, front, f)
                    run(put_x1, back, b)
                    run(put_fin, front, p)
                    run(put_r2, front, f)
                    run(put_r3, front, f)
                    run(free_fin, front, p)

                sp.sem_inc(rows_free, DLANES)
                sp.sem_inc(fin_free, DLANES)
                for i in L:
                    load(i, i)
                walk(sp, half)
                for i in L:
                    sp.wait_ge(stored[i], rounds * 16 * stores)
                    sp.wait_ge(x_in[i], (rounds + 1) * 16)

            @block.tensor
            def _(pe):

                def turn_x(i, it, n):
                    pe.wait_ge(x_in[i], (it + 1) * 16)
                    pe.wait_ge(ev[7], n)
                    for t in range(G):
                        ins = nc.tensor.transpose(pa[i][:, t * P:(t + 1) * P], x[i][:, t, :], K["ident"][:, :])
                    ins.then_inc(pe_s[0], 1)

                def times_w1(i, it, n):
                    pe.wait_ge(ev[0], n)
                    nc.tensor.matmul(pb[i][:, :], K["W1"][:, :], fa[i][:, :], start=True, stop=True).then_inc(pe_s[1], 1)

                def times_w2(i, it, n):
                    pe.wait_ge(ev[1], n)
                    add_bias(nc, K, pa[i], "b2")
                    for t in range(G):
                        h = fb[i][:, t * P:(t + 1) * P]
                        nc.tensor.matmul(pa[i][:, t * P:(t + 1) * P], h, K["W2"][:, :], start=False, stop=(t == G - 1))
                        ins = nc.tensor.matmul(pb[i][:, t * 2 * H:(t + 1) * 2 * H], h, K["A2"][:, :], start=True, stop=True)
                    ins.then_inc(pe_s[2], 1)

                def turn_h2(i, it, n):
                    pe.wait_ge(h2_done, n)
                    pe.wait_ge(ev[2], n)
                    for t in range(G):
                        ins = nc.tensor.transpose(pb[i][:, t * P:(t + 1) * P], r3[i][:, t, 0:P], K["ident"][:, :])
                    ins.then_inc(pe_s[3], 1)

                def times_w3(i, it, n):
                    pe.wait_ge(ev[3], n)
                    pe.wait_ge(r2_done, n)
                    add_bias(nc, K, pa[i], "b3")
                    for t in range(G):
                        h = fa[i][:, t * P:(t + 1) * P]
                        nc.tensor.matmul(pa[i][:, t * P:(t + 1) * P], h, K["W3m"][:, :], start=False, stop=(t == G - 1))
                        ins = nc.tensor.matmul(pb[i][:, t * 2 * H:(t + 1) * 2 * H], h, K["A3"][:, :], start=True, stop=True)
                    ins.then_inc(pe_s[4], 1)

                def turn_x1(i, it, n):
                    pe.wait_ge(x1_done, n)
                    for t in range(G):
                        ins = nc.tensor.transpose(pa[i][:, t * P:(t + 1) * P], x1[i][:, t, :], K["ident"][:, :])
                    ins.then_inc(pe_s[5], 1)

                def times_u1(i, it, n):
                    pe.wait_ge(ev[5], n)
                    nc.tensor.matmul(pb[i][:, :], K["U1a"][:, :], fb[i][:, :], start=True, stop=True).then_inc(pe_s[6], 1)

                def times_u2(i, it, n):
                    pe.wait_ge(ev[6], n)
                    add_bias(nc, K, pa[i], "c2")
                    for t in range(G):
                        ins = nc.tensor.matmul(pa[i][:, t * P:(t + 1) * P], fa[i][:, t * P:(t + 1) * P], K["U2"][:, :],
                                               start=False, stop=(t == G - 1))
                    ins.then_inc(pe_s[7], 1)

                def half(front, f, back, b, p):
                    run(turn_x, front, f)
                    run(times_w1, front, f)
                    run(times_w2, front, f)
                    run(turn_h2, front, f)
                    run(turn_x1, back, b)
                    run(times_w3, front, f)
                    run(times_u1, back, b)
                    run(times_u2, back, b)

                walk(pe, half)

            @block.scalar
            def _(act):

                def take_x(i, it, n):
                    act.wait_ge(pe_s[0], n)
                    nc.scalar.activation(fa[i][:, :], pa[i][:, :], ACT.Copy).then_inc(ev[0], 1)

                def take_h1(i, it, n):
                    act.wait_ge(pe_s[1], n)
                    nc.scalar.activation(fb[i][:, :], pb[i][:, :], ACT.Relu, bias=K["b1"][:, :]).then_inc(ev[1], 1)

                def relu_h2(i, it, n):
                    act.wait_ge(rows_free, n)
                    act.wait_ge(pe_s[2], n)
                    psum = pa[i][:, :].rearrange("p (t c) -> p t c", t=G)
                    nc.scalar.activation(r3[i][:, :, 0:P], psum, ACT.Relu).then_inc(h2_done, 1)
                    nc.scalar.activation(r2[i][:, :, P:ROW], pb[i][:, 0:G * 2 * H].rearrange("p (t c) -> p t c", t=G), ACT.Copy).then_inc(ev[2], 1)
                    nc.scalar.activation(r2[i][:, :, 0:P], psum, ACT.Copy).then_inc(r2_done, 1)

                def take_h2(i, it, n):
                    act.wait_ge(pe_s[3], n)
                    nc.scalar.activation(fa[i][:, :], pb[i][:, :], ACT.Copy).then_inc(ev[3], 1)

                def take_root1(i, it, n):
                    act.wait_ge(var1, n)
                    nc.scalar.activation(rstd[i][:, 0, :], aggr[i][:, :, 1], ACT.Sqrt, bias=K["eps"][:, :]).then_inc(root1, 1)

                def take_root2(i, it, n):
                    act.wait_ge(var2, n)
                    nc.scalar.activation(rstd[i][:, 0, :], aggr[i][:, :, 1], ACT.Sqrt, bias=K["eps"][:, :]).then_inc(root2, 1)

                def take_x1(i, it, n):
                    act.wait_ge(pe_s[5], n)
                    nc.scalar.activation(fb[i][:, :], pa[i][:, :], ACT.Copy).then_inc(ev[5], 1)

                def take_u(i, it, n):
                    act.wait_ge(pe_s[6], n)
                    nc.scalar.activation(fa[i][:, :], pb[i][:, :], ACT.Relu, bias=K["c1"][:, :]).then_inc(ev[6], 1)

                def half(front, f, back, b, p):
                    run(take_x, front, f)
                    run(take_h1, front, f)
                    run(take_root1, back, b)
                    run(relu_h2, front, f)
                    run(take_root2, front, p)
                    run(take_h2, front, f)
                    run(take_x1, back, b)
                    run(take_u, back, b)

                walk(act, half)

            @block.vector
            def _(v):
                def add_x(i, it, n):
                    v.wait_ge(pe_s[4], n)
                    nc.vector.tensor_copy(r3[i][:, :, P:ROW], pb[i][:, 0:G * 2 * H].rearrange("p (t c) -> p t c", t=G))
                    nc.vector.tensor_tensor(y[i][:, :, :], pa[i][:, :].rearrange("p (t c) -> p t c", t=G), x[i][:, :, :], ALU.add)
                    v.drain().then_inc(ev[4], 1)

                def moments1(i, it, n):
                    layer_norm_moments(nc, v, y[i], stats[i], aggr[i], G)
                    v.sem_inc(var1, 1)

                def norm1(i, it, n):
                    v.wait_ge(root1, n)
                    layer_norm_apply(nc, v, y[i], x1[i], aggr[i], rstd[i], G)
                    v.drain().then_inc(x1_done, 1)

                def add_x1(i, it, n):
                    v.wait_ge(pe_s[7], n)
                    nc.vector.tensor_tensor(y[i][:, :, :], pa[i][:, :].rearrange("p (t c) -> p t c", t=G), x1[i][:, :, :], ALU.add)
                    v.drain().then_inc(ev[7], 1)

                def moments2(i, it, n):
                    layer_norm_moments(nc, v, y[i], stats[i], aggr[i], G)
                    v.sem_inc(var2, 1)

                def norm2(i, it, n):
                    v.wait_ge(fin_free, n)
                    v.wait_ge(root2, n)
                    layer_norm_apply(nc, v, y[i], fin[i], aggr[i], rstd[i], G)
                    v.drain().then_inc(fin_done, 1)

                def half(front, f, back, b, p):
                    run(norm1, back, b)
                    run(norm2, front, p)
                    run(add_x, front, f)
                    run(add_x1, back, b)
                    run(moments1, front, f)
                    run(moments2, back, b)

                v.sem_inc(ev[7], DLANES)
                walk(v, half)

        clear_semaphores(nc, used)


def attend(nc, A, K, T, layer):
    wd, nacc = WIDE[layer], ACC[layer]
    sw = STATE[layer]
    lanes = range(2)
    with ExitStack() as ctx:
        def name_of(name):
            return f"a{layer}_{name}"

        def sb(name, shape, dt=FP32):
            return ctx.enter_context(nc.sbuf_tensor(name_of(name), shape, dt))

        used = []

        def sem(name):
            used.append(ctx.enter_context(nc.semaphore(name_of(name))))
            return used[-1]

        def bank(name):
            return ctx.enter_context(nc.psum_tensor(name_of(name), [P, G * P], FP32))

        in_w = P if layer == 1 else ROW
        out_w = P if layer == 3 else ROW
        R = 2 * G
        part = [slice(b * G, (b + 1) * G) for b in lanes]
        S, D = sb("src", [P, R, in_w]), sb("dst", [P, R, in_w])
        if layer == 2:
            S2 = sb("src_taken", [P, R, in_w])
        else:
            S2 = S
        idx = [sb(f"idx{b}", [P, G], I32) for b in lanes]
        idd = [sb(f"idd{b}", [P, G], I32) for b in lanes]
        fresh = sb("fresh", [P, H, R + 1])
        q = sb("q", [P, H, R + 1])
        m = sb("m", [P, H, R + 1])
        if layer < 3:
            w0 = sb("w0", [P, H, wd + 1, R + 1])
            sums_of = sb("sums", [P, H, wd + 1, R + 1])
        st = sb("st", [P, R + 1, sw])
        lg = sb("lg", [P, 2, R, H])
        lr = sb("lr", [P, 2, R, H])
        dd = sb("dd", [P, 3, R, H])
        wt = sb("wt", [P, 3, R, H])
        msg = sb("msg", [P, R, H, wd + 1] if layer == 3 else [P, H, wd + 1, R + 1])
        den = sb("den", [P, 2, R, H])
        o = sb("o", [P, R, H, wd])
        if layer == 1:
            hf = sb("hf", [P, R, P])
        r = sb("r", [P, R, out_w])
        pm = [[bank(f"p{b}{k}") for k in range(4)] for b in lanes]
        arrived = [K["dma_sem"](name_of(f"arrived{b}")) for b in lanes]
        s_free, d_free, d_in = sem("s_free"), sem("d_free"), sem("d_in")
        tick, sp_tick, staged = sem("tick"), sem("sp_tick"), sem("staged")
        f1, expd, f2, o_done, h_done = (sem(s) for s in ("f1", "expd", "f2", "o_done", "h_done"))
        turned_h, took_h, times, rows_done = (sem(s) for s in ("turned_h", "took_h", "times", "rows_done"))
        st_stored, r_stored, st_free, r_free = (sem(s) for s in ("st_stored", "r_stored", "st_free", "r_free"))
        if layer == 1:
            fT = [sb(f"fT{b}", [P, 2, G * P]) for b in lanes]
            al = sb("al", [P, 2, R, 2 * H])
            xd_stored = [sem(f"xd_stored{b}") for b in lanes]
            turned, took, proj, took_al, took_r = (
                sem(s) for s in ("turned", "took", "proj", "took_al", "took_r"))
            proj_taken, src_used = sem("proj_taken"), sem("src_used")
            sproj = sb("sproj", [P, R, P])
        if layer < 3:
            hT = [sb(f"hT{b}", [P, G * P]) for b in lanes]
            s2_free = sem("s2_free")
            spread, st_done = sem("spread"), sem("st_done")
        else:
            zT = [sb(f"zT{b}", [P, H, G * P]) for b in lanes]
            xr = sb("xr", [P, R, P])
            stats = sb("stats", [P, R, 6])
            aggr = sb("aggr", [P, R, 2])
            rstd = sb("rstd", [P, 2, R])
            y = sb("y", [P, R, P])
            wself = sb("wself", [P, R, H])
            xr_in, var, root, weighted, summed, y_done = (
                sem(s) for s in ("xr_in", "var", "root", "weighted", "summed", "y_done"))

        iters = COLS // R
        slots = lambda ap: ap.rearrange("(p j) c -> p j c", p=P)
        st_rows = slots(T["st", layer])
        next_rows = slots(T[layer + 1][NP:NP + EP, :])
        xd_rows = slots(T["xd"])

        def cols(it, b):
            return bass.ds((it * 2 + b) * G, G)

        def round_cols(it):
            return bass.ds(it * R, R)

        def by_head(ap):
            return ap.rearrange("p r h -> p h r")

        per_group = 2 * G if layer == 1 else G
        logit_at = 256
        tT = [pm[b][3] if layer == 1 else pm[b][2] for b in lanes]

        with nc.Block() as block:
            @block.gpsimd
            def _(g):
                def gather(it, b):
                    n = it * 2 + b + 1
                    if layer < 3:
                        g.wait_ge(s_free, n)
                        g.sem_inc(tick, 1)
                    if layer == 1:
                        nc.gpsimd.tensor_copy(idx[b][:, :], K["src_i"][:, cols(it, b)]).then_inc(staged, 1)
                        nc.gpsimd.tensor_copy(idd[b][:, :], K["dst_i"][:, cols(it, b)]).then_inc(staged, 1)
                        g.wait_ge(staged, it * 4 + 2 * b + 2)
                    else:
                        nc.gpsimd.tensor_copy(idx[b][:, :], K["gsrc_i"][:, cols(it, b)]).then_inc(staged, 1)
                        g.wait_ge(staged, n)
                    g.sem_inc(tick, 1)
                    for t in range(G):
                        pairs = ((S, idx, A["x"]), (D, idd, A["x"])) if layer == 1 else ((S, idx, T[layer]),)
                        for rows, at, table in pairs:
                            g.indirect_dma_start(rows[:, b * G + t, :], None, table[:, :],
                                                 bass.IndirectOffsetOnAxis(ap=at[b][:, t:t + 1], axis=0)).then_inc(arrived[b], 16)

                def weigh(it, b):
                    g.wait_ge(expd, it + 1)
                    g.sem_inc(tick, 1)
                    for t in range(b * G, (b + 1) * G):
                        ins = nc.gpsimd.tensor_tensor(msg[:, t, :, 0:P], S[:, t, 0:P].unsqueeze(1).to_broadcast([P, H, P]),
                                                      wt[:, 1, t, :].unsqueeze(2).to_broadcast([P, H, P]), ALU.mult)
                    ins.then_inc(weighted, 1)

                if layer < 3:
                    with g.Fori(0, iters) as it:
                        for b in lanes:
                            gather(it, b)
                else:
                    for b in lanes:
                        gather(0, b)
                    with g.Fori(1, iters) as it:
                        for b in lanes:
                            weigh(it - 1, b)
                            g.wait_ge(weighted, it * 2 + b - 1)
                            g.sem_inc(tick, 1)
                            gather(it, b)
                    for b in lanes:
                        weigh(iters - 1, b)

            @block.sync
            def _(sp):
                def inputs(it):
                    if layer > 1:
                        sp.wait_ge(d_free, it + 1)
                        sp.sem_inc(sp_tick, 1)
                        sp.dma_start(D[:, :, :], slots(T[layer][NP:NP + EP, :])[:, round_cols(it), :]).then_inc(d_in, 16)
                        return
                    for b in lanes:
                        sp.wait_ge(arrived[b], (it + 1) * (16 * per_group))
                        sp.sem_inc(sp_tick, 1)
                        sp.dma_start(xd_rows[:, cols(it, b), :], D[:, part[b], :]).then_inc(xd_stored[b], 16)
                        sp.wait_ge(xd_stored[b], (it + 1) * 16)
                        sp.sem_inc(sp_tick, 1)
                        sp.wait_ge(took, it * 2 + b + 1)
                        sp.sem_inc(s_free, 1)

                def residual_rows(it):
                    sp.dma_start(xr[:, :, :], xd_rows[:, round_cols(it), :]).then_inc(xr_in, 16)

                def store_rows(it):
                    sp.wait_ge(rows_done, it + 1)
                    sp.sem_inc(sp_tick, 1)
                    if layer == 1:
                        sp.wait_ge(took_r, it * 2 + 2)
                        sp.sem_inc(sp_tick, 1)
                    sp.dma_start(next_rows[:, round_cols(it), :], r[:, :, :]).then_inc(r_stored, 16)

                def store_states(it):
                    sp.wait_ge(st_done if layer < 3 else f2, it + 1)
                    sp.sem_inc(sp_tick, 1)
                    sp.dma_start(st_rows[:, round_cols(it), :], st[:, 1:R + 1, :]).then_inc(st_stored, 16)

                def free_rows(it):
                    sp.wait_ge(r_stored, (it + 1) * 16)
                    sp.sem_inc(r_free, 1)

                def free_states(it):
                    sp.wait_ge(st_stored, (it + 1) * 16)
                    sp.sem_inc(st_free, 1)

                sp.sem_inc(st_free, 1)
                sp.sem_inc(r_free, 1)
                if layer == 1:
                    sp.sem_inc(s_free, 2)
                inputs(0)
                if layer < 3:
                    inputs(1)
                    store_states(0)
                    free_states(0)
                    with sp.Fori(1, iters - 1) as it:
                        store_rows(it - 1)
                        free_rows(it - 1)
                        inputs(it + 1)
                        store_states(it)
                        free_states(it)
                    store_rows(iters - 2)
                    free_rows(iters - 2)
                    store_states(iters - 1)
                    free_states(iters - 1)
                else:
                    residual_rows(0)
                    store_states(0)
                    free_states(0)
                    inputs(1)
                    store_states(1)
                    free_states(1)
                    with sp.Fori(2, iters) as it:
                        inputs(it)
                        store_states(it)
                        store_rows(it - 2)
                        residual_rows(it - 1)
                        free_rows(it - 2)
                        free_states(it)
                    store_rows(iters - 2)
                    residual_rows(iters - 1)
                    free_rows(iters - 2)
                store_rows(iters - 1)
                free_rows(iters - 1)

            @block.tensor
            def _(pe):
                def turn_in(it, b):
                    pe.wait_ge(arrived[b], (it + 1) * (16 * per_group))
                    pe.wait_ge(proj_taken, it * 2 + b + 1)
                    for k, rows in enumerate((S, D)):
                        for t in range(G):
                            ins = nc.tensor.transpose(pm[b][k][:, t * P:(t + 1) * P], rows[:, b * G + t, :], K["ident"][:, :])
                    ins.then_inc(turned, 1)

                def project(it, b):
                    pe.wait_ge(took, it * 2 + b + 1)
                    for k in range(2):
                        add_bias(nc, K, pm[b][k], "b1")
                        for t in range(G):
                            f = fT[b][:, k, t * P:(t + 1) * P]
                            nc.tensor.matmul(pm[b][k][:, t * P:(t + 1) * P], f, K["W1"][:, :], start=False, stop=(t == G - 1))
                            at = (k * G + t) * 2 * H
                            ins = nc.tensor.matmul(pm[b][2][:, at:at + 2 * H], f, K["A1"][:, :], start=True, stop=True)
                    ins.then_inc(proj, 1)

                def turn_out(it, b):
                    n = it * 2 + b + 1
                    if layer < 3:
                        pe.wait_ge(h_done, n)
                        for t in range(G):
                            h = (hf if layer == 1 else r)[:, b * G + t, 0:P]
                            ins = nc.tensor.transpose(tT[b][:, t * P:(t + 1) * P], h, K["ident"][:, :])
                    else:
                        pe.wait_ge(o_done, n)
                        pe.wait_ge(y_done, n)
                        for h in range(H):
                            for t in range(G):
                                ins = nc.tensor.transpose(pm[b][h][:, t * P:(t + 1) * P], o[:, b * G + t, h, :], K["ident"][:, :])
                    ins.then_inc(turned_h, 1)

                def multiply(it, b):
                    n = it * 2 + b + 1
                    pe.wait_ge(took_h, n)
                    if layer == 3:
                        add_bias(nc, K, pm[b][0], "b3")
                        for t in range(G):
                            for h in range(H):
                                ins = nc.tensor.matmul(pm[b][0][:, t * P:(t + 1) * P], zT[b][:, h, t * P:(t + 1) * P],
                                                       K["W3"][:, h * P:(h + 1) * P], start=False,
                                                       stop=(t == G - 1 and h == H - 1))
                    else:
                        if layer == 1:
                            add_bias(nc, K, tT[b], "b2")
                        for t in range(G):
                            h = hT[b][:, t * P:(t + 1) * P]
                            if layer == 1:
                                nc.tensor.matmul(tT[b][:, t * P:(t + 1) * P], h, K["W2"][:, :], start=False, stop=(t == G - 1))
                            at = logit_at + t * 2 * H
                            ins = nc.tensor.matmul(pm[b][2][:, at:at + 2 * H], h, K[f"A{layer + 1}"][:, :], start=True, stop=True)
                    ins.then_inc(times, 1)

                def both(stage, it):
                    for b in lanes:
                        stage(it, b)

                if layer == 1:
                    both(turn_in, 0)
                    both(project, 0)
                with pe.Fori(1, iters) as it:
                    if layer == 1:
                        both(turn_in, it)
                    both(turn_out, it - 1)
                    if layer == 1:
                        both(project, it)
                        pe.wait_ge(took_al, it * 2 + 2)
                    both(multiply, it - 1)
                both(turn_out, iters - 1)
                both(multiply, iters - 1)

            @block.scalar
            def _(act):
                def take_in(it, b):
                    act.wait_ge(turned, it * 2 + b + 1)
                    for k in range(2):
                        ins = nc.scalar.activation(fT[b][:, k, :], pm[b][k][:, :], ACT.Copy)
                    ins.then_inc(took, 1)

                def take_gathered(it, b):
                    act.wait_ge(s2_free, it + 1)
                    act.wait_ge(arrived[b], (it + 1) * (16 * per_group))
                    nc.scalar.activation(S2[:, part[b], :], S[:, part[b], :], ACT.Copy).then_inc(s_free, 1)

                def take_projections(it, b):
                    n = it * 2 + b + 1
                    act.wait_ge(proj, n)
                    nc.scalar.activation(al[:, :, part[b], :], pm[b][2][:, 0:2 * G * 2 * H].rearrange("p (k t c) -> p k t c", k=2, t=G),
                                         ACT.Copy).then_inc(took_al, 1)

                def take_own(it, b):
                    act.wait_ge(src_used, it + 1)
                    nc.scalar.activation(sproj[:, part[b], :], pm[b][0][:, :].rearrange("p (t c) -> p t c", t=G), ACT.Copy)
                    act.wait_ge(st_free, it + 1)
                    nc.scalar.activation(st[:, 1 + b * G:1 + (b + 1) * G, sw - P:sw], pm[b][1][:, :].rearrange("p (t c) -> p t c", t=G),
                                         ACT.Copy).then_inc(proj_taken, 1)

                def exponentials(it):
                    act.wait_ge(f1, it + 1)
                    nc.scalar.activation(wt[:, :, :, :].rearrange("p k t h -> p (k t h)"),
                                         dd[:, :, :, :].rearrange("p k t h -> p (k t h)"), ACT.Exp).then_inc(expd, 1)

                def spread_factors(it):
                    act.wait_ge(f1, it + 1)
                    for h in range(H):
                        ins = nc.scalar.activation(w0[:, h, :, 1:R + 1], dd[:, 0, :, h].unsqueeze(1).to_broadcast([P, wd + 1, R]), ACT.Exp)
                    ins.then_inc(spread, 1)

                def take_sums(it):
                    act.wait_ge(f2, it + 1)
                    nc.scalar.activation(st[:, 1:R + 1, 0:nacc], sums_of[:, :, :, 1:R + 1].rearrange("p h c t -> p t (h c)"),
                                         ACT.Copy).then_inc(st_done, 1)

                def finish(it, b):
                    if layer == 1:
                        act.wait_ge(o_done, it + 1)
                        nc.scalar.activation(hf[:, part[b], :].rearrange("p t c -> p (t c)"),
                                             o[:, part[b], :, :].rearrange("p t h c -> p (t h c)"), ACT.Relu).then_inc(h_done, 1)
                    elif layer == 2:
                        act.wait_ge(r_free, it + 1)
                        act.wait_ge(o_done, it + 1)
                        nc.scalar.activation(r[:, part[b], 0:P], o[:, part[b], :, :].rearrange("p t h c -> p t (h c)"), ACT.Relu).then_inc(h_done, 1)
                    else:
                        act.wait_ge(summed, it * 2 + b + 1)
                        for t in range(b * G, (b + 1) * G):
                            for h in range(H):
                                ins = nc.scalar.activation(o[:, t, h, :], o[:, t, h, :], ACT.Copy, scale=den[:, 1, t, h:h + 1])
                        ins.then_inc(o_done, 1)

                def take_out(it, b):
                    act.wait_ge(turned_h, it * 2 + b + 1)
                    if layer < 3:
                        nc.scalar.activation(hT[b][:, :], tT[b][:, :], ACT.Copy).then_inc(took_h, 1)
                    else:
                        for h in range(H):
                            ins = nc.scalar.activation(zT[b][:, h, :], pm[b][h][:, :], ACT.Copy)
                        ins.then_inc(took_h, 1)

                def take_rows(it, b):
                    act.wait_ge(r_free, it + 1)
                    act.wait_ge(times, it * 2 + b + 1)
                    nc.scalar.activation(r[:, part[b], 0:P], tT[b][:, :].rearrange("p (t c) -> p t c", t=G), ACT.Copy).then_inc(took_r, 1)

                def roots(it):
                    act.wait_ge(var, it + 1)
                    nc.scalar.activation(rstd[:, 0, :], aggr[:, :, 1], ACT.Sqrt, bias=K["eps"][:, :]).then_inc(root, 1)

                def both(stage, it):
                    for b in lanes:
                        stage(it, b)

                if layer == 1:
                    both(take_in, 0)
                    both(take_projections, 0)
                    both(take_own, 0)
                    exponentials(0)
                    spread_factors(0)
                    take_in(1, 0)
                    both(finish, 0)
                    take_sums(0)
                    take_in(1, 1)
                    both(take_out, 0)
                    with act.Fori(1, iters - 1) as it:
                        both(take_projections, it)
                        both(take_own, it)
                        exponentials(it)
                        spread_factors(it)
                        both(take_rows, it - 1)
                        take_in(it + 1, 0)
                        both(finish, it)
                        take_sums(it)
                        take_in(it + 1, 1)
                        both(take_out, it)
                    both(take_projections, iters - 1)
                    both(take_own, iters - 1)
                    exponentials(iters - 1)
                    spread_factors(iters - 1)
                    both(take_rows, iters - 2)
                    both(finish, iters - 1)
                    take_sums(iters - 1)
                    both(take_out, iters - 1)
                    both(take_rows, iters - 1)
                elif layer == 2:
                    both(take_gathered, 0)
                    exponentials(0)
                    spread_factors(0)
                    both(take_gathered, 1)
                    both(finish, 0)
                    take_sums(0)
                    with act.Fori(1, iters - 1) as it:
                        both(take_out, it - 1)
                        exponentials(it)
                        spread_factors(it)
                        both(take_gathered, it + 1)
                        both(finish, it)
                        take_sums(it)
                    both(take_out, iters - 2)
                    exponentials(iters - 1)
                    spread_factors(iters - 1)
                    both(finish, iters - 1)
                    take_sums(iters - 1)
                    both(take_out, iters - 1)
                else:
                    exponentials(0)
                    exponentials(1)
                    both(finish, 0)
                    both(take_out, 0)
                    with act.Fori(2, iters) as it:
                        exponentials(it)
                        both(finish, it - 1)
                        roots(it - 2)
                        both(take_out, it - 1)
                    both(finish, iters - 1)
                    roots(iters - 2)
                    both(take_out, iters - 1)
                    roots(iters - 1)

            @block.vector
            def _(v):
                def weights(it):
                    nc.vector.tensor_copy(q[:, :, 0:1], m[:, :, R:R + 1])
                    if layer == 1:
                        v.wait_ge(took_al, it * 2 + 2)
                        nc.vector.tensor_tensor(lg[:, 0, :, :], al[:, 0, :, 0:H], al[:, 1, :, H:2 * H], ALU.add)
                        nc.vector.tensor_tensor(lg[:, 1, :, :], al[:, 1, :, 0:H], al[:, 1, :, H:2 * H], ALU.add)
                    else:
                        held = K["held"][:, :, round_cols(it)].rearrange("p c t -> p t c")
                        nc.vector.tensor_tensor(lg[:, 1, :, :], held[:, :, 0:H], held[:, :, H:2 * H], ALU.add)
                        for b in lanes:
                            if layer == 2:
                                v.wait_ge(s_free, it * 2 + b + 3)
                            else:
                                v.wait_ge(arrived[b], (it + 1) * (16 * per_group))
                            nc.vector.tensor_tensor(lg[:, 0, part[b], :], S2[:, part[b], P:P + H],
                                                    held[:, part[b], H:2 * H], ALU.add)
                    nc.vector.tensor_copy(fresh[:, :, 1:R + 1], K["fresh"][:, round_cols(it)].unsqueeze(1).to_broadcast([P, H, R]))
                    v.drain()
                    logits, leaky = (z[:, :, :, :].rearrange("p k t h -> p (k t h)") for z in (lg, lr))
                    nc.vector.scalar_tensor_tensor(leaky, logits, SLOPE, logits, ALU.mult, ALU.max)
                    v.drain()
                    nc.vector.tensor_tensor(q[:, :, 1:R + 1], by_head(lr[:, 0, :, :]), by_head(lr[:, 1, :, :]), ALU.max)
                    v.drain()
                    heads = lambda z: z[:, :, :].rearrange("p h r -> p (h r)")
                    nc.vector.tensor_tensor_scan(heads(m), heads(fresh), heads(q), 0.0, ALU.add, ALU.max)
                    v.drain()
                    now = m[:, :, 1:R + 1]
                    nc.vector.tensor_tensor(by_head(dd[:, 0, :, :]), m[:, :, 0:R], now, ALU.subtract)
                    nc.vector.tensor_tensor(by_head(dd[:, 1, :, :]), by_head(lr[:, 0, :, :]), now, ALU.subtract)
                    nc.vector.tensor_tensor(by_head(dd[:, 2, :, :]), by_head(lr[:, 1, :, :]), now, ALU.subtract)
                    v.drain()
                    nc.vector.tensor_tensor(by_head(dd[:, 0, :, :]), by_head(dd[:, 0, :, :]), fresh[:, :, 1:R + 1], ALU.add)
                    v.drain().then_inc(f1, 1)

                def sums(it, first=False):
                    v.wait_ge(st_free, it + 1)
                    nc.vector.tensor_copy(by_head(st[:, 1:R + 1, nacc:nacc + H]), m[:, :, 1:R + 1])
                    nc.vector.tensor_copy(st[:, 1:R + 1, nacc + H:nacc + 2 * H], lr[:, 1, :, :])
                    v.wait_ge(expd, it + 1)
                    w, ws = wt[:, 1, :, :], wt[:, 2, :, :]
                    if layer < 3:
                        acc = sums_of[:, :, :, 1:R + 1].rearrange("p h c t -> p t h c")
                    else:
                        acc = st[:, 1:R + 1, 0:nacc].rearrange("p t (h c) -> p t h c", h=H)
                        before = st[:, R, 0:nacc].rearrange("p (h c) -> p h c", h=H)
                    if layer < 3:
                        nc.vector.tensor_copy(msg[:, :, :, 0:1], sums_of[:, :, :, R:R + 1])
                        nc.vector.tensor_copy(msg[:, :, wd, 1:R + 1], by_head(w))
                        if layer == 1:
                            v.wait_ge(proj_taken, it * 2 + 4)
                            rows, own = sproj, st[:, 1:R + 1, sw - P:sw]
                        else:
                            rows, own = S2, D[:, :, 0:P]
                        nc.vector.tensor_tensor(msg[:, :, 0:wd, 1:R + 1], rows[:, :, 0:P].rearrange("p t (h c) -> p h c t", h=H),
                                                by_head(w).unsqueeze(2).to_broadcast([P, H, wd, R]), ALU.mult)
                        if layer == 2:
                            v.wait_ge(d_in, (it + 1) * 16)
                        nc.vector.tensor_tensor(o[:, :, :, :], own.rearrange("p t (h c) -> p t h c", h=H),
                                                ws.unsqueeze(3).to_broadcast([P, R, H, wd]), ALU.mult)
                        v.drain()
                        if layer == 1:
                            v.sem_inc(src_used, 1)
                        else:
                            v.sem_inc(s2_free, 1)
                            v.sem_inc(d_free, 1)
                        flat = lambda z: z[:, :, :, :].rearrange("p h c t -> p (h c t)")
                        v.wait_ge(spread, it + 1)
                        nc.vector.tensor_tensor_scan(flat(sums_of), flat(w0), flat(msg), 0.0, ALU.mult, ALU.add)
                        v.drain()
                    else:
                        nc.vector.tensor_copy(msg[:, :, :, wd:wd + 1].rearrange("p t h a -> p t (h a)"), w)
                        v.drain()
                        for t in range(R):
                            if t % G == 0:
                                v.wait_ge(weighted, it * 2 + t // G + 1)
                            for h in range(H):
                                old = before[:, h, :] if t == 0 else acc[:, t - 1, h, :]
                                nc.vector.scalar_tensor_tensor(acc[:, t, h, :], old, wt[:, 0, t, h:h + 1],
                                                               msg[:, t, h, :], ALU.mult, ALU.add)
                            v.drain()
                    v.sem_inc(f2, 1)
                    if layer == 3 and not first:
                        v.wait_ge(o_done, it * 2)
                    nc.vector.tensor_tensor(den[:, 0, :, :], acc[:, :, :, wd:wd + 1].rearrange("p t h a -> p t (h a)"), ws, ALU.add)
                    if layer < 3:
                        nc.vector.tensor_tensor(o[:, :, :, :], o[:, :, :, :], acc[:, :, :, 0:wd], ALU.add)
                    v.drain()
                    nc.vector.reciprocal(den[:, 1, :, :], den[:, 0, :, :])
                    if layer < 3:
                        v.drain()
                        nc.vector.tensor_tensor(o[:, :, :, :], o[:, :, :, :],
                                                den[:, 1, :, :].unsqueeze(3).to_broadcast([P, R, H, wd]), ALU.mult)
                        v.drain().then_inc(o_done, 1)
                    else:
                        nc.vector.tensor_copy(wself[:, :, :], ws)
                        v.drain()

                def add_self(it, first=False):
                    acc = st[:, 1:R + 1, 0:nacc].rearrange("p t (h c) -> p t h c", h=H)
                    v.wait_ge(d_in, (it + 1) * 16)
                    for b in lanes:
                        for t in range(b * G, (b + 1) * G):
                            for h in range(H):
                                if not first and t == b * G and h == 0:
                                    v.wait_ge(turned_h, it * 2 + b - 1)
                                nc.vector.scalar_tensor_tensor(o[:, t, h, :], D[:, t, 0:P], wself[:, t, h:h + 1],
                                                               acc[:, t, h, 0:P], ALU.mult, ALU.add)
                        v.drain().then_inc(summed, 1)
                    v.sem_inc(d_free, 1)

                def logits_out(it):
                    v.wait_ge(r_free, it + 1)
                    for b in lanes:
                        v.wait_ge(times, it * 2 + b + 1)
                        logits = pm[b][2][:, logit_at:logit_at + G * 2 * H].rearrange("p (t c) -> p t c", t=G)
                        nc.vector.tensor_copy(r[:, part[b], P:ROW], logits)
                        nc.vector.tensor_copy(K["held"][:, :, cols(it, b)].rearrange("p c t -> p t c"), logits)
                    v.drain().then_inc(rows_done, 1)

                def residual(it):
                    v.wait_ge(xr_in, (it + 1) * 16)
                    for b in lanes:
                        v.wait_ge(times, it * 2 + b + 1)
                        nc.vector.tensor_tensor(y[:, part[b], :], pm[b][0][:, :].rearrange("p (t c) -> p t c", t=G), xr[:, part[b], :], ALU.add)
                    v.drain().then_inc(y_done, 2)
                    layer_norm_moments(nc, v, y, stats, aggr, R)
                    v.sem_inc(var, 1)

                def norm(it):
                    v.wait_ge(r_free, it + 1)
                    v.wait_ge(root, it + 1)
                    layer_norm_apply(nc, v, y, r, aggr, rstd, R)
                    v.drain().then_inc(rows_done, 1)

                if layer == 1:
                    v.sem_inc(proj_taken, 2)
                    v.sem_inc(src_used, 1)
                else:
                    v.sem_inc(d_free, 1)
                if layer == 2:
                    v.sem_inc(s_free, 2)
                    v.sem_inc(s2_free, 1)
                nc.vector.memset(m[:, :, R:R + 1], 0.0)
                nc.vector.memset(fresh[:, :, 0:1], -BIG)
                if layer < 3:
                    nc.vector.memset(w0[:, :, :, 0:1], 0.0)
                    nc.vector.memset(sums_of[:, :, :, R:R + 1], 0.0)
                else:
                    nc.vector.memset(st[:, R, 0:nacc], 0.0)
                v.drain()
                weights(0)
                sums(0, first=True)
                if layer < 3:
                    with v.Fori(1, iters) as it:
                        weights(it)
                        logits_out(it - 1)
                        sums(it)
                    logits_out(iters - 1)
                else:
                    v.sem_inc(y_done, 2)
                    weights(1)
                    add_self(0, first=True)
                    sums(1)
                    with v.Fori(2, iters) as it:
                        weights(it)
                        add_self(it - 1)
                        residual(it - 2)
                        sums(it)
                        norm(it - 2)
                    add_self(iters - 1)
                    for last in (iters - 2, iters - 1):
                        residual(last)
                        norm(last)
                nc.vector.tensor_copy(K["carry_m"][:, :], m[:, :, R])
                ends = sums_of[:, :, :, R].rearrange("p h c -> p (h c)") if layer < 3 else st[:, R, 0:nacc]
                nc.vector.tensor_copy(K["carry_acc"][:, 0:nacc], ends)

        clear_semaphores(nc, used)


def seam_attend(nc, K, T, layer):
    wd, nacc, sw = WIDE[layer], ACC[layer], STATE[layer]
    blocks = 1 if layer < 3 else H
    hb = H // blocks
    with ExitStack() as ctx:
        def sb(name, shape, dt=FP32):
            return ctx.enter_context(nc.sbuf_tensor(f"s{layer}_{name}", shape, dt))

        used = []

        def sem(name):
            used.append(ctx.enter_context(nc.semaphore(f"s{layer}_{name}")))
            return used[-1]

        def bank(name):
            return ctx.enter_context(nc.psum_tensor(f"s{layer}_{name}", [P, 512], FP32))

        out_w = P if layer == 3 else ROW
        head = sb("head", [P, sw])
        xrow = sb("xrow", [P, ROW])
        tin = [sb(f"tin{k}", [P, 3, P]) for k in range(blocks)]
        tT = sb("tT", [P, 3, P])
        run = sb("run", [P, 3, P + 1])
        ex = sb("ex", [P, 2, P])
        we = sb("we", [P, 2, P])
        tw = sb("tw", [P, 2, P])
        cin = sb("cin", [P, 3, P])
        hm = sb("hm", [P, 4, P])
        e3 = sb("e3", [P, 3, P])
        w3 = sb("w3", [P, 3, P])
        u = sb("u", [P, 5, P])
        z = sb("z", [P, H, P] if layer == 3 else [P, 1, P])
        zT = sb("zT", [P, H, P] if layer == 3 else [P, 1, P])
        r = sb("r", [P, out_w])
        xr = sb("xr", [P, P])
        y = sb("y", [P, 1, P])
        stats, aggr, rstd = sb("stats", [P, 1, 6]), sb("aggr", [P, 1, 2]), sb("rstd", [P, 2, 1])
        val = sb("val", [P, 2 * H])
        pt, pback, ph, pr, pa = bank("pt"), bank("pback"), bank("ph"), bank("pr"), bank("pa")
        got, put = K["dma_sem"](f"s{layer}_got"), K["dma_sem"](f"s{layer}_put")
        packed, turned, f1, x1, carried, back, f2, x2, zdone, zturn, ztook, prod, rdone, var, root = (
            sem(s) for s in ("packed", "turned", "f1", "x1", "carried", "back", "f2", "x2", "zdone",
                             "zturn", "ztook", "prod", "rdone", "var", "root"))

        with nc.Block() as block:
            @block.gpsimd
            def _(g):
                at = bass.IndirectOffsetOnAxis(ap=K["head_slot_i"][:, :], axis=0)
                g.indirect_dma_start(head[:, :], None, T["st", layer][:, :], at).then_inc(got, 16)
                if layer > 1:
                    g.indirect_dma_start(xrow[:, :], None, T[layer][:, :],
                                         bass.IndirectOffsetOnAxis(ap=K["head_read_i"][:, :], axis=0)).then_inc(got, 16)
                if layer == 3:
                    g.indirect_dma_start(xr[:, :], None, T["xd"][:, :], at).then_inc(got, 16)
                g.wait_ge(rdone, 1)
                g.indirect_dma_start(T[layer + 1][:, :], bass.IndirectOffsetOnAxis(ap=K["head_row_i"][:, :], axis=0),
                                     r[:, :], None, bounds_check=NP + EP - 1, oob_is_err=False).then_inc(put, 16)
                g.wait_ge(put, 16)

            n_got = 16 * (1 + (layer > 1) + (layer == 3))

            @block.tensor
            def _(pe):
                for k in range(blocks):
                    pe.wait_ge(packed, k + 1)
                    for i in range(3):
                        ins = nc.tensor.transpose(pt[:, i * P:(i + 1) * P], tin[k][:, i, :], K["ident"][:, :])
                    ins.then_inc(turned, 1)
                    pe.wait_ge(carried, k + 1)
                    for i in range(3):
                        ins = nc.tensor.transpose(pback[:, i * P:(i + 1) * P], run[:, i, 0:P], K["ident"][:, :])
                    ins.then_inc(back, 1)
                pe.wait_ge(zdone, 1)
                for k in range(blocks):
                    ins = nc.tensor.transpose(ph[:, k * P:(k + 1) * P], z[:, k, :], K["ident"][:, :])
                ins.then_inc(zturn, 1)
                pe.wait_ge(ztook, 1)
                if layer == 3:
                    for k in range(H):
                        ins = nc.tensor.matmul(pr[:, 0:P], zT[:, k, :], K["W3"][:, k * P:(k + 1) * P], start=(k == 0), stop=(k == H - 1))
                else:
                    if layer == 1:
                        nc.tensor.matmul(pr[:, 0:P], zT[:, 0, :], K["W2"][:, :], start=True, stop=True)
                    ins = nc.tensor.matmul(pa[:, 0:2 * H], zT[:, 0, :], K[f"A{layer + 1}"][:, :], start=True, stop=True)
                ins.then_inc(prod, 1)

            @block.scalar
            def _(act):
                for k in range(blocks):
                    act.wait_ge(f1, k + 1)
                    nc.scalar.activation(we[:, :, :], ex[:, :, :], ACT.Exp).then_inc(x1, 1)
                    act.wait_ge(f2, k + 1)
                    nc.scalar.activation(w3[:, :, :], e3[:, :, :], ACT.Exp).then_inc(x2, 1)
                act.wait_ge(zturn, 1)
                nc.scalar.activation(zT[:, :, :].rearrange("p k c -> p (k c)"), ph[:, 0:blocks * P], ACT.Copy).then_inc(ztook, 1)
                if layer == 3:
                    act.wait_ge(var, 1)
                    nc.scalar.activation(rstd[:, 0, :], aggr[:, :, 1], ACT.Sqrt, bias=K["eps"][:, :]).then_inc(root, 1)

            @block.vector
            def _(v):
                def of_heads(ap, k):
                    return ap[:, k * hb:(k + 1) * hb].unsqueeze(2).to_broadcast([P, hb, wd])

                def heads(ap):
                    return ap.rearrange("p (h c) -> p h c", h=hb)

                tail_acc = K["carry_acc"][:, 0:nacc].rearrange("p (h c) -> p h c", h=H)
                head_acc = head[:, 0:nacc].rearrange("p (h c) -> p h c", h=H)
                nc.vector.memset(run[:, :, :], 0.0)
                v.wait_ge(got, n_got)
                for k in range(blocks):
                    hs = slice(k * hb, (k + 1) * hb)
                    nc.vector.tensor_copy(heads(tin[k][:, 0, :]), of_heads(K["carry_m"][:, :], k))
                    nc.vector.tensor_copy(heads(tin[k][:, 1, :]), tail_acc[:, hs, wd:wd + 1].to_broadcast([P, hb, wd]))
                    nc.vector.tensor_copy(heads(tin[k][:, 2, :]), tail_acc[:, hs, 0:wd])
                    v.drain().then_inc(packed, 1)
                    v.wait_ge(turned, k + 1)
                    nc.vector.tensor_copy(tT[:, :, :].rearrange("p i c -> p (i c)"), pt[:, 0:3 * P])
                    v.drain()
                    nc.vector.tensor_tensor_scan(run[:, 0, 1:P + 1], K["chain"][:, :], tT[:, 0, :], 0.0, ALU.add, ALU.max)
                    v.drain()
                    nc.vector.tensor_tensor(ex[:, 0, :], run[:, 0, 0:P], run[:, 0, 1:P + 1], ALU.subtract)
                    nc.vector.tensor_tensor(ex[:, 1, :], tT[:, 0, :], run[:, 0, 1:P + 1], ALU.subtract)
                    v.drain()
                    nc.vector.tensor_tensor(ex[:, 0, :], ex[:, 0, :], K["chain"][:, :], ALU.add)
                    v.drain().then_inc(f1, 1)
                    v.wait_ge(x1, k + 1)
                    for i in range(2):
                        nc.vector.tensor_tensor(tw[:, i, :], tT[:, i + 1, :], we[:, 1, :], ALU.mult)
                    v.drain()
                    for i in range(2):
                        nc.vector.tensor_tensor_scan(run[:, i + 1, 1:P + 1], we[:, 0, :], tw[:, i, :], 0.0, ALU.mult, ALU.add)
                    v.drain().then_inc(carried, 1)
                    v.wait_ge(back, k + 1)
                    nc.vector.tensor_copy(cin[:, :, :].rearrange("p i c -> p (i c)"), pback[:, 0:3 * P])
                    nc.vector.tensor_copy(heads(hm[:, 0, :]), of_heads(head[:, nacc:nacc + H], k))
                    nc.vector.tensor_copy(heads(hm[:, 1, :]), head_acc[:, hs, wd:wd + 1].to_broadcast([P, hb, wd]))
                    nc.vector.tensor_copy(heads(hm[:, 2, :]), of_heads(head[:, nacc + H:nacc + 2 * H], k))
                    v.drain()
                    nc.vector.tensor_scalar(cin[:, 0, :], cin[:, 0, :], K["joins"][:, :], None, ALU.add)
                    v.drain()
                    nc.vector.tensor_tensor(hm[:, 3, :], cin[:, 0, :], hm[:, 0, :], ALU.max)
                    v.drain()
                    nc.vector.tensor_tensor(e3[:, 0, :], cin[:, 0, :], hm[:, 3, :], ALU.subtract)
                    nc.vector.tensor_tensor(e3[:, 1, :], hm[:, 0, :], hm[:, 3, :], ALU.subtract)
                    nc.vector.tensor_tensor(e3[:, 2, :], hm[:, 2, :], hm[:, 3, :], ALU.subtract)
                    v.drain().then_inc(f2, 1)
                    v.wait_ge(x2, k + 1)
                    nc.vector.tensor_tensor(u[:, 0, :], cin[:, 1, :], w3[:, 0, :], ALU.mult)
                    nc.vector.tensor_tensor(u[:, 1, :], hm[:, 1, :], w3[:, 1, :], ALU.mult)
                    nc.vector.tensor_tensor(u[:, 2, :], cin[:, 2, :], w3[:, 0, :], ALU.mult)
                    nc.vector.tensor_tensor(heads(u[:, 3, :]), head_acc[:, hs, 0:wd], heads(w3[:, 1, :]), ALU.mult)
                    xd = head[:, sw - P:sw] if layer == 1 else xrow[:, 0:P]
                    nc.vector.tensor_tensor(u[:, 4, :], xd, w3[:, 2, :], ALU.mult)
                    v.drain()
                    nc.vector.tensor_tensor(u[:, 0, :], u[:, 0, :], u[:, 1, :], ALU.add)
                    nc.vector.tensor_tensor(u[:, 2, :], u[:, 2, :], u[:, 3, :], ALU.add)
                    v.drain()
                    nc.vector.tensor_tensor(u[:, 0, :], u[:, 0, :], w3[:, 2, :], ALU.add)
                    nc.vector.tensor_tensor(u[:, 2, :], u[:, 2, :], u[:, 4, :], ALU.add)
                    v.drain()
                    nc.vector.reciprocal(u[:, 1, :], u[:, 0, :])
                    v.drain()
                    nc.vector.tensor_tensor(z[:, k, :], u[:, 2, :], u[:, 1, :], ALU.mult)
                    v.drain()
                if layer < 3:
                    nc.vector.tensor_scalar(z[:, 0, :], z[:, 0, :], 0.0, None, ALU.max)
                    v.drain()
                v.sem_inc(zdone, 1)
                v.wait_ge(prod, 1)
                if layer < 3:
                    if layer == 1:
                        nc.vector.tensor_tensor(r[:, 0:P], pr[:, 0:P], K["b2r"][:, :], ALU.add)
                    else:
                        nc.vector.tensor_copy(r[:, 0:P], z[:, 0, :])
                    nc.vector.tensor_copy(r[:, P:ROW], pa[:, 0:2 * H])
                    nc.vector.tensor_copy(val[:, :], pa[:, 0:2 * H])
                    v.drain().then_inc(rdone, 1)
                    for c in range(2 * H):
                        old = K["held"][:, c, :]
                        nc.vector.tensor_tensor(old, old, K["not_headend"][:, :], ALU.mult)
                    v.drain()
                    for c in range(2 * H):
                        old = K["held"][:, c, :]
                        nc.vector.scalar_tensor_tensor(old, K["headend"][:, :], val[:, c:c + 1], old, ALU.mult, ALU.add)
                else:
                    nc.vector.tensor_tensor(y[:, 0, :], pr[:, 0:P], xr[:, :], ALU.add)
                    v.drain()
                    nc.vector.tensor_tensor(y[:, 0, :], y[:, 0, :], K["b3r"][:, :], ALU.add)
                    v.drain()
                    layer_norm_moments(nc, v, y, stats, aggr, 1)
                    v.sem_inc(var, 1)
                    v.wait_ge(root, 1)
                    layer_norm_apply(nc, v, y, r[:, :].unsqueeze(1), aggr, rstd, 1)
                    v.drain().then_inc(rdone, 1)

        clear_semaphores(nc, used)


def hold_logits(nc, K, T, layer):
    with ExitStack() as ctx:
        tail = ctx.enter_context(nc.sbuf_tensor(f"h{layer}_tail", [P, ROW], FP32))
        masked = ctx.enter_context(nc.sbuf_tensor(f"h{layer}_masked", [P, 2 * H, COLS], FP32))
        got = K["dma_sem"](f"h{layer}_got")
        with nc.Block() as block:
            @block.gpsimd
            def _(g):
                g.indirect_dma_start(tail[:, :], None, T[layer][:, :],
                                     bass.IndirectOffsetOnAxis(ap=K["tail_row_i"][:, :], axis=0)).then_inc(got, 16)

            @block.vector
            def _(v):
                for c in range(2 * H):
                    nc.vector.tensor_tensor(masked[:, c, :], K["held"][:, c, :], K["last"][:, :], ALU.mult)
                v.wait_ge(got, 16)
                v.drain()
                for c in range(2 * H):
                    nc.vector.tensor_tensor_scan(K["held"][:, c, ::-1], K["goes_on"][:, ::-1], masked[:, c, ::-1],
                                                 tail[:, P + c:P + c + 1], ALU.mult, ALU.add)

def message(nc, A, K, T, out):
    lanes = range(2)
    with ExitStack() as ctx:
        def sb(name, shape, dt=FP32):
            return ctx.enter_context(nc.sbuf_tensor("e_" + name, shape, dt))

        used = []

        def sem(name):
            used.append(ctx.enter_context(nc.semaphore("e_" + name)))
            return used[-1]

        S = [sb(f"src{b}", [P, G, P]) for b in lanes]
        D = [sb(f"dst{b}", [P, G, P]) for b in lanes]
        idx = [sb(f"idx{b}", [P, 3, G], I32) for b in lanes]
        wrow = [sb(f"wrow{b}", [1, G * P]) for b in lanes]
        fresh = [sb(f"fresh{b}", [P, G]) for b in lanes]
        sT = [sb(f"sT{b}", [P, G * P]) for b in lanes]
        dT = [sb(f"dT{b}", [P, G * P]) for b in lanes]
        rT = [sb(f"rT{b}", [P, G * P]) for b in lanes]
        gT = [sb(f"gT{b}", [P, G * P]) for b in lanes]
        uT = [sb(f"uT{b}", [P, G * P]) for b in lanes]
        agg = [sb(f"agg{b}", [P, G, P]) for b in lanes]
        xnew = [sb(f"xnew{b}", [P, G, P]) for b in lanes]
        xres = [sb(f"xres{b}", [P, G, P]) for b in lanes]
        y = [sb(f"y{b}", [P, G, P]) for b in lanes]
        fin = [sb(f"fin{b}", [P, G, P]) for b in lanes]
        to = [sb(f"to{b}", [P, G], I32) for b in lanes]
        stats = [sb(f"stats{b}", [P, G, 6]) for b in lanes]
        aggr = [sb(f"aggr{b}", [P, G, 2]) for b in lanes]
        rstd = [sb(f"rstd{b}", [P, 2, G]) for b in lanes]
        pm = [[ctx.enter_context(nc.psum_tensor(f"e_p{b}{k}", [P, G * P], FP32)) for k in range(4)] for b in lanes]
        w_in, agg_stored = ([sem(f"{s}{b}") for b in lanes] for s in ("w_in", "agg_stored"))
        arrived, sent = ([K["dma_sem"](f"e_{s}{b}") for b in lanes] for s in ("arrived", "sent"))
        (in_free, tick, staged, turned, took, pre, took_r, msgs, maxed, turned_g, took_g, upd, took_u, last_mm,
         var, root, fin_done, out_free, agg_free, y_read, msg_read) = (
            sem(s) for s in ("in_free", "tick", "staged", "turned", "took", "pre", "took_r", "msgs", "maxed",
                             "turned_g", "took_g", "upd", "took_u", "last_mm", "var", "root", "fin_done", "out_free",
                             "agg_free", "y_read", "msg_read"))
        sp_tick = sem("sp_tick")
        iters = EG // 2

        def cols(it, b):
            return bass.ds((it * 2 + b) * G, G)

        w_rows = A["w"].rearrange("(g t) p -> g (t p)", t=G)
        agg_rows = T["st", 4].rearrange("(p j) c -> p j c", p=P)

        def both(stage, it):
            for b in lanes:
                stage(it, b)

        with nc.Block() as block:
            @block.gpsimd
            def _(g):
                def gather(it, b, staged_before):
                    g.wait_ge(in_free, it * 2 + b + 1)
                    g.sem_inc(tick, 1)
                    nc.gpsimd.tensor_copy(idx[b][:, 0, :], K["gsrc_i"][:, cols(it, b)]).then_inc(staged, 1)
                    nc.gpsimd.tensor_copy(idx[b][:, 1, :], K["gdst_i"][:, cols(it, b)]).then_inc(staged, 1)
                    g.wait_ge(staged, staged_before + 2)
                    g.sem_inc(tick, 1)
                    for t in range(G):
                        for k, rows in enumerate((S, D)):
                            g.indirect_dma_start(rows[b][:, t, :], None, T[4][:, :],
                                                 bass.IndirectOffsetOnAxis(ap=idx[b][:, k, t:t + 1], axis=0)).then_inc(arrived[b], 16)

                def scatter(it, staged_before):
                    for b in lanes:
                        nc.gpsimd.tensor_copy(to[b][:, :], K["scat_i"][:, cols(it, b)]).then_inc(staged, 1)
                    g.wait_ge(staged, staged_before + 2)
                    g.sem_inc(tick, 1)
                    for b in lanes:
                        g.wait_ge(fin_done, it * 2 + b + 1)
                        g.sem_inc(tick, 1)
                        for t in range(G):
                            g.indirect_dma_start(out[:, :], bass.IndirectOffsetOnAxis(ap=to[b][:, t:t + 1], axis=0),
                                                 fin[b][:, t, :], None, bounds_check=NP - 1, oob_is_err=False).then_inc(sent[b], 16)
                    for b in lanes:
                        g.wait_ge(sent[b], (it + 1) * (16 * G))
                        g.sem_inc(out_free, 1)

                g.sem_inc(out_free, 2)
                for r in range(2):
                    for b in lanes:
                        gather(r, b, 4 * r + 2 * b)
                with g.Fori(1, iters - 1) as it:
                    for b in lanes:
                        gather(it + 1, b, it * 6 + 2 * b + 2)
                    scatter(it - 1, it * 6 + 6)
                scatter(iters - 2, iters * 6 - 4)
                scatter(iters - 1, iters * 6 - 2)

            @block.sync
            def _(sp):
                sp.sem_inc(agg_free, 2)
                for b in lanes:
                    sp.dma_start(wrow[b][:, :], w_rows[b:b + 1, :]).then_inc(w_in[b], 16)
                with sp.Fori(0, iters) as it:
                    for b in lanes:
                        sp.wait_ge(maxed, it * 2 + b + 1)
                        sp.sem_inc(sp_tick, 1)
                        sp.dma_start(agg_rows[:, cols(it, b), :], agg[b][:, :, :]).then_inc(agg_stored[b], 16)
                        sp.dma_start(wrow[b][:, :], w_rows[bass.ds(it * 2 + b + 2, 1), :]).then_inc(w_in[b], 16)
                    for b in lanes:
                        sp.wait_ge(agg_stored[b], (it + 1) * 16)
                        sp.sem_inc(agg_free, 1)
                for b in lanes:
                    sp.wait_ge(w_in[b], (iters + 1) * 16)

            @block.tensor
            def _(pe):
                def turn_in(it, b):
                    pe.wait_ge(arrived[b], (it + 1) * (16 * 2 * G))
                    pe.wait_ge(msg_read, it * 2 + b + 1)
                    for k, rows in enumerate((S, D)):
                        for t in range(G):
                            ins = nc.tensor.transpose(pm[b][k][:, t * P:(t + 1) * P], rows[b][:, t, :], K["ident"][:, :])
                    ins.then_inc(turned, 1)

                def edge_in(it, b):
                    pe.wait_ge(took, it * 2 + b + 1)
                    pe.wait_ge(w_in[b], (it + 1) * 16)
                    nc.tensor.matmul(pm[b][0][:, :], K["M1a"][:, :], sT[b][:, :], start=True, stop=False)
                    nc.tensor.matmul(pm[b][0][:, :], K["M1b"][:, :], dT[b][:, :], start=False, stop=False)
                    nc.tensor.matmul(pm[b][0][:, :], K["w1c"][:, :], wrow[b][:, :], start=False, stop=True).then_inc(pre, 1)

                def edge_out(it, b):
                    pe.wait_ge(took_r, it * 2 + b + 1)
                    add_bias(nc, K, pm[b][1], "m2")
                    for t in range(G):
                        ins = nc.tensor.matmul(pm[b][1][:, t * P:(t + 1) * P], rT[b][:, t * P:(t + 1) * P], K["M2"][:, :],
                                               start=False, stop=(t == G - 1))
                    ins.then_inc(msgs, 1)

                def own_part(it, b):
                    nc.tensor.matmul(pm[b][2][:, :], K["U1a"][:, :], dT[b][:, :], start=True, stop=False)

                def turn_max(it, b):
                    pe.wait_ge(y_read, it * 2 + b + 1)
                    pe.wait_ge(maxed, it * 2 + b + 1)
                    for t in range(G):
                        ins = nc.tensor.transpose(pm[b][3][:, t * P:(t + 1) * P], agg[b][:, t, :], K["ident"][:, :])
                    ins.then_inc(turned_g, 1)

                def node_in(it, b):
                    pe.wait_ge(took_g, it * 2 + b + 1)
                    nc.tensor.matmul(pm[b][2][:, :], K["U1b"][:, :], gT[b][:, :], start=False, stop=True).then_inc(upd, 1)

                def node_out(it, b):
                    pe.wait_ge(took_u, it * 2 + b + 1)
                    add_bias(nc, K, pm[b][3], "c2")
                    for t in range(G):
                        ins = nc.tensor.matmul(pm[b][3][:, t * P:(t + 1) * P], uT[b][:, t * P:(t + 1) * P], K["U2"][:, :],
                                               start=False, stop=(t == G - 1))
                    ins.then_inc(last_mm, 1)

                for stage in (turn_in, edge_in, edge_out, own_part):
                    both(stage, 0)
                with pe.Fori(1, iters) as it:
                    both(turn_in, it)
                    both(turn_max, it - 1)
                    both(edge_in, it)
                    both(node_in, it - 1)
                    both(edge_out, it)
                    both(node_out, it - 1)
                    both(own_part, it)
                for stage in (turn_max, node_in, node_out):
                    both(stage, iters - 1)

            @block.scalar
            def _(act):
                def take_in(it, b):
                    act.wait_ge(turned, it * 2 + b + 1)
                    nc.scalar.activation(sT[b][:, :], pm[b][0][:, :], ACT.Copy)
                    nc.scalar.activation(dT[b][:, :], pm[b][1][:, :], ACT.Copy).then_inc(took, 1)

                def take_edge(it, b):
                    act.wait_ge(pre, it * 2 + b + 1)
                    nc.scalar.activation(rT[b][:, :], pm[b][0][:, :], ACT.Relu, bias=K["mb1"][:, :]).then_inc(took_r, 1)

                def take_max(it, b):
                    act.wait_ge(turned_g, it * 2 + b + 1)
                    nc.scalar.activation(gT[b][:, :], pm[b][3][:, :], ACT.Copy).then_inc(took_g, 1)

                def take_node(it, b):
                    act.wait_ge(upd, it * 2 + b + 1)
                    nc.scalar.activation(uT[b][:, :], pm[b][2][:, :], ACT.Relu, bias=K["c1"][:, :]).then_inc(took_u, 1)

                def roots(it, b):
                    act.wait_ge(var, it * 2 + b + 1)
                    nc.scalar.activation(rstd[b][:, 0, :], aggr[b][:, :, 1], ACT.Sqrt, bias=K["eps"][:, :]).then_inc(root, 1)

                both(take_in, 0)
                both(take_edge, 0)
                with act.Fori(1, iters) as it:
                    both(take_in, it)
                    both(take_max, it - 1)
                    both(take_edge, it)
                    both(take_node, it - 1)
                    both(roots, it - 1)
                for stage in (take_max, take_node, roots):
                    both(stage, iters - 1)

            @block.vector
            def _(v):
                def keep(it, b):
                    v.wait_ge(turned, it * 2 + b + 1)
                    nc.vector.tensor_copy(xnew[b][:, :, :], D[b][:, :, :])
                    nc.vector.tensor_copy(fresh[b][:, :], K["fresh"][:, cols(it, b)])
                    v.drain().then_inc(in_free, 1)

                def pass_on(it, b):
                    nc.vector.tensor_copy(xres[b][:, :, :], xnew[b][:, :, :])

                def maximum(it, b):
                    n = it * 2 + b + 1
                    v.wait_ge(agg_free, n)
                    v.wait_ge(msgs, n)
                    for t in range(G):
                        old = agg[1 - b][:, G - 1, :] if t == 0 else agg[b][:, t - 1, :]
                        nc.vector.scalar_tensor_tensor(agg[b][:, t, :], old, fresh[b][:, t:t + 1],
                                                       pm[b][1][:, t * P:(t + 1) * P], ALU.add, ALU.max)
                        v.drain()
                    v.sem_inc(maxed, 1)
                    v.sem_inc(msg_read, 1)

                def residual(it, b):
                    v.wait_ge(last_mm, it * 2 + b + 1)
                    nc.vector.tensor_tensor(y[b][:, :, :], pm[b][3][:, :].rearrange("p (t c) -> p t c", t=G), xres[b][:, :, :], ALU.add)
                    v.drain().then_inc(y_read, 1)
                    layer_norm_moments(nc, v, y[b], stats[b], aggr[b], G)
                    v.sem_inc(var, 1)

                def norm(it, b):
                    n = it * 2 + b + 1
                    v.wait_ge(out_free, n)
                    v.wait_ge(root, n)
                    layer_norm_apply(nc, v, y[b], fin[b], aggr[b], rstd[b], G)
                    v.drain().then_inc(fin_done, 1)

                nc.vector.memset(agg[1][:, :, :], 0.0)
                v.drain()
                v.sem_inc(y_read, 2)
                v.sem_inc(msg_read, 2)
                v.sem_inc(in_free, 2)
                both(keep, 0)
                both(maximum, 0)
                both(pass_on, 0)
                v.drain()
                with v.Fori(1, iters) as it:
                    both(keep, it)
                    both(maximum, it)
                    both(residual, it - 1)
                    both(norm, it - 1)
                    both(pass_on, it)
                    v.drain()
                both(residual, iters - 1)
                both(norm, iters - 1)
                nc.vector.tensor_copy(K["carry_acc"][:, 0:P], agg[1][:, G - 1, :])

        clear_semaphores(nc, used)


def seam_message(nc, K, T, out):
    with ExitStack() as ctx:
        def sb(name, shape, dt=FP32):
            return ctx.enter_context(nc.sbuf_tensor("z_" + name, shape, dt))

        used = []

        def sem(name):
            used.append(ctx.enter_context(nc.semaphore("z_" + name)))
            return used[-1]

        head, xd, g, y, r = sb("head", [P, P]), sb("xd", [P, P]), sb("g", [P, P]), sb("y", [P, 1, P]), sb("r", [P, 1, P])
        tT, run, cin = sb("tT", [P, P]), sb("run", [P, P + 1]), sb("cin", [P, P])
        xT, gT, uT = sb("xT", [P, P]), sb("gT", [P, P]), sb("uT", [P, P])
        stats, aggr, rstd = sb("stats", [P, 1, 6]), sb("aggr", [P, 1, 2]), sb("rstd", [P, 2, 1])
        ps = [ctx.enter_context(nc.psum_tensor(f"z_p{k}", [P, 512], FP32)) for k in range(6)]
        s, a, d = sem("pe"), sem("act"), sem("dve")
        got, put = K["dma_sem"]("z_got"), K["dma_sem"]("z_put")

        with nc.Block() as block:
            @block.gpsimd
            def _(p):
                p.indirect_dma_start(head[:, :], None, T["st", 4][:, :],
                                     bass.IndirectOffsetOnAxis(ap=K["head_slot_i"][:, :], axis=0)).then_inc(got, 16)
                p.indirect_dma_start(xd[:, :], None, T[4][:, :],
                                     bass.IndirectOffsetOnAxis(ap=K["head_read_i"][:, :], axis=0)).then_inc(got, 16)
                p.wait_ge(d, 4)
                p.indirect_dma_start(out[:, :], bass.IndirectOffsetOnAxis(ap=K["head_out_i"][:, :], axis=0),
                                     r[:, 0, :], None, bounds_check=NP - 1, oob_is_err=False).then_inc(put, 16)
                p.wait_ge(put, 16)

            @block.tensor
            def _(pe):
                nc.tensor.transpose(ps[0][:, 0:P], K["carry_acc"][:, 0:P], K["ident"][:, :])
                pe.wait_ge(got, 32)
                nc.tensor.transpose(ps[1][:, 0:P], xd[:, :], K["ident"][:, :]).then_inc(s, 1)
                pe.wait_ge(d, 1)
                nc.tensor.transpose(ps[2][:, 0:P], run[:, 0:P], K["ident"][:, :]).then_inc(s, 1)
                pe.wait_ge(d, 2)
                nc.tensor.transpose(ps[3][:, 0:P], g[:, :], K["ident"][:, :]).then_inc(s, 1)
                pe.wait_ge(a, 2)
                nc.tensor.matmul(ps[4][:, 0:P], K["U1a"][:, :], xT[:, :], start=True, stop=False)
                nc.tensor.matmul(ps[4][:, 0:P], K["U1b"][:, :], gT[:, :], start=False, stop=True).then_inc(s, 1)
                pe.wait_ge(a, 3)
                nc.tensor.matmul(ps[5][:, 0:P], uT[:, :], K["U2"][:, :], start=True, stop=True).then_inc(s, 1)

            @block.scalar
            def _(act):
                act.wait_ge(s, 1)
                nc.scalar.activation(xT[:, :], ps[1][:, 0:P], ACT.Copy).then_inc(a, 1)
                act.wait_ge(s, 3)
                nc.scalar.activation(gT[:, :], ps[3][:, 0:P], ACT.Copy).then_inc(a, 1)
                act.wait_ge(s, 4)
                nc.scalar.activation(uT[:, :], ps[4][:, 0:P], ACT.Relu, bias=K["c1"][:, :]).then_inc(a, 1)
                act.wait_ge(d, 3)
                nc.scalar.activation(rstd[:, 0, :], aggr[:, :, 1], ACT.Sqrt, bias=K["eps"][:, :]).then_inc(a, 1)

            @block.vector
            def _(v):
                nc.vector.memset(run[:, :], 0.0)
                v.wait_ge(s, 1)
                nc.vector.tensor_copy(tT[:, :], ps[0][:, 0:P])
                v.drain()
                nc.vector.tensor_tensor_scan(run[:, 1:P + 1], K["chain"][:, :], tT[:, :], 0.0, ALU.add, ALU.max)
                v.drain().then_inc(d, 1)
                v.wait_ge(s, 2)
                nc.vector.tensor_scalar(cin[:, :], ps[2][:, 0:P], K["joins"][:, :], None, ALU.add)
                v.drain()
                nc.vector.tensor_tensor(g[:, :], cin[:, :], head[:, :], ALU.max)
                v.drain().then_inc(d, 1)
                v.wait_ge(s, 5)
                nc.vector.tensor_tensor(y[:, 0, :], ps[5][:, 0:P], xd[:, :], ALU.add)
                v.drain()
                nc.vector.tensor_tensor(y[:, 0, :], y[:, 0, :], K["c2r"][:, :], ALU.add)
                v.drain()
                layer_norm_moments(nc, v, y, stats, aggr, 1)
                v.sem_inc(d, 1)
                v.wait_ge(a, 4)
                layer_norm_apply(nc, v, y, r, aggr, rstd, 1)
                v.drain().then_inc(d, 1)

        clear_semaphores(nc, used)



TABLE_KIND = "Internal"



def kernel(**inputs):
    import numpy as _np
    import concourse.bacc as _bacc
    from concourse import mybir as _mybir
    from concourse.bass_utils import run_bass_kernel_spmd as _run

    nc = _bacc.Bacc("TRN2", target_bir_lowering=False, num_devices=1)
    inputs = {k: _np.ascontiguousarray(v) for k, v in inputs.items()}
    x = _np.zeros((NP + DLANES * G * P, P), inputs["x"].dtype)
    x[:N] = inputs["x"]
    pad = EP - E
    src = _np.concatenate([inputs["src"], _np.zeros(pad, inputs["src"].dtype)])
    dst = _np.concatenate([inputs["dst"], _np.full(pad, N, inputs["dst"].dtype)])
    w = _np.concatenate([inputs["edge_weight"], _np.zeros(pad, inputs["edge_weight"].dtype)])
    edge = _np.full(1, -1, dst.dtype)
    arrays = {
        "x": x, "src": src.reshape(P, COLS), "dst": dst.reshape(P, COLS),
        "dst_before": _np.concatenate([edge, dst[:-1]]).reshape(P, COLS),
        "dst_after": _np.concatenate([dst[1:], edge]).reshape(P, COLS),
        "w": _np.concatenate([w.reshape(P, COLS).T, _np.zeros((2 * G, P), w.dtype)]),
        "node_ids": _np.arange(NP, dtype=_np.int32).reshape(NP, 1),
        "slot_ids": (NP + _np.arange(EP, dtype=_np.int32)).reshape(P, COLS),
        "eye": _np.eye(P, dtype=_np.float32),
    }
    for name, value in inputs.items():
        if name.startswith(("L0_", "L1_")):
            arrays[name] = value
    feeds, aps = {}, {}
    for name, a in arrays.items():
        feeds["in_" + name] = a
        aps[name] = nc.dram_tensor("in_" + name, a.shape, _mybir.dt.from_np(a.dtype), kind="ExternalInput").ap()
    out = nc.dram_tensor("out_rows", (NP, P), _mybir.dt.float32, kind="ExternalOutput").ap()
    build(nc, aps, out)
    r = _run(nc, [feeds], core_ids=[0])
    return r.results[0]["out_rows"][:N]
```
